# Optimizing a Trainium2 kernel written in Bass

```python
import numpy as np
import jax
import jax.numpy as jnp

def _softmax(x, axis=-1):
    return jax.nn.softmax(x, axis=axis)

def _gelu(x):
    return jax.nn.gelu(x, approximate=True)

def _silu(x):
    return jax.nn.silu(x)

def _sigmoid(x):
    return jax.nn.sigmoid(x)

def _layernorm(x, axis=-1, eps=1e-05):
    m = jnp.mean(x, axis=axis, keepdims=True)
    v = jnp.var(x, axis=axis, keepdims=True)
    return (x - m) / jnp.sqrt(v + eps)

def _scatter_add(tgt, idx, src, axis=0):
    return tgt.at[idx].add(src)

def _segment_sum(src, seg, n):
    return jax.ops.segment_sum(src, seg, n)
kernel_name = 'mk_audio_tower_d1_tok_audfeat768_r4_3c0399'

def setup_inputs(seed: int=0):
    np.random.seed(seed)
    _w = jnp.asarray

    def _rec_inputs():
        import jax
        import jax.numpy as jnp
        _rk = jax.random.key(seed)
        x = -0.00040386 + 0.999972 * jax.random.normal(jax.random.fold_in(_rk, 1), (64, 256, 192), jnp.float32)
        return x
    x = _rec_inputs()

    def _L0_tok_setup():
        import jax, jax.numpy as jnp
        import numpy as np
        HEADS = 12
        Q_STRIDE = 4
        WINDOW_SIZE = 64
        key = jax.random.key(seed)
        ks = jax.random.split(key, 3)
        B, N, dim = (8, 512, 192)
        x = jax.random.normal(ks[0], (B, N, dim), dtype=jnp.float32)
        w_qkv = jax.random.normal(ks[1], (3 * dim, dim), dtype=jnp.float32) * dim ** (-0.5)
        b_qkv = jnp.zeros((3 * dim,), dtype=jnp.float32)
        w_proj = jax.random.normal(ks[2], (dim, dim), dtype=jnp.float32) * dim ** (-0.5)
        b_proj = jnp.zeros((dim,), dtype=jnp.float32)
        return {'x': x, 'w_qkv': w_qkv, 'b_qkv': b_qkv, 'w_proj': w_proj, 'b_proj': b_proj}
    _L0_tok_all = _L0_tok_setup()
    _L0_tok_in = {k: v for k, v in _L0_tok_all.items() if k in ('w_qkv', 'b_qkv', 'w_proj', 'b_proj')}
    del _L0_tok_all

    def _L0_attn_setup():
        import jax, jax.numpy as jnp
        import numpy as np
        import math
        MAX_REL = 32
        key = jax.random.key(seed)
        ks = jax.random.split(key, 6)
        B, S, D = (2, 512, 192)
        H = 12
        dk = D // H
        s = 1.0 / math.sqrt(D)
        return {'x': jax.random.normal(ks[0], (B, S, D), jnp.float32), 'Wq': jax.random.normal(ks[1], (D, D), jnp.float32) * s, 'bq': jnp.zeros((D,), jnp.float32), 'Wk': jax.random.normal(ks[2], (D, D), jnp.float32) * s, 'bk': jnp.zeros((D,), jnp.float32), 'Wv': jax.random.normal(ks[3], (D, D), jnp.float32) * s, 'bv': jnp.zeros((D,), jnp.float32), 'Wo': jax.random.normal(ks[4], (D, D), jnp.float32) * s, 'bo': jnp.zeros((D,), jnp.float32), 'rel_emb': jax.random.normal(ks[5], (2 * MAX_REL + 1, dk), jnp.float32)}
    _L0_attn_all = _L0_attn_setup()
    _L0_attn_in = {k: v for k, v in _L0_attn_all.items() if k in ('Wq', 'bq', 'Wk', 'bk', 'Wv', 'bv', 'Wo', 'bo', 'rel_emb')}
    del _L0_attn_all

    def _L0_ffn_setup():
        import jax, jax.numpy as jnp
        import numpy as np
        B, S, H = (2, 256, 192)
        E, K, I = (16, 4, 192)
        ALPHA, LIMIT, EPS = (1.702, 7.0, 1e-05)

        def _swiglu(h):
            x_glu, x_lin = jnp.split(h, 2, axis=-1)
            x_glu = jnp.minimum(x_glu, LIMIT)
            x_lin = jnp.clip(x_lin, -LIMIT, LIMIT)
            return x_glu * jax.nn.sigmoid(ALPHA * x_glu) * (x_lin + 1.0)
        key = jax.random.key(seed)
        ks = jax.random.split(key, 7)
        x = jax.random.normal(ks[0], (B, S, H), dtype=jnp.float32)
        scale = jnp.ones((H,), jnp.float32)
        gate_w = jax.random.normal(ks[1], (E, H), jnp.float32) * 0.02
        gate_b = jnp.zeros((E,), jnp.float32)
        w1 = jax.random.normal(ks[2], (E, H, 2 * I), jnp.float32) * 0.02
        b1 = jax.random.normal(ks[3], (E, 2 * I), jnp.float32) * 0.02
        w2 = jax.random.normal(ks[4], (E, I, H), jnp.float32) * 0.02
        b2 = jax.random.normal(ks[5], (E, H), jnp.float32) * 0.02
        return {'x': x, 'scale': scale, 'gate_w': gate_w, 'gate_b': gate_b, 'w1': w1, 'b1': b1, 'w2': w2, 'b2': b2}
    _L0_ffn_all = _L0_ffn_setup()
    _L0_ffn_in = {k: v for k, v in _L0_ffn_all.items() if k in ('scale', 'gate_w', 'gate_b', 'w1', 'b1', 'w2', 'b2')}
    del _L0_ffn_all
    return {'x': x, 'L0_tok_w_qkv': _L0_tok_in['w_qkv'], 'L0_tok_b_qkv': _L0_tok_in['b_qkv'], 'L0_tok_w_proj': _L0_tok_in['w_proj'], 'L0_tok_b_proj': _L0_tok_in['b_proj'], 'L0_attn_Wq': _L0_attn_in['Wq'], 'L0_attn_bq': _L0_attn_in['bq'], 'L0_attn_Wk': _L0_attn_in['Wk'], 'L0_attn_bk': _L0_attn_in['bk'], 'L0_attn_Wv': _L0_attn_in['Wv'], 'L0_attn_bv': _L0_attn_in['bv'], 'L0_attn_Wo': _L0_attn_in['Wo'], 'L0_attn_bo': _L0_attn_in['bo'], 'L0_attn_rel_emb': _L0_attn_in['rel_emb'], 'L0_ffn_scale': _L0_ffn_in['scale'], 'L0_ffn_gate_w': _L0_ffn_in['gate_w'], 'L0_ffn_gate_b': _L0_ffn_in['gate_b'], 'L0_ffn_w1': _L0_ffn_in['w1'], 'L0_ffn_b1': _L0_ffn_in['b1'], 'L0_ffn_w2': _L0_ffn_in['w2'], 'L0_ffn_b2': _L0_ffn_in['b2']}

def reference(x, L0_tok_w_qkv, L0_tok_b_qkv, L0_tok_w_proj, L0_tok_b_proj, L0_attn_Wq, L0_attn_bq, L0_attn_Wk, L0_attn_bk, L0_attn_Wv, L0_attn_bv, L0_attn_Wo, L0_attn_bo, L0_attn_rel_emb, L0_ffn_scale, L0_ffn_gate_w, L0_ffn_gate_b, L0_ffn_w1, L0_ffn_b1, L0_ffn_w2, L0_ffn_b2):
    import jax
    import jax.numpy as jnp

    def _L0_tok_ref(x, w_qkv, b_qkv, w_proj, b_proj):
        import jax, jax.numpy as jnp
        import numpy as np
        HEADS = 12
        Q_STRIDE = 4
        WINDOW_SIZE = 64
        B, N, dim = x.shape
        head_dim = dim // HEADS
        num_windows = N // (Q_STRIDE * WINDOW_SIZE)
        tpw = N // num_windows
        qkv = x @ w_qkv.T + b_qkv
        qkv = qkv.reshape(B, tpw, num_windows, 3, HEADS, head_dim)
        qkv = jnp.transpose(qkv, (3, 0, 4, 2, 1, 5))
        q, k, v = (qkv[0], qkv[1], qkv[2])
        q = q.reshape(B, HEADS, num_windows, Q_STRIDE, WINDOW_SIZE, head_dim).max(axis=3)
        scale = head_dim ** (-0.5)
        attn = jnp.einsum('bhwqd,bhwkd->bhwqk', q * scale, k)
        attn = jax.nn.softmax(attn, axis=-1)
        o = jnp.einsum('bhwqk,bhwkd->bhwqd', attn, v)
        o = jnp.transpose(o, (0, 3, 2, 1, 4)).reshape(B, WINDOW_SIZE * num_windows, dim)
        return o @ w_proj.T + b_proj

    def _L0_attn_ref(x, Wq, bq, Wk, bk, Wv, bv, Wo, bo, rel_emb):
        import jax, jax.numpy as jnp
        import numpy as np
        import math
        MAX_REL = 32
        B, S, D = x.shape
        dk = rel_emb.shape[-1]
        H = D // dk
        scale = 1.0 / math.sqrt(dk)

        def proj(W, b):
            return (x @ W + b).reshape(B, S, H, dk).transpose(0, 2, 1, 3)
        Q = proj(Wq, bq)
        K = proj(Wk, bk)
        V = proj(Wv, bv)
        pos = jnp.arange(S)
        rel_idx = jnp.clip(pos[:, None] - pos[None, :], -MAX_REL, MAX_REL) + MAX_REL
        rel = rel_emb[rel_idx]
        scores = jnp.einsum('bhqd,bhkd->bhqk', Q, K)
        scores = scores + jnp.einsum('bhqd,qkd->bhqk', Q, rel)
        scores = scores * scale
        attn = jax.nn.softmax(scores, axis=-1)
        ctx = jnp.einsum('bhqk,bhkd->bhqd', attn, V)
        ctx = ctx.transpose(0, 2, 1, 3).reshape(B, S, D)
        return ctx @ Wo + bo

    def _L0_ffn_ref(x, scale, gate_w, gate_b, w1, b1, w2, b2):
        import jax, jax.numpy as jnp
        import numpy as np
        B, S, H = (2, 256, 192)
        E, K, I = (16, 4, 192)
        ALPHA, LIMIT, EPS = (1.702, 7.0, 1e-05)

        def _swiglu(h):
            x_glu, x_lin = jnp.split(h, 2, axis=-1)
            x_glu = jnp.minimum(x_glu, LIMIT)
            x_lin = jnp.clip(x_lin, -LIMIT, LIMIT)
            return x_glu * jax.nn.sigmoid(ALPHA * x_glu) * (x_lin + 1.0)
        Bx, Sx, Hx = x.shape
        xf = x.astype(jnp.float32)
        t = xf * jax.lax.rsqrt(jnp.mean(xf * xf, axis=-1, keepdims=True) + EPS) * scale
        t = t.reshape(-1, Hx)
        T = t.shape[0]
        g = t @ gate_w.T + gate_b
        vals, idx = jax.lax.top_k(g, K)
        w = jax.nn.softmax(vals, axis=-1) / K
        full_w = jnp.zeros((T, E), jnp.float32).at[jnp.arange(T)[:, None], idx].set(w)
        h = jnp.einsum('th,ehf->tef', t, w1) + b1
        h = _swiglu(h)
        y = jnp.einsum('tei,eih->teh', h, w2) + b2
        out = jnp.einsum('teh,te->th', y, full_w) * K
        return x + out.astype(x.dtype).reshape(Bx, Sx, Hx)
    h = _L0_tok_ref(x, L0_tok_w_qkv, L0_tok_b_qkv, L0_tok_w_proj, L0_tok_b_proj)
    h = h + _L0_attn_ref(_layernorm(h, axis=-1), L0_attn_Wq, L0_attn_bq, L0_attn_Wk, L0_attn_bk, L0_attn_Wv, L0_attn_bv, L0_attn_Wo, L0_attn_bo, L0_attn_rel_emb)
    h = h + _L0_ffn_ref(_layernorm(h, axis=-1), L0_ffn_scale, L0_ffn_gate_w, L0_ffn_gate_b, L0_ffn_w1, L0_ffn_b1, L0_ffn_w2, L0_ffn_b2)
    return h

_drawn_inputs = setup_inputs


def setup_inputs(seed=0):
    import zlib

    import numpy as np

    out = dict(_drawn_inputs(seed))
    spreads = {'L0_tok_b_qkv': (0.0, 0.1),
     'L0_tok_b_proj': (0.0, 0.1),
     'L0_attn_bq': (0.0, 0.575),
     'L0_attn_bk': (0.0, 0.8),
     'L0_attn_bv': (0.0, 0.1),
     'L0_attn_bo': (0.0, 0.1),
     'L0_ffn_scale': (1.0, 0.6),
     'L0_ffn_gate_b': (0.0, 0.8)}
    factors = {'L0_ffn_gate_w': 4.91,
     'L0_ffn_w1': 4.697,
     'L0_ffn_b1': 8.0,
     'L0_ffn_w2': 4.915,
     'L0_ffn_b2': 8.0}
    for name, (base, spread) in spreads.items():
        noise = np.random.default_rng([zlib.crc32(name.encode()), seed]).standard_normal(out[name].shape)
        drawn = base * np.exp(spread * noise) if base else spread * noise
        out[name] = jnp.asarray(drawn.astype(out[name].dtype))
    for name, factor in factors.items():
        out[name] = (out[name] * factor).astype(out[name].dtype)
    return out
```

```python
import concourse.bass as bass
from concourse import mybir
from contextlib import ExitStack

F32 = mybir.dt.float32
F32R = mybir.dt.float32r
I32 = mybir.dt.int32
ALU = mybir.AluOpType
ACT = mybir.ActivationFunctionType
AX = mybir.AxisListType

B, N, D = 64, 256, 192
H, DK = 12, 16
Q = 64
STRIDE = N // Q
G, GC = 2, D // 2
PR = H // 2
PG = PR // G
PC = 2 * DK
MAXREL = 32
T = B * Q
NT = T // 128
TOK = 2 * N
REL = 128
E, TOPK, I = 16, 4, 192
EP = E // 2
M1 = 6 * 128
CH = 512
NC = T // CH
ALPHA, LIMIT, EPS = 1.702, 7.0, 1e-5
SCALE = DK ** -0.5


class At:

    def __init__(self, c, r=None):
        self.c, self.r, self.par = c, r, c % 2

    def __add__(self, d):
        return At(self.c + d, self.r)

    @property
    def n(self):
        return self.c if self.r is None else 2 * self.r + self.c

    @property
    def half(self):
        return self.c // 2 if self.r is None else self.r + self.c // 2

    def on(self, n):
        return self.r is not None or 0 <= self.c < n


def wait(e, sem, value):
    if not isinstance(value, int) or value > 0:
        e.wait_ge(sem, value)


def sweep(e, n, body, lead=1, lag=1):
    rounds = (n - 3 - lead) // 2
    for c in range(-lead, 3):
        body(At(c))
    with e.Fori(0, rounds) as r:
        for p in range(2):
            body(At(3 + p, r))
    for c in range(3 + 2 * rounds, n + lag):
        body(At(c))


class Chain:

    def __init__(self, e, sem, per, k):
        self.e, self.sem, self.base, self.m = e, sem, per * k.n, 0

    def __call__(self, ins):
        self.m += 1
        ins.then_inc(self.sem, 1)
        self.e.wait_ge(self.sem, self.base + self.m)


def tile_of(hall, k):
    return hall[:, bass.ds(k.n * D, D)]


def pool_attention(nc, hall, ident, hmask, qmask, a):
    with ExitStack() as c:
        sb = lambda n, s, d=F32: c.enter_context(nc.sbuf_tensor(n, s, d))
        ps = lambda n, s: c.enter_context(nc.psum_tensor(n, s, F32))
        sem = lambda n: c.enter_context(nc.semaphore(n))
        x = sb("p_x", [128, 2, 2, TOK])
        xah = sb("p_xA_high", [128, 2, TOK], F32R)
        xal = sb("p_xA_low", [128, 2, TOK], F32R)
        xbs = sb("p_xB_high_low", [128, 2, TOK], F32R)
        wqk = sb("p_wqk", [128, 2, 2 * D])
        wqkh = sb("p_wqk_high", [128, 2, 2 * D], F32R)
        wqkl = sb("p_wqk_low", [128, 2, 2 * D], F32R)
        wv = sb("p_wv", [128, 2, D])
        wproj = sb("p_wproj", [GC, G, D])
        bqk = sb("p_bqk", [GC, 2 * G])
        bv = sb("p_bv", [128, D])
        bproj = sb("p_bproj", [128, D])
        qmax = sb("p_qmax", [GC, G, 2, Q])
        qpad = sb("p_qpad", [GC, 2, G, 2, PG * 2 * Q])
        kT = sb("p_kT", [GC, 2, G, TOK])
        v = sb("p_v", [128, 2, 4, D])
        p = sb("p_p", [128, 2, PR, N])
        pT = sb("p_pT", [128, 2, PR * 2, 128])
        negmax = sb("p_negmax", [128, 2, PR])
        total = sb("p_total", [128, 2, PR])
        inv = sb("p_inv", [128, 2, PR])
        idle = sb("p_idle", [128, 2])
        osel = sb("p_osel", [GC, G * 2, Q])
        oT = sb("p_oT", [GC, G, 2 * Q])
        ringA = [ps(f"p_psA{n}", [128, 512]) for n in range(2)]
        scores = [ps(f"p_psS{n}", [128, 2, N]) for n in range(3)]
        ringT = [ps(f"p_psT{n}", [128, 4, 128]) for n in range(2)]
        psO = ps("p_psO", [128, 512])

        s_w = sem("p_weights")
        s_zero = sem("p_wv_zeros")
        s_wh = sem("p_wqk_high_done")
        s_wl = sem("p_wqk_low_done")
        s_xh = sem("p_x_high_done")
        s_xal = sem("p_xA_low_done")
        s_xbl = sem("p_xB_low_done")
        s_x = [sem(f"p_x_in{n}") for n in range(2)]
        s_qk = sem("p_qk_mm")
        s_v = sem("p_v_mm")
        s_qmax = sem("p_qmax_done")
        s_qpad = sem("p_qpad_done")
        s_kT = sem("p_kT_done")
        s_vsb = sem("p_v_done")
        s_s = sem("p_scores_mm")
        s_mx = sem("p_max_done")
        s_exp = sem("p_exp_done")
        s_inv = sem("p_inv_done")
        s_p = sem("p_probs_done")
        s_t = sem("p_transposed")
        s_ta = sem("p_pT_by_act")
        s_tv = sem("p_pT_by_dve")
        s_pv = sem("p_pv_mm")
        s_osel = sem("p_osel_half")
        s_oT = sem("p_oT_done")
        s_out = sem("p_out_mm")
        s_h = sem("p_h_done")

        loads = ((wqk[:, 0, :], a["wqkvT"][0:128, 0:2 * D]), (wqk[0:64, 1, :], a["wqkvT"][128:D, 0:2 * D]),
                 (wqk[64:128, 1, :], a["wqkvT"][128:D, 0:2 * D]), (wv[:, 0, :], a["wqkvT"][0:128, 2 * D:]),
                 (wv[0:64, 1, :], a["wqkvT"][128:D, 2 * D:]), (wproj[:, :, :], a["wprojT"]),
                 (bqk[:, :], a["bqk"]), (bv[:, :], a["bv"]), (bproj[:, :], a["bproj"]))
        W_ALL = 16 * len(loads)

        with nc.Block() as block:

            @block.sync
            def _(sp):
                sp.wait_ge(s_zero, 1)
                for dst, src in loads:
                    sp.dma_start(dst, src).then_inc(s_w, 16)

                def load(k):
                    if not k.on(NT):
                        return
                    wait(sp, s_v, 2 * (k.n - 1))
                    wait(sp, s_xal, k.n - 1)
                    wait(sp, s_xbl, k.n - 1)
                    cols = bass.ds(k.n * TOK, TOK)
                    for dst, src in ((x[:, k.par, 0, :], a["xT"][0:128, cols]),
                                     (x[0:64, k.par, 1, :], a["xT"][128:D, cols]),
                                     (x[64:128, k.par, 1, :], a["xT"][128:D, cols])):
                        sp.dma_start(dst, src).then_inc(s_x[k.par], 16)

                sweep(sp, NT, load, lead=0, lag=0)

            @block.tensor
            def _(pe):
                pe.wait_ge(s_w, W_ALL)
                pe.wait_ge(s_wl, 1)

                def project_qk(k):
                    if not k.on(NT):
                        return
                    pe.wait_ge(s_xh, 2 * k.n + 2)
                    pe.wait_ge(s_xal, k.n + 1)
                    pe.wait_ge(s_xbl, k.n + 1)
                    for n in range(4):
                        which, g = n // G, n % G
                        if n < 2:
                            wait(pe, s_vsb, 2 * (k.n - 1) + n + 1)
                        else:
                            pe.wait_ge(s_qmax, 2 * k.n + g + 1)
                        w = slice(which * D + g * GC, which * D + (g + 1) * GC)
                        parts = ((wqkh[:, 0, w], xah), (wqkh[:, 0, w], xal), (wqkl[:, 0, w], xah),
                                 (wqkh[:, 1, w], xbs), (wqkl[:, 1, w], xbs))
                        for q, (lhsT, rhs) in enumerate(parts):
                            last = nc.tensor.matmul(ringA[n % 2][0:GC, :], lhsT, rhs[:, k.par, :],
                                                    start=q == 0, stop=q == len(parts) - 1)
                        last.then_inc(s_qk, 1)

                def project_v(k):
                    if not k.on(NT):
                        return
                    for t in range(4):
                        if t % 2 == 0:
                            pe.wait_ge(s_kT, 2 * k.n + t // 2 + 1)
                        for h in range(2):
                            last = nc.tensor.matmul(
                                ringA[t // 2][:, (t % 2) * D:(t % 2 + 1) * D],
                                x[:, k.par, h, t * 128:(t + 1) * 128], wv[:, h, :],
                                start=h == 0, stop=h == 1)
                        if t % 2:
                            last.then_inc(s_v, 1)

                def score(k, b):
                    if not k.on(NT):
                        return
                    if b == 0:
                        pe.wait_ge(s_qpad, 4 * k.n + 4)
                        pe.wait_ge(s_kT, 2 * k.n + 2)
                    for j in range(PR):
                        if j % 2 == 0:
                            wait(pe, s_exp, 12 * k.n + 6 * (b - 1) + j + 2)
                        g, i = j // PG, j % PG
                        last = nc.tensor.matmul(
                            scores[j // 2][:, j % 2, :], qpad[:, k.par, g, b, i * 128:(i + 1) * 128],
                            kT[:, k.par, g, b * N:(b + 1) * N], start=True, stop=True)
                        if j % 2:
                            last.then_inc(s_s, 1)

                def weigh(k, b):
                    if not k.on(NT):
                        return
                    for u in range(3):
                        n = 3 * b + u
                        s, per, before = ((s_tv, 2, 0), (s_ta, 4, 0), (s_ta, 4, 1),
                                          (s_tv, 2, 1), (s_ta, 4, 2), (s_ta, 4, 3))[n]
                        wait(pe, s, per * k.n + before)
                        pe.wait_ge(s_p, 6 * k.n + n + 1)
                        for m in range(4):
                            last = nc.tensor.transpose(
                                ringT[n % 2][:, m, :],
                                p[:, b, 2 * u + m // 2, (m % 2) * 128:(m % 2 + 1) * 128], ident[:, :])
                        last.then_inc(s_t, 1)
                    if b == 0:
                        wait(pe, s_h, k.n)
                    for j in range(PR):
                        if j % 2 == 0:
                            u, n = j // 2, 3 * b + j // 2
                            if u == 1:
                                pe.wait_ge(s_tv, 2 * k.n + b + 1)
                            else:
                                pe.wait_ge(s_ta, 4 * k.n + 2 * b + u // 2 + 1)
                        if j == 0:
                            pe.wait_ge(s_vsb, 2 * k.n + 2)
                        g, i = j // PG, j % PG
                        for kt in range(2):
                            last = nc.tensor.matmul(
                                psO[i * PC:(i + 1) * PC, (2 * g + b) * 128:(2 * g + b + 1) * 128],
                                v[:, k.par, 2 * b + kt, j * PC:(j + 1) * PC], pT[:, b, 2 * j + kt, :],
                                start=kt == 0, stop=kt == 1)
                    last.then_inc(s_pv, 1)

                def project_out(k):
                    if not k.on(NT):
                        return
                    pe.wait_ge(s_oT, k.n + 1)
                    for g in range(G):
                        last = nc.tensor.matmul(psO[:, 0:D], oT[:, g, :], wproj[:, g, :],
                                                start=g == 0, stop=g == G - 1)
                    last.then_inc(s_out, 1)

                def body(i):
                    score(i, 0)
                    project_qk(i + 1)
                    weigh(i + -1, 1)
                    score(i, 1)
                    project_out(i + -1)
                    project_v(i + 1)
                    weigh(i, 0)

                sweep(pe, NT, body)

            @block.scalar
            def _(act):
                act.wait_ge(s_w, W_ALL)
                nc.scalar.activation(wqkh[:, :, :], wqk[:, :, :], ACT.Copy).then_inc(s_wh, 1)

                def round_x(k):
                    if not k.on(NT):
                        return
                    act.wait_ge(s_x[k.par], 48 * (k.half + 1))
                    nc.scalar.activation(xah[:, k.par, :], x[:, k.par, 0, :], ACT.Copy).then_inc(s_xh, 1)
                    nc.scalar.activation(xbs[:, k.par, :], x[:, k.par, 1, :], ACT.Copy).then_inc(s_xh, 1)

                def exps(k, b):
                    if not k.on(NT):
                        return
                    for j in range(PR):
                        if j % 2 == 0:
                            act.wait_ge(s_mx, 6 * k.n + 3 * b + j // 2 + 1)
                        nc.scalar.activation(p[:, b, j, :], scores[j // 2][:, j % 2, :], ACT.Exp,
                                             bias=negmax[:, b, j:j + 1], scale=1.0,
                                             accum_out=total[:, b, j:j + 1]).then_inc(s_exp, 1)

                def copy_k(k):
                    if not k.on(NT):
                        return
                    for g in range(G):
                        act.wait_ge(s_qk, 4 * k.n + 2 + g + 1)
                        nc.scalar.activation(kT[:, k.par, g, :], ringA[g][0:GC, :], ACT.Identity,
                                             bias=bqk[:, G + g:G + g + 1]).then_inc(s_kT, 1)

                def copy_pT(k, b):
                    if not k.on(NT):
                        return
                    for u in (0, 2):
                        n = 3 * b + u
                        act.wait_ge(s_t, 6 * k.n + n + 1)
                        nc.scalar.activation(pT[:, b, 4 * u:4 * u + 4, :], ringT[n % 2][:, :, :],
                                             ACT.Copy).then_inc(s_ta, 1)

                def body(i):
                    exps(i, 0)
                    copy_k(i + 1)
                    copy_pT(i + -1, 1)
                    round_x(i + 2)
                    exps(i, 1)
                    copy_pT(i, 0)

                sweep(act, NT, body, lead=2)

            @block.vector
            def _(dve):
                dve.wait_ge(s_w, W_ALL)

                def rest_of_x(k):
                    if not k.on(NT):
                        return
                    dve.wait_ge(s_xh, 2 * k.n + 2)
                    low = xbs[64:128, k.par, :]
                    nc.vector.tensor_tensor(low, x[64:128, k.par, 1, :], low.bitcast(F32), ALU.subtract)\
                      .then_inc(s_xbl, 1)

                def pool_q(k):
                    if not k.on(NT):
                        return
                    for g in range(G):
                        dve.wait_ge(s_qk, 4 * k.n + g + 1)
                        nc.vector.tensor_reduce(
                            qmax[:, g, :, :],
                            ringA[g][0:GC, :].rearrange("p (b s w) -> p b w s", b=2, s=STRIDE),
                            AX.X, ALU.max).then_inc(s_qmax, 1)
                    for g in range(G):
                        dve.wait_ge(s_qmax, 2 * k.n + g + 1)
                        for b in range(2):
                            nc.vector.scalar_tensor_tensor(
                                out=qpad[:, k.par, g, b, :].rearrange("p (m w) -> p m w", w=Q),
                                in0=qmax[:, g, b, :].unsqueeze(1).broadcast_to([GC, 2 * PG, Q]),
                                scalar=bqk[:, g:g + 1], in1=qmask[:, :, :],
                                op0=ALU.add, op1=ALU.mult).then_inc(s_qpad, 1)

                def row_max(k, b):
                    if not k.on(NT):
                        return
                    for u in range(3):
                        dve.wait_ge(s_s, 6 * k.n + 3 * b + u + 1)
                        nc.vector.tensor_reduce(negmax[:, b, 2 * u:2 * u + 2], scores[u][:, :, :], AX.X,
                                                ALU.max, negate=True).then_inc(s_mx, 1)

                def invert(k, b):
                    if not k.on(NT):
                        return
                    dve.wait_ge(s_exp, 12 * k.n + 6 * b + 6)
                    nc.vector.reciprocal(inv[:, b, :], total[:, b, :]).then_inc(s_inv, 1)

                def copy_pT(k, b):
                    if not k.on(NT):
                        return
                    n = 3 * b + 1
                    dve.wait_ge(s_t, 6 * k.n + n + 1)
                    nc.vector.tensor_copy(pT[:, b, 4:8, :], ringT[n % 2][:, :, :]).then_inc(s_tv, 1)

                def select_heads(k):
                    if not k.on(NT):
                        return
                    dve.wait_ge(s_pv, 2 * k.n + 2)
                    o = psO[0:GC, :].rearrange("p (m h w) -> p m h w", h=2, w=Q)
                    nc.vector.tensor_scalar(osel[:, :, :], o[:, :, 0, :], hmask[:, 0:1], None, ALU.mult)\
                      .then_inc(s_osel, 1)
                    dve.wait_ge(s_osel, k.n + 1)
                    nc.vector.scalar_tensor_tensor(
                        out=oT[:, :, :].rearrange("p g (b w) -> p (g b) w", w=Q), in0=o[:, :, 1, :],
                        scalar=hmask[:, 1:2], in1=osel[:, :, :], op0=ALU.mult, op1=ALU.add).then_inc(s_oT, 1)

                def copy_out(k):
                    if not k.on(NT):
                        return
                    dve.wait_ge(s_out, k.n + 1)
                    nc.vector.tensor_tensor(tile_of(hall, k), psO[:, 0:D], bproj[:, :], ALU.add)\
                      .then_inc(s_h, 1)

                def copy_v(k):
                    if not k.on(NT):
                        return
                    for t in range(2):
                        dve.wait_ge(s_v, 2 * k.n + t + 1)
                        nc.vector.tensor_tensor(
                            v[:, k.par, 2 * t:2 * t + 2, :],
                            ringA[t][:, 0:2 * D].rearrange("p (m n) -> p m n", n=D),
                            bv[:, :].unsqueeze(1).broadcast_to([128, 2, D]), ALU.add).then_inc(s_vsb, 1)

                def body(i):
                    row_max(i, 0)
                    pool_q(i + 1)
                    invert(i, 0)
                    copy_pT(i + -1, 1)
                    select_heads(i + -1)
                    row_max(i, 1)
                    rest_of_x(i + 2)
                    copy_out(i + -1)
                    copy_v(i + 1)
                    invert(i, 1)
                    copy_pT(i, 0)

                sweep(dve, NT, body, lead=2)

            @block.gpsimd
            def _(pool):
                nc.gpsimd.memset(wv[:, 1, :], 0.0).then_inc(s_zero, 1)
                pool.wait_ge(s_wh, 1)
                nc.gpsimd.tensor_tensor(wqkl[:, :, :], wqk[:, :, :], wqkh[:, :, :].bitcast(F32), ALU.subtract)\
                  .then_inc(s_wl, 1)

                def rest_of_x(k):
                    if not k.on(NT):
                        return
                    pool.wait_ge(s_xh, 2 * k.n + 2)
                    nc.gpsimd.tensor_tensor(xal[:, k.par, :], x[:, k.par, 0, :], xah[:, k.par, :].bitcast(F32),
                                            ALU.subtract).then_inc(s_xal, 1)

                def normalise(k):
                    if not k.on(NT):
                        return
                    for b in range(2):
                        pool.wait_ge(s_inv, 2 * k.n + b + 1)
                        nc.gpsimd.tensor_tensor(idle[:, b:b + 1], inv[:, b, 0:1], inv[:, b, 0:1], ALU.mult)
                        for j in range(PR):
                            last = nc.gpsimd.tensor_scalar(p[:, b, j, :], p[:, b, j, :], inv[:, b, j:j + 1],
                                                           1.0, ALU.mult, ALU.mult)
                            if j % 2:
                                last.then_inc(s_p, 1)

                def body(i):
                    normalise(i)
                    rest_of_x(i + 2)

                sweep(pool, NT, body, lead=2, lag=0)


def local_attention(nc, hall, tAh, tAl, tBs, wT, ident, hmask, qmask, scratch, a):
    with ExitStack() as c:
        sb = lambda n, s, d=F32: c.enter_context(nc.sbuf_tensor(n, s, d))
        ps = lambda n, s: c.enter_context(nc.psum_tensor(n, s, F32))
        sem = lambda n: c.enter_context(nc.semaphore(n))
        wqkv = sb("l_wqkv", [GC, G, 3 * D])
        wo = sb("l_wo", [GC, G, D])
        bqk = sb("l_bqk", [GC, 2 * G])
        bv = sb("l_bv", [128, D])
        bo = sb("l_bo", [128, D])
        tscale = sb("l_tscale", [128, D])
        gw = sb("l_gw", [128, 2, E])
        gb = sb("l_gb", [128, E])
        lower = sb("l_lower", [128, E, E], I32)
        b2 = sb("l_b2", [2 * E, D])
        mhalf = sb("l_minus_half", [128, 1])
        idle = sb("l_idle", [128, 3])
        stats = sb("l_stats", [128, 6])
        meanvar = sb("l_meanvar", [128, 2, 2])
        vareps = sb("l_vareps", [128, 2])
        rstd = sb("l_rstd", [128, 2])
        xn = sb("l_xn", [128, D])
        xnT = sb("l_xnT", [GC, G, 128])
        qpad = sb("l_qpad", [GC, G, 2, PG * 2 * Q])
        kr = sb("l_k_rel", [GC, G, 2, Q + REL])
        qb = sb("l_q", [GC, G, 2 * Q])
        v = sb("l_v", [128, 2, 2, D])
        sq = sb("l_sq", [128, 2, 2, PR, Q + REL])
        bias = sb("l_bias", [128, 2, 2, PR, Q])
        z = sb("l_z", [128, PR, 2, Q])
        p2 = sb("l_p", [128, PR, 2, Q])
        rowmax = sb("l_rowmax", [128, PR * 2])
        total = sb("l_total", [128, PR * 2])
        inv = sb("l_inv", [128, PR * 2])
        pT = sb("l_pT", [128, PR, 128])
        osel = sb("l_osel", [GC, G * 2, Q])
        oT = sb("l_oT", [GC, G, 2 * Q])
        h2 = sb("l_h2", [128, D])
        hn = sb("l_hn", [128, D])
        square = sb("l_square", [128, D])
        ss = sb("l_ss", [128, 1])
        mseps = sb("l_mseps", [128, 1])
        rrms = sb("l_rrms", [128, 1])
        t = sb("l_t", [128, 256])
        tT = sb("l_tT", [128, 2, 128])
        tBr = sb("l_tB_round", [128, 128], F32R)
        gate = sb("l_gate", [128, E])
        above = sb("l_above", [128, E, E])
        notbelow = sb("l_notbelow", [128, E, E])
        rank = sb("l_rank", [128, E])
        gmax = sb("l_gmax", [128, 1])
        gexp = sb("l_gexp", [128, E])
        chosen = sb("l_chosen", [128, E])
        gsum = sb("l_gsum", [128, 1])
        ginv = sb("l_ginv", [128, 1])
        w = sb("l_w", [128, E])
        w32 = sb("l_w32", [128, 2 * E], F32R)
        w32T = sb("l_w32T", [2 * E, 128])
        ringA = [ps(f"l_psA{n}", [128, 512]) for n in range(2)]
        ringS = [ps(f"l_psS{n}", [128, 2, Q + REL]) for n in range(3)]
        psT = ps("l_psT", [128, 4, 128])
        psO = ps("l_psO", [128, G * 2, 128])
        psH = ps("l_psH", [128, 512])

        s_w = sem("l_weights")
        s_zero = sem("l_gate_zeros")
        s_vz = sem("l_v_zeros")
        s_half = sem("l_minus_half_done")
        s_ln = sem("l_ln_steps")
        s_ve = sem("l_vareps_done")
        s_rstd = sem("l_rstd_done")
        s_xn = sem("l_xn_done")
        s_xT = sem("l_xn_transposed")
        s_xnT = sem("l_xnT_done")
        s_q = sem("l_q_mm")
        s_qb = sem("l_q_done")
        s_qpad = sem("l_qpad_done")
        s_k = sem("l_k_mm")
        s_kr = sem("l_k_done")
        s_v = sem("l_v_mm")
        s_vsb = sem("l_v_done")
        s_s = sem("l_scores_mm")
        s_sq = sem("l_sq_done")
        s_wr = [sem(f"l_rel_written{n}") for n in range(2)]
        s_rd = [sem(f"l_rel_read{n}") for n in range(2)]
        s_z = sem("l_z_done")
        s_sm = sem("l_softmax_steps")
        s_sub = sem("l_z_less_max")
        s_exp = sem("l_exp_done")
        s_inv = sem("l_inv_done")
        s_p = sem("l_probs_done")
        s_t = sem("l_p_transposed")
        s_pTa = sem("l_pT_first_done")
        s_pTb = sem("l_pT_rest_done")
        s_pv = sem("l_pv_mm")
        s_os = sem("l_osel_steps")
        s_oT = sem("l_oT_done")
        s_out = sem("l_out_mm")
        s_h2 = sem("l_h2_done")
        s_n2 = sem("l_norm2_steps")
        s_ve2 = sem("l_vareps2_done")
        s_rstd2 = sem("l_rstd2_done")
        s_hn = sem("l_hn_done")
        s_ss = sem("l_ss_done")
        s_ms = sem("l_mseps_done")
        s_rr = sem("l_rrms_done")
        s_tt = sem("l_t_done")
        s_tTm = sem("l_t_transposed")
        s_tT = sem("l_tT_done")
        s_sp = sem("l_split_done")
        s_gm = sem("l_gate_mm")
        s_g = sem("l_gate_copied")
        s_gs = sem("l_gate_steps")
        s_gmx = sem("l_gmax_done")
        s_gex = sem("l_gexp_done")
        s_w32 = sem("l_w32_done")
        s_wTm = sem("l_w32_transposed")
        s_wT = sem("l_w32T_done")
        s_b2m = sem("l_b2_mm")
        s_b2 = sem("l_b2_added")

        loads = ((wqkv[:, :, :], a["awqkv"]), (wo[:, :, :], a["awo"]), (bqk[:, :], a["abqk"]),
                 (bv[:, :], a["abv"]), (bo[:, :], a["abo"]), (tscale[:, :], a["tscale"]),
                 (gw[:, 0, :], a["gwT"][0:128, :]), (gw[0:D - 128, 1, :], a["gwT"][128:D, :]),
                 (gb[:, :], a["gb"]), (lower[:, :, :], a["lower"]), (b2[:, :], a["b2dup"]),
                 (kr[:, 0, 0, Q:], a["relT"]), (kr[:, 0, 1, Q:], a["relT"]),
                 (kr[:, 1, 0, Q:], a["relT"]), (kr[:, 1, 1, Q:], a["relT"]))
        W_ALL = 16 * len(loads)

        with nc.Block() as block:

            @block.sync
            def _(sp):
                sp.wait_ge(s_zero, 1)
                for dst, src in loads:
                    sp.dma_start(dst, src).then_inc(s_w, 16)

                sp.wait_ge(s_w, W_ALL)

                def skew(k):
                    par = k.par
                    sp.wait_ge(s_sq, 6 * k.n + 3)
                    sp.dma_start(scratch[par, 0, :, :, :], sq[:, par, 0, :, Q:]).then_inc(s_wr[par], 16)
                    sp.wait_ge(s_sq, 6 * k.n + 6)
                    sp.dma_start(scratch[par, 1, :, :, :], sq[:, par, 1, :, Q:]).then_inc(s_wr[par], 16)
                    sp.wait_ge(s_wr[par], 32 * (k.half + 1))
                    row = PR * REL
                    for b in range(2):
                        for h in range(2):
                            src = bass.AP(scratch.tensor, ((par * 2 + b) * 128 + h * Q) * row + Q - 1,
                                          [[row - 1, Q], [REL, PR], [1, Q]])
                            sp.dma_start(bias[h * Q:(h + 1) * Q, par, b, :, :], src).then_inc(s_rd[par], 16)

                sweep(sp, NT, skew, lead=0, lag=0)

            @block.tensor
            def _(pe):
                pe.wait_ge(s_w, W_ALL)

                def transpose_xn(k):
                    if not k.on(NT):
                        return
                    pe.wait_ge(s_xn, k.n + 1)
                    wait(pe, s_kr, 2 * k.n)
                    for g in range(G):
                        last = nc.tensor.transpose(ringA[0][0:GC, g * 128:(g + 1) * 128],
                                                   xn[:, g * GC:(g + 1) * GC], ident[:, :])
                    last.then_inc(s_xT, 1)

                def project_kq(k):
                    if not k.on(NT):
                        return
                    pe.wait_ge(s_xnT, k.n + 1)
                    for which, bank, done in ((1, 0, s_k), (0, 1, s_q)):
                        if which == 0:
                            wait(pe, s_vsb, 2 * k.n)
                        for g in range(G):
                            for h in range(G):
                                last = nc.tensor.matmul(
                                    ringA[bank][0:GC, g * 128:(g + 1) * 128],
                                    wqkv[:, h, which * D + g * GC:which * D + (g + 1) * GC], xnT[:, h, :],
                                    start=h == 0, stop=h == G - 1)
                        last.then_inc(done, 1)

                def project_v(k):
                    if not k.on(NT):
                        return
                    pe.wait_ge(s_qb, 2 * k.n + 2)
                    for h in range(G):
                        last = nc.tensor.matmul(ringA[1][:, 0:D], xnT[:, h, :], wqkv[:, h, 2 * D:3 * D],
                                                start=h == 0, stop=h == G - 1)
                    last.then_inc(s_v, 1)

                def score(k):
                    if not k.on(NT):
                        return
                    pe.wait_ge(s_qpad, 2 * k.n + 2)
                    pe.wait_ge(s_kr, 2 * k.n + 2)
                    for u in range(6):
                        b = u // 3
                        wait(pe, s_sq, 6 * k.n + u - 2)
                        for m in range(2):
                            j = 2 * (u % 3) + m
                            g, i = j // PG, j % PG
                            last = nc.tensor.matmul(ringS[u % 3][:, m, :], qpad[:, g, b, i * 128:(i + 1) * 128],
                                                    kr[:, g, b, :], start=True, stop=True)
                        last.then_inc(s_s, 1)

                def weigh(k):
                    if not k.on(NT):
                        return
                    wait(pe, s_oT, k.n)
                    pe.wait_ge(s_p, k.n + 1)
                    for r, js in ((0, range(0, 4)), (1, range(4, 6))):
                        wait(pe, (s_pTb, s_pTa)[r], k.n + r)
                        for j in js:
                            last = nc.tensor.transpose(psT[:, j % 4, :],
                                                       p2[:, j, :, :].rearrange("p b w -> p (b w)"), ident[:, :])
                        last.then_inc(s_t, 1)
                    for j in range(PR):
                        if j == 4:
                            pe.wait_ge(s_pTb, k.n + 1)
                        g, i = j // PG, j % PG
                        for b in range(2):
                            last = nc.tensor.matmul(psO[i * PC:(i + 1) * PC, 2 * g + b, :],
                                                    v[:, k.par, b, j * PC:(j + 1) * PC], pT[:, j, :],
                                                    start=True, stop=True)
                    last.then_inc(s_pv, 1)

                def project_out(k):
                    if not k.on(NT):
                        return
                    wait(pe, s_b2, k.n)
                    pe.wait_ge(s_oT, k.n + 1)
                    for g in range(G):
                        last = nc.tensor.matmul(psH[:, 0:D], oT[:, g, :], wo[:, g, :],
                                                start=g == 0, stop=g == G - 1)
                    last.then_inc(s_out, 1)

                def transpose_t(k):
                    if not k.on(NT):
                        return
                    pe.wait_ge(s_tt, 2 * k.n + 2)
                    for m in range(2):
                        last = nc.tensor.transpose(psH[:, m * 128:(m + 1) * 128], t[:, m * 128:(m + 1) * 128],
                                                   ident[:, :])
                    last.then_inc(s_tTm, 1)

                def gates(k):
                    if not k.on(NT):
                        return
                    pe.wait_ge(s_tT, k.n + 1)
                    for m in range(2):
                        last = nc.tensor.matmul(psH[:, 0:E], tT[:, m, :], gw[:, m, :], start=m == 0, stop=m == 1)
                    last.then_inc(s_gm, 1)

                def transpose_w(k):
                    if not k.on(NT):
                        return
                    pe.wait_ge(s_w32, k.n + 1)
                    nc.tensor.transpose(psH[0:2 * E, 0:128], w32[:, :].bitcast(F32), ident[:, :])\
                      .then_inc(s_wTm, 1)

                def expert_bias(k):
                    if not k.on(NT):
                        return
                    pe.wait_ge(s_wT, k.n + 1)
                    nc.tensor.matmul(psH[:, 0:D], w32T[:, :], b2[:, :], start=True, stop=True).then_inc(s_b2m, 1)

                def body(i):
                    score(i)
                    transpose_t(i + -2)
                    project_kq(i + 1)
                    gates(i + -2)
                    weigh(i + -1)
                    transpose_w(i + -2)
                    project_v(i + 1)
                    expert_bias(i + -2)
                    transpose_xn(i + 2)
                    project_out(i + -1)

                sweep(pe, NT, body, lead=2, lag=2)

            @block.scalar
            def _(act):
                act.wait_ge(s_w, W_ALL)

                def copy_xnT(k):
                    if not k.on(NT):
                        return
                    act.wait_ge(s_xT, k.n + 1)
                    nc.scalar.activation(xnT[:, :, :], ringA[0][0:GC, 0:G * 128], ACT.Copy).then_inc(s_xnT, 1)

                def copy_k(k):
                    if not k.on(NT):
                        return
                    act.wait_ge(s_k, k.n + 1)
                    for g in range(G):
                        nc.scalar.activation(
                            kr[:, g, :, 0:Q],
                            ringA[0][0:GC, g * 128:(g + 1) * 128].rearrange("p (b w) -> p b w", b=2),
                            ACT.Identity, bias=bqk[:, G + g:G + g + 1]).then_inc(s_kr, 1)

                def copy_q(k):
                    if not k.on(NT):
                        return
                    act.wait_ge(s_q, k.n + 1)
                    for g in range(G):
                        nc.scalar.activation(qb[:, g, :], ringA[1][0:GC, g * 128:(g + 1) * 128], ACT.Identity,
                                             bias=bqk[:, g:g + 1]).then_inc(s_qb, 1)

                def copy_scores(k):
                    if not k.on(NT):
                        return
                    wait(act, s_wr[k.par], 32 * k.half)
                    for u in range(6):
                        act.wait_ge(s_s, 6 * k.n + u + 1)
                        j = 2 * (u % 3)
                        nc.scalar.activation(sq[:, k.par, u // 3, j:j + 2, :], ringS[u % 3][:, :, :], ACT.Copy)\
                          .then_inc(s_sq, 1)

                def exps(k):
                    if not k.on(NT):
                        return
                    act.wait_ge(s_sub, k.n + 1)
                    nc.scalar.activation(z[:, :, :, :], z[:, :, :, :], ACT.Exp).then_inc(s_exp, 1)

                def copy_pT(k):
                    if not k.on(NT):
                        return
                    for r, (lo, hi) in enumerate(((0, 4), (4, 6))):
                        act.wait_ge(s_t, 2 * k.n + r + 1)
                        nc.scalar.activation(pT[:, lo:hi, :], psT[:, 0:hi - lo, :], ACT.Copy)\
                          .then_inc((s_pTa, s_pTb)[r], 1)

                def copy_tT(k):
                    if not k.on(NT):
                        return
                    act.wait_ge(s_tTm, k.n + 1)
                    nc.scalar.activation(tT[:, :, :], psH[:, 0:256], ACT.Copy).then_inc(s_tT, 1)

                def gate_exp(k):
                    if not k.on(NT):
                        return
                    act.wait_ge(s_gmx, k.n + 1)
                    nc.scalar.activation(gexp[:, :], gate[:, :], ACT.Exp, bias=gmax[:, 0:1]).then_inc(s_gex, 1)

                def body(i):
                    exps(i + -1)
                    copy_scores(i)
                    copy_tT(i + -2)
                    copy_k(i + 1)
                    copy_q(i + 1)
                    gate_exp(i + -2)
                    copy_pT(i + -1)
                    copy_xnT(i + 2)

                sweep(act, NT, body, lead=2, lag=2)

            @block.vector
            def _(dve):
                nc.vector.memset(mhalf[:, :], -0.5).then_inc(s_half, 1)
                dve.wait_ge(s_w, W_ALL)
                dve.wait_ge(s_vz, 1)

                def carry(n):
                    nc.vector.memset(idle[:, n:n + 1], 0.0)

                def norm1_stats(k):
                    if not k.on(NT):
                        return
                    do = Chain(dve, s_ln, 2, k)
                    do(nc.vector.bn_stats(stats[:, :], tile_of(hall, k)))
                    carry(0)
                    do(nc.vector.bn_aggr(meanvar[:, 0, :], stats[:, :]))
                    nc.vector.tensor_scalar(vareps[:, 0:1], meanvar[:, 0, 1:2], EPS, None, ALU.add)\
                      .then_inc(s_ve, 1)

                def norm1(k):
                    if not k.on(NT):
                        return
                    dve.wait_ge(s_rstd, k.n + 1)
                    wait(dve, s_xT, k.n)
                    nc.vector.tensor_scalar(xn[:, :], tile_of(hall, k), meanvar[:, 0, 0:1], rstd[:, 0:1],
                                            ALU.subtract, ALU.mult).then_inc(s_xn, 1)

                def copy_v(k):
                    if not k.on(NT):
                        return
                    dve.wait_ge(s_v, k.n + 1)
                    for b in range(2):
                        rows = slice(b * Q, (b + 1) * Q)
                        nc.vector.tensor_tensor(v[rows, k.par, b, :], ringA[1][rows, 0:D], bv[rows, :], ALU.add)\
                          .then_inc(s_vsb, 1)

                zr = z[:, :, :, :].rearrange("p j b w -> p (j b) w")

                def less_max(k):
                    if not k.on(NT):
                        return
                    dve.wait_ge(s_z, k.n + 1)
                    do = Chain(dve, s_sm, 2, k)
                    do(nc.vector.tensor_reduce(rowmax[:, :], zr, AX.X, ALU.max))
                    nc.vector.tensor_tensor(zr, zr, rowmax[:, :].unsqueeze(2).broadcast_to([128, 2 * PR, Q]),
                                            ALU.subtract).then_inc(s_sub, 1)

                def row_sum(k):
                    if not k.on(NT):
                        return
                    dve.wait_ge(s_exp, k.n + 1)
                    nc.vector.tensor_reduce(total[:, :], zr, AX.X, ALU.add).then_inc(s_sm, 1)
                    dve.wait_ge(s_sm, 2 * k.n + 2)
                    nc.vector.reciprocal(inv[:, :], total[:, :]).then_inc(s_inv, 1)

                def select_heads(k):
                    if not k.on(NT):
                        return
                    dve.wait_ge(s_pv, k.n + 1)
                    o = psO[0:GC, :, :].rearrange("p m (h w) -> p m h w", w=Q)
                    nc.vector.tensor_scalar(osel[:, :, :], o[:, :, 0, :], hmask[:, 0:1], None, ALU.mult)\
                      .then_inc(s_os, 1)
                    dve.wait_ge(s_os, k.n + 1)
                    nc.vector.scalar_tensor_tensor(
                        out=oT[:, :, :].rearrange("p g (b w) -> p (g b) w", w=Q), in0=o[:, :, 1, :],
                        scalar=hmask[:, 1:2], in1=osel[:, :, :], op0=ALU.mult, op1=ALU.add).then_inc(s_oT, 1)

                def norm2_stats(k):
                    if not k.on(NT):
                        return
                    do = Chain(dve, s_n2, 5, k)
                    do(nc.vector.tensor_tensor(h2[:, :], tile_of(hall, k), bo[:, :], ALU.add))
                    dve.wait_ge(s_out, k.n + 1)
                    do(nc.vector.tensor_tensor(h2[:, :], psH[:, 0:D], h2[:, :], ALU.add))
                    do(nc.vector.bn_stats(stats[:, :], h2[:, :]))
                    carry(1)
                    do(nc.vector.bn_aggr(meanvar[:, 1, :], stats[:, :]))
                    nc.vector.tensor_scalar(vareps[:, 1:2], meanvar[:, 1, 1:2], EPS, None, ALU.add)\
                      .then_inc(s_ve2, 1)

                def norm2(k):
                    if not k.on(NT):
                        return
                    dve.wait_ge(s_rstd2, k.n + 1)
                    nc.vector.tensor_scalar(hn[:, :], h2[:, :], meanvar[:, 1, 0:1], rstd[:, 1:2],
                                            ALU.subtract, ALU.mult).then_inc(s_hn, 1)
                    dve.wait_ge(s_hn, k.n + 1)
                    nc.vector.scalar_tensor_tensor(out=square[:, :], in0=hn[:, :], scalar=1.0, in1=hn[:, :],
                                                   op0=ALU.mult, op1=ALU.mult, accum_out=ss[:, :])\
                      .then_inc(s_ss, 1)
                    dve.wait_ge(s_ss, k.n + 1)
                    nc.vector.tensor_scalar(mseps[:, :], ss[:, :], 1.0 / D, EPS, ALU.mult, ALU.add)\
                      .then_inc(s_ms, 1)
                    nc.vector.tensor_tensor(tile_of(hall, k), h2[:, :], hn[:, :], ALU.add).then_inc(s_n2, 1)

                def scale_t(k):
                    if not k.on(NT):
                        return
                    dve.wait_ge(s_rr, k.n + 1)
                    nc.vector.scalar_tensor_tensor(out=t[:, 0:D], in0=hn[:, :], scalar=rrms[:, :],
                                                   in1=tscale[:, :], op0=ALU.mult, op1=ALU.mult)\
                      .then_inc(s_tt, 1)
                    nc.vector.scalar_tensor_tensor(out=t[:, D:256], in0=hn[:, 128:D], scalar=rrms[:, :],
                                                   in1=tscale[:, 128:D], op0=ALU.mult, op1=ALU.mult)\
                      .then_inc(s_tt, 1)

                def split_t(k):
                    if not k.on(NT):
                        return
                    dve.wait_ge(s_tT, k.n + 1)
                    cols = bass.ds(k.n * 128, 128)
                    nc.vector.tensor_copy(tAh[:, cols], tT[:, 0, :]).then_inc(s_sp, 1)
                    nc.vector.tensor_copy(tBs[0:64, cols], tT[0:64, 1, :]).then_inc(s_sp, 1)
                    nc.vector.tensor_copy(tBr[64:128, :], tT[64:128, 1, :]).then_inc(s_sp, 1)
                    dve.wait_ge(s_sp, 5 * k.n + 3)
                    nc.vector.tensor_tensor(tAl[:, cols], tT[:, 0, :], tAh[:, cols].bitcast(F32), ALU.subtract)\
                      .then_inc(s_sp, 1)
                    nc.vector.tensor_tensor(tBs[64:128, cols], tT[64:128, 1, :], tBr[64:128, :].bitcast(F32),
                                            ALU.subtract).then_inc(s_sp, 1)

                def route(k):
                    if not k.on(NT):
                        return
                    do = Chain(dve, s_gs, 8, k)
                    dve.wait_ge(s_gm, k.n + 1)
                    do(nc.vector.tensor_tensor(gate[:, :], psH[:, 0:E], gb[:, :], ALU.add))
                    other = gate[:, :].unsqueeze(1).broadcast_to([128, E, E])
                    own = gate[:, :].unsqueeze(2).broadcast_to([128, E, E])
                    nc.vector.tensor_reduce(gmax[:, :], gate[:, :], AX.X, ALU.max, negate=True)\
                      .then_inc(s_gmx, 1)
                    nc.vector.tensor_tensor(above[:, :, :], other, own, ALU.is_gt).then_inc(s_gs, 1)
                    nc.vector.tensor_tensor(notbelow[:, :, :], other, own, ALU.is_ge).then_inc(s_gs, 1)
                    do.m += 2
                    dve.wait_ge(s_gs, 8 * k.n + 3)
                    carry(2)
                    do(nc.vector.copy_predicated(above[:, :, :], lower[:, :, :], notbelow[:, :, :]))
                    do(nc.vector.tensor_reduce(rank[:, :], above[:, :, :], AX.X, ALU.add))
                    dve.wait_ge(s_gex, k.n + 1)
                    do(nc.vector.scalar_tensor_tensor(out=chosen[:, :], in0=rank[:, :], scalar=float(TOPK),
                                                      in1=gexp[:, :], op0=ALU.is_lt, op1=ALU.mult))
                    do(nc.vector.reduce_sum(gsum[:, :], chosen[:, :], AX.X))
                    do(nc.vector.reciprocal(ginv[:, :], gsum[:, :]))

                def split_w(k):
                    if not k.on(NT):
                        return
                    do = Chain(dve, s_w32, 1, k)
                    nc.vector.tensor_scalar(w[:, :], chosen[:, :], ginv[:, :], None, ALU.mult).then_inc(s_gw, 1)
                    nc.vector.tensor_scalar(w32[:, 0:E], chosen[:, :], ginv[:, :], None, ALU.mult)\
                      .then_inc(s_gw, 1)
                    dve.wait_ge(s_gw, 2 * k.n + 2)
                    nc.vector.tensor_tensor(w32[:, E:2 * E], w[:, :], w32[:, 0:E].bitcast(F32), ALU.subtract)\
                      .then_inc(s_w32, 1)

                def copy_wT(k):
                    if not k.on(NT):
                        return
                    dve.wait_ge(s_wTm, k.n + 1)
                    nc.vector.tensor_copy(w32T[:, :], psH[0:2 * E, 0:128]).then_inc(s_wT, 1)
                    dve.wait_ge(s_wT, k.n + 1)
                    nc.vector.tensor_copy(wT[0:2 * E, bass.ds(k.n * 128, 128)], w32T[:, :]).then_inc(s_wTa, 1)

                def add_bias(k):
                    if not k.on(NT):
                        return
                    dve.wait_ge(s_b2m, k.n + 1)
                    nc.vector.tensor_tensor(tile_of(hall, k), tile_of(hall, k), psH[:, 0:D], ALU.add)\
                      .then_inc(s_b2, 1)

                def body(i):
                    norm1_stats(i + 2)
                    row_sum(i + -1)
                    norm1(i + 2)
                    split_t(i + -2)
                    route(i + -2)
                    split_w(i + -2)
                    copy_wT(i + -2)
                    select_heads(i + -1)
                    copy_v(i + 1)
                    add_bias(i + -2)
                    norm2_stats(i + -1)
                    less_max(i)
                    norm2(i + -1)
                    scale_t(i + -1)

                s_gw = sem("l_w_steps")
                s_wTa = sem("l_wT_stored")
                sweep(dve, NT, body, lead=2, lag=2)

            @block.gpsimd
            def _(pool):
                nc.gpsimd.memset(gw[:, 1, :], 0.0).then_inc(s_zero, 1)
                nc.gpsimd.memset(v[:, :, :, :], 0.0).then_inc(s_vz, 1)

                def add_bias(k):
                    if not k.on(NT):
                        return
                    pool.wait_ge(s_rd[k.par], 64 * (k.half + 1))
                    wait(pool, s_p, k.n)
                    nc.gpsimd.tensor_tensor(z[:, :, :, :].rearrange("p j b w -> p b j w"),
                                            sq[:, k.par, :, :, 0:Q], bias[:, k.par, :, :, :], ALU.add)\
                      .then_inc(s_z, 1)

                def pad_q(k):
                    if not k.on(NT):
                        return
                    for g in range(G):
                        pool.wait_ge(s_qb, 2 * k.n + g + 1)
                        src = qb[:, g, :].rearrange("p (b w) -> p b w", b=2)
                        nc.gpsimd.tensor_tensor(
                            qpad[:, g, :, :].rearrange("p b (m w) -> p b m w", w=Q),
                            src.unsqueeze(2).broadcast_to([GC, 2, 2 * PG, Q]),
                            qmask[:, :, :].unsqueeze(1).broadcast_to([GC, 2, 2 * PG, Q]), ALU.mult)\
                          .then_inc(s_qpad, 1)

                def normalise(k):
                    if not k.on(NT):
                        return
                    pool.wait_ge(s_inv, k.n + 1)
                    wait(pool, s_t, 2 * k.n)
                    nc.gpsimd.tensor_tensor(p2[:, :, :, :].rearrange("p j b w -> p (j b) w"),
                                            z[:, :, :, :].rearrange("p j b w -> p (j b) w"),
                                            inv[:, :].unsqueeze(2).broadcast_to([128, 2 * PR, Q]),
                                            ALU.mult).then_inc(s_p, 1)

                def power(k, need, src, dst, done):
                    if not k.on(NT):
                        return
                    pool.wait_ge(need, k.n + 1)
                    nc.gpsimd.tensor_tensor(dst, src, mhalf[:, :], ALU.pow).then_inc(done, 1)

                def body(i):
                    power(i + 2, s_ve, vareps[:, 0:1], rstd[:, 0:1], s_rstd)
                    normalise(i + -1)
                    pad_q(i + 1)
                    add_bias(i)
                    power(i + -1, s_ve2, vareps[:, 1:2], rstd[:, 1:2], s_rstd2)
                    power(i + -1, s_ms, mseps[:, :], rrms[:, :], s_rr)

                pool.wait_ge(s_half, 1)
                sweep(pool, NT, body, lead=2, lag=1)


def experts(nc, hall, tAh, tAl, tBs, wT, out, a):
    STEPS = EP * NC
    with ExitStack() as c:
        sb = lambda n, s, d=F32: c.enter_context(nc.sbuf_tensor(n, s, d))
        ps = lambda n, s: c.enter_context(nc.psum_tensor(n, s, F32))
        sem = lambda n: c.enter_context(nc.semaphore(n))
        stage = sb("e_w1_stage", [128, 2, M1])
        selst = sb("e_sel_stage", [128, 3, 128])
        w1h = sb("e_w1_high", [128, 2, 2, M1], F32R)
        w1l = sb("e_w1_low", [128, 2, 2, M1], F32R)
        sel = sb("e_sel", [128, 2, 3, 128], F32R)
        w2 = sb("e_w2", [128, 2, 3, D])
        b1 = sb("e_b1", [128, EP, 6])
        b1g = sb("e_b1_pair", [128, 2, 6])
        glu = sb("e_glu", [128, 2, CH])
        lin = sb("e_lin", [128, 2, CH])
        sig = sb("e_sig", [128, 2, CH])
        y = sb("e_act", [128, 2, 3, CH])
        psG = [ps(f"e_psG{n}", [128, CH]) for n in range(2)]
        psL = [ps(f"e_psL{n}", [128, CH]) for n in range(2)]
        psW = [ps(f"e_psW{n}", [128, CH]) for n in range(2)]
        psY = [ps(f"e_psY{n}", [128, 2, D]) for n in range(2)]

        s_b1 = sem("e_b1_in")
        s_st = sem("e_stage_in")
        s_w2 = [sem(f"e_w2_in{n}") for n in range(2)]
        s_hi = sem("e_high_done")
        s_lo = sem("e_low_done")
        s_bp = sem("e_b1_pair_done")
        s_g = sem("e_glu_mm")
        s_l = sem("e_lin_mm")
        s_wb = sem("e_weight_mm")
        s_gs = sem("e_glu_done")
        s_ls = sem("e_lin_done")
        s_u = sem("e_product_done")
        s_sg = sem("e_sigmoid_done")
        s_v = sem("e_weighted_done")
        s_a = sem("e_act_done")
        s_y = sem("e_out_mm")
        s_acc = sem("e_out_added")
        s_out = sem("e_written")

        class Ep:

            def __init__(self, p, r=None):
                self.par, self.n = p % 2, p if r is None else 2 * r + p
                self.half = p // 2 if r is None else r + p // 2

        def pairs(e, each):
            for p in range(2):
                each(Ep(p))
            with e.Fori(1, EP // 2 - 1) as r:
                for p in range(2):
                    each(Ep(p, r))
            for p in range(EP - 2, EP):
                each(Ep(p))

        def next_pair(ep, prepare):
            if not (isinstance(ep.n, int) and ep.n == EP - 1):
                prepare(ep.n + 1, 1 - ep.par)

        def chunks(e, ep, step, middle=None):
            step(ep, 0, 0, NC * ep.n)
            step(ep, 1, 1, NC * ep.n + 1)
            if middle:
                middle()
            with e.Fori(1, NC // 2) as r:
                for p in range(2):
                    step(ep, 2 * r + p, p, NC * ep.n + 2 * r + p)

        with nc.Block() as block:

            @block.sync
            def _(sp):
                sp.dma_start(b1[:, :, :], a["b1"]).then_inc(s_b1, 16)

                def load_stage(n):
                    sp.dma_start(stage[:, :, :], a["w1"][:, bass.ds(n * 2 * M1, 2 * M1)]).then_inc(s_st, 16)
                    sp.dma_start(selst[:, :, :], a["sel"][:, bass.ds(n * 3 * 128, 3 * 128)]).then_inc(s_st, 16)

                def load_w2(n, par):
                    sp.dma_start(w2[:, par, :, :], a["w2"][:, bass.ds(n * 3 * D, 3 * D)]).then_inc(s_w2[par], 16)

                load_stage(0)
                load_w2(0, 0)
                for n in range(1, EP):
                    sp.wait_ge(s_hi, 3 * n)
                    sp.wait_ge(s_lo, 2 * n)
                    load_stage(n)
                    if n > 1:
                        sp.wait_ge(s_y, 2 * NC * (n - 1))
                    load_w2(n, n % 2)
                for ch in range(NC):
                    sp.wait_ge(s_acc, 2 * (NC * (EP - 1) + ch + 1))
                    sp.dma_start(out[:, ch * 4:(ch + 1) * 4, :],
                                 hall[:, ch * 4 * D:(ch + 1) * 4 * D].rearrange("p (t n) -> p t n", n=D))\
                      .then_inc(s_out, 16)
                sp.wait_ge(s_out, 16 * NC)

            @block.tensor
            def _(pe):
                def second(s, par, wpar, subs):
                    for sub in subs:
                        if sub == 0:
                            pe.wait_ge(s_a, 3 * s)
                        if sub % 2 == 0:
                            wait(pe, s_acc, 2 * (s - 2) + sub // 2 + 1)
                        for m in range(3):
                            last = nc.tensor.matmul(psY[sub // 2][:, sub % 2, :],
                                                    y[:, par, m, sub * 128:(sub + 1) * 128], w2[:, wpar, m, :],
                                                    start=m == 0, stop=m == 2)
                        if sub % 2:
                            last.then_inc(s_y, 1)

                def each(ep):
                    pe.wait_ge(s_lo, 2 * ep.n + 2)
                    pe.wait_ge(s_hi, 3 * ep.n + 3)

                    def step(ep, ch, par, s):
                        cols = bass.ds(ch * CH, CH)
                        for m in range(3):
                            n = 3 * s + m
                            ring = (par + m) % 2
                            for dst, half, need, done in ((psG, 0, s_gs, s_g), (psL, 1, s_ls, s_l)):
                                wait(pe, need, n - 1)
                                w = slice((2 * m + half) * 128, (2 * m + half + 1) * 128)
                                parts = ((w1h[:, ep.par, 0, w], tAh), (w1h[:, ep.par, 0, w], tAl),
                                         (w1l[:, ep.par, 0, w], tAh), (w1h[:, ep.par, 1, w], tBs),
                                         (w1l[:, ep.par, 1, w], tBs))
                                for q, (lhsT, rhs) in enumerate(parts):
                                    last = nc.tensor.matmul(dst[ring][:, :], lhsT, rhs[:, cols],
                                                            start=q == 0, stop=q == len(parts) - 1)
                                last.then_inc(done, 1)
                            wait(pe, s_v, n - 1)
                            nc.tensor.matmul(psW[ring][:, :], sel[:, ep.par, m, :], wT[:, cols],
                                             start=True, stop=True).then_inc(s_wb, 1)
                            if isinstance(s, int) and s == 0:
                                continue
                            wpar = 1 - ep.par if isinstance(ch, int) and ch == 0 else ep.par
                            if m == 0 and isinstance(ch, int) and ch == 1:
                                pe.wait_ge(s_w2[ep.par], 16 * (ep.half + 1))
                            second(s, 1 - par, wpar, ((0,), (1,), (2, 3))[m])

                    chunks(pe, ep, step)

                pairs(pe, each)
                second(STEPS, 1, 1, range(4))

            @block.scalar
            def _(act):
                def round_weights(n, par):
                    act.wait_ge(s_st, 32 * (n + 1))
                    for m in range(2):
                        nc.scalar.activation(w1h[:, par, m, :], stage[:, m, :], ACT.Copy).then_inc(s_hi, 1)
                    nc.scalar.activation(sel[:, par, :, :], selst[:, :, :], ACT.Copy).then_inc(s_hi, 1)

                def each(ep):
                    def step(ep, ch, par, s):
                        for m in range(3):
                            n, ring = 3 * s + m, (par + m) % 2
                            act.wait_ge(s_gs, n + 1)
                            wait(act, s_a, n - 1)
                            nc.scalar.activation(sig[:, ring, :], glu[:, ring, :], ACT.Sigmoid, scale=ALPHA)\
                               .then_inc(s_sg, 1)

                    chunks(act, ep, step, lambda: next_pair(ep, round_weights))

                round_weights(0, 0)
                pairs(act, each)

            @block.vector
            def _(dve):
                dve.wait_ge(s_b1, 16)

                def each(ep):
                    nc.vector.tensor_copy(b1g[:, ep.par, :], b1[:, bass.ds(ep.n, 1), :]).then_inc(s_bp, 1)
                    dve.wait_ge(s_bp, 2 * ep.n + 1)
                    bl = b1g[:, ep.par, :].rearrange("p (m h) -> p m h", h=2)
                    nc.vector.tensor_scalar(bl[:, :, 1], bl[:, :, 1], 1.0, None, ALU.add).then_inc(s_bp, 1)
                    dve.wait_ge(s_bp, 2 * ep.n + 2)

                    def step(ep, ch, par, s):
                        for m in range(3):
                            n, ring = 3 * s + m, (par + m) % 2
                            dve.wait_ge(s_g, n + 1)
                            nc.vector.tensor_scalar(glu[:, ring, :], psG[ring][:, :], b1g[:, ep.par, 2 * m:2 * m + 1],
                                                    LIMIT, ALU.add, ALU.min).then_inc(s_gs, 1)
                            dve.wait_ge(s_l, n + 1)
                            wait(dve, s_a, n - 1)
                            nc.vector.tensor_scalar(lin[:, ring, :], psL[ring][:, :],
                                                    b1g[:, ep.par, 2 * m + 1:2 * m + 2], 1.0 - LIMIT,
                                                    ALU.add, ALU.max).then_inc(s_ls, 1)
                            dve.wait_ge(s_ls, n + 1)
                            nc.vector.scalar_tensor_tensor(out=lin[:, ring, :], in0=lin[:, ring, :],
                                                           scalar=1.0 + LIMIT, in1=glu[:, ring, :],
                                                           op0=ALU.min, op1=ALU.mult).then_inc(s_u, 1)
                            dve.wait_ge(s_sg, n + 1)
                            dve.wait_ge(s_wb, n + 1)
                            nc.vector.tensor_tensor(sig[:, ring, :], psW[ring][:, :], sig[:, ring, :], ALU.mult)\
                              .then_inc(s_v, 1)
                            if m == 2 and not (isinstance(s, int) and s == 0):
                                prev = ch - 1 if not (isinstance(ch, int) and ch == 0) else NC - 1
                                add(prev, s)

                    chunks(dve, ep, step)

                def add(ch, s):
                    for b in range(2):
                        dve.wait_ge(s_y, 2 * (s - 1) + b + 1)
                        part = hall[:, bass.ds((ch * 4 + 2 * b) * D, 2 * D)]
                        nc.vector.tensor_tensor(part, psY[b][:, :, :].rearrange("p t n -> p (t n)"), part,
                                                ALU.add).then_inc(s_acc, 1)

                pairs(dve, each)
                add(NC - 1, STEPS)

            @block.gpsimd
            def _(pool):
                def rest_of_weights(n, par):
                    pool.wait_ge(s_hi, 3 * n + 2)
                    for m in range(2):
                        nc.gpsimd.tensor_tensor(w1l[:, par, m, :], stage[:, m, :], w1h[:, par, m, :].bitcast(F32),
                                                ALU.subtract).then_inc(s_lo, 1)

                def each(ep):
                    def step(ep, ch, par, s):
                        for m in range(3):
                            n, ring = 3 * s + m, (par + m) % 2
                            pool.wait_ge(s_u, n + 1)
                            pool.wait_ge(s_v, n + 1)
                            nc.gpsimd.tensor_tensor(y[:, par, m, :], lin[:, ring, :], sig[:, ring, :], ALU.mult)\
                              .then_inc(s_a, 1)

                    chunks(pool, ep, step, lambda: next_pair(ep, rest_of_weights))

                rest_of_weights(0, 0)
                pairs(pool, each)


def audio_tower(nc, a, out):
    with ExitStack() as c:
        sb = lambda n, s, d=F32: c.enter_context(nc.sbuf_tensor(n, s, d))
        hall = sb("hall", [128, NT * D])
        tAh = sb("tA_high", [128, T], F32R)
        tAl = sb("tA_low", [128, T], F32R)
        tBs = sb("tB_high_low", [128, T], F32R)
        wT = sb("wT", [128, T], F32R)
        ident = sb("ident", [128, 128])
        hmask = sb("hmask", [GC, 2])
        qmask = sb("qmask", [GC, 2 * PG, Q])
        scratch = nc.dram_tensor("rel_scratch", (2, 2, 128, PR, REL), F32, kind="Internal").ap()
        s_c = c.enter_context(nc.semaphore("constants_in"))
        s_z = c.enter_context(nc.semaphore("wT_zero"))
        with nc.Block() as block:

            @block.sync
            def _(sp):
                for dst, src in ((ident[:, :], a["ident"]), (hmask[:, :], a["hmask"]), (qmask[:, :, :], a["qmask"])):
                    sp.dma_start(dst, src).then_inc(s_c, 16)
                sp.wait_ge(s_c, 48)

            @block.gpsimd
            def _(pool):
                nc.gpsimd.memset(wT[:, :].bitcast(F32), 0.0).then_inc(s_z, 1)
                pool.wait_ge(s_z, 1)

        pool_attention(nc, hall, ident, hmask, qmask, a)
        local_attention(nc, hall, tAh, tAl, tBs, wT, ident, hmask, qmask, scratch, a)
        experts(nc, hall, tAh, tAl, tBs, wT, out, a)


def kernel(**inputs):
    import numpy as np
    import concourse.bacc as bacc
    from concourse.bass_utils import run_bass_kernel_spmd as run

    f = np.float32
    x = {n: np.asarray(v) for n, v in inputs.items()}

    def grouped(w):
        return np.ascontiguousarray(w.reshape(G, GC, -1).transpose(1, 0, 2))

    def rows(b):
        return np.ascontiguousarray(np.broadcast_to(b, (128, b.size)))

    def per_group(*bs):
        return np.ascontiguousarray(np.concatenate([b.reshape(G, GC).T for b in bs], axis=1))

    bqkv = x["L0_tok_b_qkv"]
    head = np.arange(GC) // DK
    hmask = np.stack([head % 2 == 0, head % 2 == 1], axis=1).astype(f)
    qmask = np.zeros((GC, 2 * PG, Q), f)
    qmask[np.arange(GC), head, :] = SCALE
    lower = (np.arange(E)[None, :] < np.arange(E)[:, None]).astype(np.int32)
    rel = np.clip(Q - 1 - np.arange(REL), -MAXREL, MAXREL) + MAXREL
    relT = np.tile(x["L0_attn_rel_emb"][rel].T, (GC // DK, 1))
    w1, b1 = x["L0_ffn_w1"].reshape(EP, 2, D, 2 * I), x["L0_ffn_b1"].reshape(EP, 2, 1, 2 * I)

    def tiles(w):
        parts = []
        for e in range(2):
            parts += [w[:, e, :, 0:128], w[:, e, :, I:I + 128]]
        for o in (0, I):
            parts += [w[:, 0, :, o + 128:o + I], w[:, 1, :, o + 128:o + I]]
        return np.concatenate(parts, axis=2)

    w1t = tiles(w1)
    w1k = np.stack([w1t[:, 0:128], np.concatenate([w1t[:, 128:D], w1t[:, 128:D]], axis=1)], axis=2)
    b1t = tiles(b1).reshape(EP, 6, 128)
    w2 = x["L0_ffn_w2"].reshape(EP, 2, I, D)
    w2k = np.stack([w2[:, 0, 0:128], w2[:, 1, 0:128], np.concatenate([w2[:, 0, 128:I], w2[:, 1, 128:I]], axis=1)],
                   axis=2)
    sel = np.zeros((128, EP, 3, 128), f)
    for p in range(EP):
        for half in (0, E):
            sel[half + 2 * p, p, 0, :] = 1.0
            sel[half + 2 * p + 1, p, 1, :] = 1.0
            sel[half + 2 * p, p, 2, 0:64] = 1.0
            sel[half + 2 * p + 1, p, 2, 64:128] = 1.0
    arrays = {
        "xT": np.ascontiguousarray(x["x"].reshape(B * N, D).T),
        "wqkvT": np.ascontiguousarray(x["L0_tok_w_qkv"].T), "wprojT": grouped(x["L0_tok_w_proj"].T),
        "bqk": per_group(bqkv[0:D], bqkv[D:2 * D]), "bv": rows(bqkv[2 * D:]), "bproj": rows(x["L0_tok_b_proj"]),
        "ident": np.eye(128, dtype=f), "hmask": hmask, "qmask": qmask,
        "awqkv": grouped(np.concatenate([x["L0_attn_Wq"], x["L0_attn_Wk"], x["L0_attn_Wv"]], axis=1)),
        "awo": grouped(x["L0_attn_Wo"]), "abqk": per_group(x["L0_attn_bq"], x["L0_attn_bk"]),
        "abv": rows(x["L0_attn_bv"]), "abo": rows(x["L0_attn_bo"]), "tscale": rows(x["L0_ffn_scale"]),
        "gwT": np.ascontiguousarray(x["L0_ffn_gate_w"].T), "gb": rows(x["L0_ffn_gate_b"]),
        "lower": np.ascontiguousarray(np.broadcast_to(lower, (128, E, E))),
        "b2dup": np.concatenate([x["L0_ffn_b2"], x["L0_ffn_b2"]]), "relT": np.ascontiguousarray(relT),
        "w1": np.ascontiguousarray(w1k.transpose(1, 0, 2, 3).reshape(128, -1)),
        "b1": np.ascontiguousarray(b1t.transpose(2, 0, 1)),
        "w2": np.ascontiguousarray(w2k.transpose(1, 0, 2, 3).reshape(128, -1)),
        "sel": sel.reshape(128, -1),
    }
    nc = bacc.Bacc("TRN2", target_bir_lowering=False, num_devices=1)
    feeds, aps = {}, {}
    for name, array in arrays.items():
        feeds["in_" + name] = array
        aps[name] = nc.dram_tensor("in_" + name, array.shape, mybir.dt.from_np(array.dtype), kind="ExternalInput").ap()
    out = nc.dram_tensor("out", (B, Q, D), F32, kind="ExternalOutput").ap()
    audio_tower(nc, aps, out.rearrange("b q n -> (b q) n").rearrange("(t p) n -> p t n", p=128))
    r = run(nc, [feeds], core_ids=[0])
    return r.results[0]["out"]
```

```python
import concourse.bass as bass
from concourse import mybir
from contextlib import ExitStack

F32 = mybir.dt.float32
F32R = mybir.dt.float32r
I32 = mybir.dt.int32
ALU = mybir.AluOpType
ACT = mybir.ActivationFunctionType
AX = mybir.AxisListType

B, N, D = 64, 256, 192
H, DK = 12, 16
Q = 64
STRIDE = N // Q
G, GC = 2, D // 2
PR = H // 2
PG = PR // G
PC = 2 * DK
MAXREL = 32
T = B * Q
NT = T // 128
TOK = 2 * N
REL = 128
E, TOPK, I = 16, 4, 192
EP = E // 2
M1 = 6 * 128
CH = 512
NC = T // CH
ALPHA, LIMIT, EPS = 1.702, 7.0, 1e-5
SCALE = DK ** -0.5


class At:

    def __init__(self, c, r=None):
        self.c, self.r, self.par = c, r, c % 2

    def __add__(self, d):
        return At(self.c + d, self.r)

    @property
    def n(self):
        return self.c if self.r is None else 2 * self.r + self.c

    @property
    def half(self):
        return self.c // 2 if self.r is None else self.r + self.c // 2

    def on(self, n):
        return self.r is not None or 0 <= self.c < n


def wait(e, sem, value):
    if not isinstance(value, int) or value > 0:
        e.wait_ge(sem, value)


def sweep(e, n, body, lead=1, lag=1):
    rounds = (n - 3 - lead) // 2
    for c in range(-lead, 3):
        body(At(c))
    with e.Fori(0, rounds) as r:
        for p in range(2):
            body(At(3 + p, r))
    for c in range(3 + 2 * rounds, n + lag):
        body(At(c))


class Chain:

    def __init__(self, e, sem, per, k, done=0):
        self.e, self.sem, self.base, self.m = e, sem, per * k.n, done

    def __call__(self, ins):
        self.m += 1
        ins.then_inc(self.sem, 1)
        self.e.wait_ge(self.sem, self.base + self.m)


def tile_of(hall, k):
    return hall[:, bass.ds(k.n * D, D)]


class LocalWeights:

    def __init__(self, nc, c, a):
        sb = lambda n, s, d=F32: c.enter_context(nc.sbuf_tensor(n, s, d))
        self.wqkv = sb("l_wqkv", [GC, G, 3 * D])
        self.wo = sb("l_wo", [GC, G, D])
        self.bqk = sb("l_bqk", [GC, 2 * G])
        self.bv = sb("l_bv", [128, D])
        self.bo = sb("l_bo", [128, D])
        self.tscale = sb("l_tscale", [128, D])
        self.gw = sb("l_gw", [128, 2, E])
        self.gb = sb("l_gb", [128, E])
        self.lower = sb("l_lower", [128, E, E], I32)
        self.b2 = sb("l_b2", [2 * E, D])
        self.kr = sb("l_k_rel", [GC, G, 2, Q + REL])
        self.loaded = c.enter_context(nc.semaphore("l_weights"))
        self.zeros = c.enter_context(nc.semaphore("l_gate_zeros"))
        self.loads = (
            (self.wqkv[:, :, :], a["awqkv"]), (self.wo[:, :, :], a["awo"]), (self.bqk[:, :], a["abqk"]),
            (self.bv[:, :], a["abv"]), (self.bo[:, :], a["abo"]), (self.tscale[:, :], a["tscale"]),
            (self.gw[:, 0, :], a["gwT"][0:128, :]), (self.gw[0:D - 128, 1, :], a["gwT"][128:D, :]),
            (self.gb[:, :], a["gb"]), (self.lower[:, :, :], a["lower"]), (self.b2[:, :], a["b2dup"]),
            (self.kr[:, 0, 0, Q:], a["relT"]), (self.kr[:, 0, 1, Q:], a["relT"]),
            (self.kr[:, 1, 0, Q:], a["relT"]), (self.kr[:, 1, 1, Q:], a["relT"]))
        self.count = 16 * len(self.loads)


class ExpertWeights:

    def __init__(self, nc, c, a):
        sb = lambda n, s, d=F32: c.enter_context(nc.sbuf_tensor(n, s, d))
        sem = lambda n: c.enter_context(nc.semaphore(n))
        self.nc, self.a = nc, a
        self.stage = sb("e_w1_stage", [128, 2, M1])
        self.selst = sb("e_sel_stage", [128, 3, 128])
        self.w1h = sb("e_w1_high", [128, 2, 2, M1], F32R)
        self.w1l = sb("e_w1_low", [128, 2, 2, M1], F32R)
        self.sel = sb("e_sel", [128, 2, 3, 128], F32R)
        self.w2 = sb("e_w2", [128, 2, 3, D])
        self.b1 = sb("e_b1", [128, EP, 6])
        self.b1_in = sem("e_b1_in")
        self.staged = sem("e_stage_in")
        self.w2_in = [sem(f"e_w2_in{n}") for n in range(2)]
        self.high = sem("e_high_done")
        self.low = sem("e_low_done")

    def load_stage(self, sp, n):
        sp.dma_start(self.stage[:, :, :], self.a["w1"][:, bass.ds(n * 2 * M1, 2 * M1)]).then_inc(self.staged, 16)
        sp.dma_start(self.selst[:, :, :], self.a["sel"][:, bass.ds(n * 3 * 128, 3 * 128)])\
          .then_inc(self.staged, 16)

    def load_w2(self, sp, n, par):
        sp.dma_start(self.w2[:, par, :, :], self.a["w2"][:, bass.ds(n * 3 * D, 3 * D)])\
          .then_inc(self.w2_in[par], 16)

    def round(self, act, n, par):
        act.wait_ge(self.staged, 32 * (n + 1))
        for m in range(2):
            self.nc.scalar.activation(self.w1h[:, par, m, :], self.stage[:, m, :], ACT.Copy).then_inc(self.high, 1)
        self.nc.scalar.activation(self.sel[:, par, :, :], self.selst[:, :, :], ACT.Copy).then_inc(self.high, 1)

    def rest(self, pool, n, par):
        pool.wait_ge(self.high, 3 * n + 2)
        for m in range(2):
            self.nc.gpsimd.tensor_tensor(self.w1l[:, par, m, :], self.stage[:, m, :],
                                         self.w1h[:, par, m, :].bitcast(F32), ALU.subtract).then_inc(self.low, 1)


def pool_attention(nc, hall, wT, ident, hmask, qmask, lw, a):
    with ExitStack() as c:
        sb = lambda n, s, d=F32: c.enter_context(nc.sbuf_tensor(n, s, d))
        ps = lambda n, s: c.enter_context(nc.psum_tensor(n, s, F32))
        sem = lambda n: c.enter_context(nc.semaphore(n))
        x = sb("p_x", [128, 2, 2, TOK])
        xah = sb("p_xA_high", [128, 2, TOK], F32R)
        xal = sb("p_xA_low", [128, 2, TOK], F32R)
        xbs = sb("p_xB_high_low", [128, 2, TOK], F32R)
        wqk = sb("p_wqk", [128, 2, 2 * D])
        wqkh = sb("p_wqk_high", [128, 2, 2 * D], F32R)
        wqkl = sb("p_wqk_low", [128, 2, 2 * D], F32R)
        wv = sb("p_wv", [128, 2, D])
        wproj = sb("p_wproj", [GC, G, D])
        bqk = sb("p_bqk", [GC, 2 * G])
        bv = sb("p_bv", [128, D])
        bproj = sb("p_bproj", [128, D])
        qmax = sb("p_qmax", [GC, G, 2, Q])
        qpad = sb("p_qpad", [GC, 2, G, 2, PG * 2 * Q])
        kT = sb("p_kT", [GC, 2, G, TOK])
        v = sb("p_v", [128, 2, 4, D])
        p = sb("p_p", [128, 2, PR, N])
        pT = sb("p_pT", [128, 2, PR * 2, 128])
        negmax = sb("p_negmax", [128, 2, PR])
        total = sb("p_total", [128, 2, PR])
        inv = sb("p_inv", [128, 2, PR])
        idle = sb("p_idle", [128, 2])
        osel = sb("p_osel", [GC, G * 2, Q])
        oT = sb("p_oT", [GC, G, 2 * Q])
        ringA = [ps(f"p_psA{n}", [128, 512]) for n in range(2)]
        scores = [ps(f"p_psS{n}", [128, 2, N]) for n in range(3)]
        ringT = [ps(f"p_psT{n}", [128, 4, 128]) for n in range(2)]
        psO = ps("p_psO", [128, 512])

        s_wqk = sem("p_wqk_in")
        s_w = sem("p_weights")
        s_zero = sem("p_wv_zeros")
        s_wh = sem("p_wqk_high_done")
        s_wl = sem("p_wqk_low_done")
        s_xh = sem("p_x_high_done")
        s_xal = sem("p_xA_low_done")
        s_xbl = sem("p_xB_low_done")
        s_x = [sem(f"p_x_in{n}") for n in range(2)]
        s_qk = sem("p_qk_mm")
        s_v = sem("p_v_mm")
        s_qmax = sem("p_qmax_done")
        s_qpad = sem("p_qpad_done")
        s_kT = sem("p_kT_done")
        s_vsb = sem("p_v_done")
        s_s = sem("p_scores_mm")
        s_mx = sem("p_max_done")
        s_exp = sem("p_exp_done")
        s_inv = sem("p_inv_done")
        s_p = sem("p_probs_done")
        s_t = sem("p_transposed")
        s_ta = sem("p_pT_by_act")
        s_tv = sem("p_pT_by_dve")
        s_pv = sem("p_pv_mm")
        s_osel = sem("p_osel_half")
        s_oT = sem("p_oT_done")
        s_out = sem("p_out_mm")
        s_h = sem("p_h_done")
        s_wz = sem("p_wT_zeros")

        loads_qk = ((wqk[:, 0, :], a["wqkvT"][0:128, 0:2 * D]), (wqk[0:64, 1, :], a["wqkvT"][128:D, 0:2 * D]),
                    (wqk[64:128, 1, :], a["wqkvT"][128:D, 0:2 * D]))
        loads = ((bqk[:, :], a["bqk"]), (qmask[:, :, :], a["qmask"]), (wv[:, 0, :], a["wqkvT"][0:128, 2 * D:]),
                 (wv[0:64, 1, :], a["wqkvT"][128:D, 2 * D:]), (bv[:, :], a["bv"]), (ident[:, :], a["ident"]),
                 (hmask[:, :], a["hmask"]), (wproj[:, :, :], a["wprojT"]), (bproj[:, :], a["bproj"]))
        W_ALL = 16 * len(loads)

        with nc.Block() as block:

            @block.sync
            def _(sp):
                for dst, src in loads_qk:
                    sp.dma_start(dst, src).then_inc(s_wqk, 16)

                def load(k):
                    if not k.on(NT):
                        return
                    wait(sp, s_v, 2 * (k.n - 1))
                    wait(sp, s_xal, k.n - 1)
                    wait(sp, s_xbl, k.n - 1)
                    cols = bass.ds(k.n * TOK, TOK)
                    for dst, src in ((x[:, k.par, 0, :], a["xT"][0:128, cols]),
                                     (x[0:64, k.par, 1, :], a["xT"][128:D, cols]),
                                     (x[64:128, k.par, 1, :], a["xT"][128:D, cols])):
                        sp.dma_start(dst, src).then_inc(s_x[k.par], 16)

                load(At(0))
                sp.wait_ge(s_zero, 1)
                for dst, src in loads:
                    sp.dma_start(dst, src).then_inc(s_w, 16)
                sweep(sp, NT, lambda k: load(k + 1), lead=0, lag=0)
                sp.wait_ge(lw.zeros, 1)
                for dst, src in lw.loads:
                    sp.dma_start(dst, src).then_inc(lw.loaded, 16)

            @block.tensor
            def _(pe):
                pe.wait_ge(s_wl, 1)

                def project_qk(k):
                    if not k.on(NT):
                        return
                    pe.wait_ge(s_xh, 2 * k.n + 2)
                    pe.wait_ge(s_xal, k.n + 1)
                    pe.wait_ge(s_xbl, k.n + 1)
                    for n in range(4):
                        which, g = n // G, n % G
                        if n < 2:
                            wait(pe, s_vsb, 2 * (k.n - 1) + n + 1)
                        else:
                            pe.wait_ge(s_qmax, 2 * k.n + g + 1)
                        w = slice(which * D + g * GC, which * D + (g + 1) * GC)
                        parts = ((wqkh[:, 0, w], xah), (wqkh[:, 0, w], xal), (wqkl[:, 0, w], xah),
                                 (wqkh[:, 1, w], xbs), (wqkl[:, 1, w], xbs))
                        for q, (lhsT, rhs) in enumerate(parts):
                            last = nc.tensor.matmul(ringA[n % 2][0:GC, :], lhsT, rhs[:, k.par, :],
                                                    start=q == 0, stop=q == len(parts) - 1)
                        last.then_inc(s_qk, 1)

                def project_v(k):
                    if not k.on(NT):
                        return
                    if k.c == 0:
                        pe.wait_ge(s_w, W_ALL)
                    for t in range(4):
                        if t % 2 == 0:
                            pe.wait_ge(s_kT, 2 * k.n + t // 2 + 1)
                        for h in range(2):
                            last = nc.tensor.matmul(
                                ringA[t // 2][:, (t % 2) * D:(t % 2 + 1) * D],
                                x[:, k.par, h, t * 128:(t + 1) * 128], wv[:, h, :],
                                start=h == 0, stop=h == 1)
                        if t % 2:
                            last.then_inc(s_v, 1)

                def score(k, b):
                    if not k.on(NT):
                        return
                    if b == 0:
                        pe.wait_ge(s_qpad, 4 * k.n + 4)
                        pe.wait_ge(s_kT, 2 * k.n + 2)
                    for j in range(PR):
                        if j % 2 == 0:
                            wait(pe, s_exp, 12 * k.n + 6 * (b - 1) + j + 2)
                        g, i = j // PG, j % PG
                        last = nc.tensor.matmul(
                            scores[j // 2][:, j % 2, :], qpad[:, k.par, g, b, i * 128:(i + 1) * 128],
                            kT[:, k.par, g, b * N:(b + 1) * N], start=True, stop=True)
                        if j % 2:
                            last.then_inc(s_s, 1)

                def weigh(k, b):
                    if not k.on(NT):
                        return
                    for u in range(3):
                        n = 3 * b + u
                        s, per, before = ((s_tv, 2, 0), (s_ta, 4, 0), (s_ta, 4, 1),
                                          (s_tv, 2, 1), (s_ta, 4, 2), (s_ta, 4, 3))[n]
                        wait(pe, s, per * k.n + before)
                        pe.wait_ge(s_p, 6 * k.n + n + 1)
                        for m in range(4):
                            last = nc.tensor.transpose(
                                ringT[n % 2][:, m, :],
                                p[:, b, 2 * u + m // 2, (m % 2) * 128:(m % 2 + 1) * 128], ident[:, :])
                        last.then_inc(s_t, 1)
                    if b == 0:
                        wait(pe, s_h, k.n)
                    for j in range(PR):
                        if j % 2 == 0:
                            u, n = j // 2, 3 * b + j // 2
                            if u == 1:
                                pe.wait_ge(s_tv, 2 * k.n + b + 1)
                            else:
                                pe.wait_ge(s_ta, 4 * k.n + 2 * b + u // 2 + 1)
                        if j == 0:
                            pe.wait_ge(s_vsb, 2 * k.n + 2)
                        g, i = j // PG, j % PG
                        for kt in range(2):
                            last = nc.tensor.matmul(
                                psO[i * PC:(i + 1) * PC, (2 * g + b) * 128:(2 * g + b + 1) * 128],
                                v[:, k.par, 2 * b + kt, j * PC:(j + 1) * PC], pT[:, b, 2 * j + kt, :],
                                start=kt == 0, stop=kt == 1)
                    last.then_inc(s_pv, 1)

                def project_out(k):
                    if not k.on(NT):
                        return
                    pe.wait_ge(s_oT, k.n + 1)
                    for g in range(G):
                        last = nc.tensor.matmul(psO[:, 0:D], oT[:, g, :], wproj[:, g, :],
                                                start=g == 0, stop=g == G - 1)
                    last.then_inc(s_out, 1)

                def body(i):
                    score(i, 0)
                    project_qk(i + 1)
                    weigh(i + -1, 1)
                    score(i, 1)
                    project_out(i + -1)
                    project_v(i + 1)
                    weigh(i, 0)

                sweep(pe, NT, body)

            @block.scalar
            def _(act):
                act.wait_ge(s_wqk, 16 * len(loads_qk))
                nc.scalar.activation(wqkh[:, :, :], wqk[:, :, :], ACT.Copy).then_inc(s_wh, 1)

                def round_x(k):
                    if not k.on(NT):
                        return
                    act.wait_ge(s_x[k.par], 48 * (k.half + 1))
                    nc.scalar.activation(xah[:, k.par, :], x[:, k.par, 0, :], ACT.Copy).then_inc(s_xh, 1)
                    nc.scalar.activation(xbs[:, k.par, :], x[:, k.par, 1, :], ACT.Copy).then_inc(s_xh, 1)

                def exps(k, b):
                    if not k.on(NT):
                        return
                    for j in range(PR):
                        if j % 2 == 0:
                            act.wait_ge(s_mx, 6 * k.n + 3 * b + j // 2 + 1)
                        nc.scalar.activation(p[:, b, j, :], scores[j // 2][:, j % 2, :], ACT.Exp,
                                             bias=negmax[:, b, j:j + 1], scale=1.0,
                                             accum_out=total[:, b, j:j + 1]).then_inc(s_exp, 1)

                def copy_k(k):
                    if not k.on(NT):
                        return
                    if k.c == 0:
                        act.wait_ge(s_w, W_ALL)
                    for g in range(G):
                        act.wait_ge(s_qk, 4 * k.n + 2 + g + 1)
                        nc.scalar.activation(kT[:, k.par, g, :], ringA[g][0:GC, :], ACT.Identity,
                                             bias=bqk[:, G + g:G + g + 1]).then_inc(s_kT, 1)

                def copy_pT(k, b):
                    if not k.on(NT):
                        return
                    for u in (0, 2):
                        n = 3 * b + u
                        act.wait_ge(s_t, 6 * k.n + n + 1)
                        nc.scalar.activation(pT[:, b, 4 * u:4 * u + 4, :], ringT[n % 2][:, :, :],
                                             ACT.Copy).then_inc(s_ta, 1)

                def body(i):
                    exps(i, 0)
                    copy_k(i + 1)
                    copy_pT(i + -1, 1)
                    round_x(i + 2)
                    exps(i, 1)
                    copy_pT(i, 0)

                sweep(act, NT, body, lead=2)

            @block.vector
            def _(dve):

                def rest_of_x(k):
                    if not k.on(NT):
                        return
                    dve.wait_ge(s_xh, 2 * k.n + 2)
                    low = xbs[64:128, k.par, :]
                    nc.vector.tensor_tensor(low, x[64:128, k.par, 1, :], low.bitcast(F32), ALU.subtract)\
                      .then_inc(s_xbl, 1)

                def pool_q(k):
                    if not k.on(NT):
                        return
                    if k.c == 0:
                        dve.wait_ge(s_w, W_ALL)
                    for g in range(G):
                        dve.wait_ge(s_qk, 4 * k.n + g + 1)
                        nc.vector.tensor_reduce(
                            qmax[:, g, :, :],
                            ringA[g][0:GC, :].rearrange("p (b s w) -> p b w s", b=2, s=STRIDE),
                            AX.X, ALU.max).then_inc(s_qmax, 1)
                    for g in range(G):
                        dve.wait_ge(s_qmax, 2 * k.n + g + 1)
                        for b in range(2):
                            nc.vector.scalar_tensor_tensor(
                                out=qpad[:, k.par, g, b, :].rearrange("p (m w) -> p m w", w=Q),
                                in0=qmax[:, g, b, :].unsqueeze(1).broadcast_to([GC, 2 * PG, Q]),
                                scalar=bqk[:, g:g + 1], in1=qmask[:, :, :],
                                op0=ALU.add, op1=ALU.mult).then_inc(s_qpad, 1)

                def row_max(k, b):
                    if not k.on(NT):
                        return
                    for u in range(3):
                        dve.wait_ge(s_s, 6 * k.n + 3 * b + u + 1)
                        nc.vector.tensor_reduce(negmax[:, b, 2 * u:2 * u + 2], scores[u][:, :, :], AX.X,
                                                ALU.max, negate=True).then_inc(s_mx, 1)

                def invert(k, b):
                    if not k.on(NT):
                        return
                    dve.wait_ge(s_exp, 12 * k.n + 6 * b + 6)
                    nc.vector.reciprocal(inv[:, b, :], total[:, b, :]).then_inc(s_inv, 1)

                def copy_pT(k, b):
                    if not k.on(NT):
                        return
                    n = 3 * b + 1
                    dve.wait_ge(s_t, 6 * k.n + n + 1)
                    nc.vector.tensor_copy(pT[:, b, 4:8, :], ringT[n % 2][:, :, :]).then_inc(s_tv, 1)

                def select_heads(k):
                    if not k.on(NT):
                        return
                    dve.wait_ge(s_pv, 2 * k.n + 2)
                    o = psO[0:GC, :].rearrange("p (m h w) -> p m h w", h=2, w=Q)
                    nc.vector.tensor_scalar(osel[:, :, :], o[:, :, 0, :], hmask[:, 0:1], None, ALU.mult)\
                      .then_inc(s_osel, 1)
                    dve.wait_ge(s_osel, k.n + 1)
                    nc.vector.scalar_tensor_tensor(
                        out=oT[:, :, :].rearrange("p g (b w) -> p (g b) w", w=Q), in0=o[:, :, 1, :],
                        scalar=hmask[:, 1:2], in1=osel[:, :, :], op0=ALU.mult, op1=ALU.add).then_inc(s_oT, 1)

                def copy_out(k):
                    if not k.on(NT):
                        return
                    dve.wait_ge(s_out, k.n + 1)
                    nc.vector.tensor_tensor(tile_of(hall, k), psO[:, 0:D], bproj[:, :], ALU.add)\
                      .then_inc(s_h, 1)

                def copy_v(k):
                    if not k.on(NT):
                        return
                    for t in range(2):
                        dve.wait_ge(s_v, 2 * k.n + t + 1)
                        nc.vector.tensor_tensor(
                            v[:, k.par, 2 * t:2 * t + 2, :],
                            ringA[t][:, 0:2 * D].rearrange("p (m n) -> p m n", n=D),
                            bv[:, :].unsqueeze(1).broadcast_to([128, 2, D]), ALU.add).then_inc(s_vsb, 1)

                def body(i):
                    row_max(i, 0)
                    pool_q(i + 1)
                    invert(i, 0)
                    copy_pT(i + -1, 1)
                    select_heads(i + -1)
                    row_max(i, 1)
                    rest_of_x(i + 2)
                    copy_out(i + -1)
                    copy_v(i + 1)
                    invert(i, 1)
                    copy_pT(i, 0)

                sweep(dve, NT, body, lead=2)

            @block.gpsimd
            def _(pool):
                nc.gpsimd.memset(wv[:, 1, :], 0.0).then_inc(s_zero, 1)
                nc.gpsimd.memset(lw.gw[:, 1, :], 0.0).then_inc(lw.zeros, 1)
                pool.wait_ge(s_wh, 1)
                nc.gpsimd.tensor_tensor(wqkl[:, :, :], wqk[:, :, :], wqkh[:, :, :].bitcast(F32), ALU.subtract)\
                  .then_inc(s_wl, 1)

                def rest_of_x(k):
                    if not k.on(NT):
                        return
                    pool.wait_ge(s_xh, 2 * k.n + 2)
                    nc.gpsimd.tensor_tensor(xal[:, k.par, :], x[:, k.par, 0, :], xah[:, k.par, :].bitcast(F32),
                                            ALU.subtract).then_inc(s_xal, 1)

                def normalise(k):
                    if not k.on(NT):
                        return
                    for b in range(2):
                        pool.wait_ge(s_inv, 2 * k.n + b + 1)
                        nc.gpsimd.tensor_tensor(idle[:, b:b + 1], inv[:, b, 0:1], inv[:, b, 0:1], ALU.mult)
                        for j in range(PR):
                            last = nc.gpsimd.tensor_scalar(p[:, b, j, :], p[:, b, j, :], inv[:, b, j:j + 1],
                                                           1.0, ALU.mult, ALU.mult)
                            if j % 2:
                                last.then_inc(s_p, 1)

                def body(i):
                    normalise(i)
                    rest_of_x(i + 2)

                sweep(pool, NT, body, lead=2, lag=0)
                nc.gpsimd.memset(wT[:, :].bitcast(F32), 0.0).then_inc(s_wz, 1)
                pool.wait_ge(s_wz, 1)


def local_attention(nc, hall, tAh, tAl, tBs, wT, ident, hmask, qmask, scratch, lw, ew):
    with ExitStack() as c:
        sb = lambda n, s, d=F32: c.enter_context(nc.sbuf_tensor(n, s, d))
        ps = lambda n, s: c.enter_context(nc.psum_tensor(n, s, F32))
        sem = lambda n: c.enter_context(nc.semaphore(n))
        wqkv, wo, bqk, bv, bo, tscale = lw.wqkv, lw.wo, lw.bqk, lw.bv, lw.bo, lw.tscale
        gw, gb, lower, b2, kr = lw.gw, lw.gb, lw.lower, lw.b2, lw.kr
        mhalf = sb("l_minus_half", [128, 1])
        idle = sb("l_idle", [128, 3])
        stats = sb("l_stats", [128, 6])
        meanvar = sb("l_meanvar", [128, 2, 2])
        vareps = sb("l_vareps", [128, 2])
        rstd = sb("l_rstd", [128, 2])
        xn = sb("l_xn", [128, D])
        xnT = sb("l_xnT", [GC, G, 128])
        qpad = sb("l_qpad", [GC, G, 2, PG * 2 * Q])
        qb = sb("l_q", [GC, G, 2 * Q])
        v = sb("l_v", [128, 2, 2, D])
        sq = sb("l_sq", [128, 2, 2, PR, Q + REL])
        bias = sb("l_bias", [128, 2, 2, PR, Q])
        z = sb("l_z", [128, PR, 2, Q])
        p2 = sb("l_p", [128, PR, 2, Q])
        rowmax = sb("l_rowmax", [128, PR * 2])
        total = sb("l_total", [128, PR * 2])
        inv = sb("l_inv", [128, PR * 2])
        pT = sb("l_pT", [128, PR, 128])
        osel = sb("l_osel", [GC, G * 2, Q])
        oT = sb("l_oT", [GC, G, 2 * Q])
        h2 = sb("l_h2", [128, D])
        hn = sb("l_hn", [128, D])
        square = sb("l_square", [128, D])
        ss = sb("l_ss", [128, 1])
        mseps = sb("l_mseps", [128, 1])
        rrms = sb("l_rrms", [128, 1])
        t = sb("l_t", [128, 256])
        tT = sb("l_tT", [128, 2, 128])
        tBr = sb("l_tB_round", [128, 128], F32R)
        gate = sb("l_gate", [128, E])
        above = sb("l_above", [128, E, E])
        notbelow = sb("l_notbelow", [128, E, E])
        rank = sb("l_rank", [128, E])
        gmax = sb("l_gmax", [128, 1])
        gexp = sb("l_gexp", [128, E])
        chosen = sb("l_chosen", [128, E])
        gsum = sb("l_gsum", [128, 1])
        ginv = sb("l_ginv", [128, 1])
        w = sb("l_w", [128, E])
        w32 = sb("l_w32", [128, 2 * E], F32R)
        w32T = sb("l_w32T", [2 * E, 128])
        ringA = [ps(f"l_psA{n}", [128, 512]) for n in range(2)]
        ringS = [ps(f"l_psS{n}", [128, 2, Q + REL]) for n in range(3)]
        psT = ps("l_psT", [128, 4, 128])
        psO = ps("l_psO", [128, G * 2, 128])
        psH = ps("l_psH", [128, 512])

        s_vz = sem("l_v_zeros")
        s_half = sem("l_minus_half_done")
        s_ln = sem("l_ln_steps")
        s_ve = sem("l_vareps_done")
        s_rstd = sem("l_rstd_done")
        s_xn = sem("l_xn_done")
        s_xT = sem("l_xn_transposed")
        s_xnT = sem("l_xnT_done")
        s_q = sem("l_q_mm")
        s_qb = sem("l_q_done")
        s_qpad = sem("l_qpad_done")
        s_k = sem("l_k_mm")
        s_kr = sem("l_k_done")
        s_v = sem("l_v_mm")
        s_vsb = sem("l_v_done")
        s_s = sem("l_scores_mm")
        s_sq = sem("l_sq_done")
        s_wr = [sem(f"l_rel_written{n}") for n in range(2)]
        s_rd = [sem(f"l_rel_read{n}") for n in range(2)]
        s_z = sem("l_z_done")
        s_sm = sem("l_softmax_steps")
        s_sub = sem("l_z_less_max")
        s_exp = sem("l_exp_done")
        s_inv = sem("l_inv_done")
        s_p = sem("l_probs_done")
        s_t = sem("l_p_transposed")
        s_pTa = sem("l_pT_first_done")
        s_pTb = sem("l_pT_rest_done")
        s_pv = sem("l_pv_mm")
        s_os = sem("l_osel_steps")
        s_oT = sem("l_oT_done")
        s_out = sem("l_out_mm")
        s_h2 = sem("l_h2_done")
        s_n2 = sem("l_norm2_steps")
        s_ve2 = sem("l_vareps2_done")
        s_rstd2 = sem("l_rstd2_done")
        s_hn = sem("l_hn_done")
        s_ss = sem("l_ss_done")
        s_ms = sem("l_mseps_done")
        s_rr = sem("l_rrms_done")
        s_tt = sem("l_t_done")
        s_tTm = sem("l_t_transposed")
        s_tT = sem("l_tT_done")
        s_sp = sem("l_split_done")
        s_gm = sem("l_gate_mm")
        s_g = sem("l_gate_copied")
        s_gs = sem("l_gate_steps")
        s_gmx = sem("l_gmax_done")
        s_gex = sem("l_gexp_done")
        s_w32 = sem("l_w32_done")
        s_wTm = sem("l_w32_transposed")
        s_wT = sem("l_w32T_done")
        s_b2m = sem("l_b2_mm")
        s_b2 = sem("l_b2_added")


        with nc.Block() as block:

            @block.sync
            def _(sp):
                def skew(k):
                    par = k.par
                    sp.wait_ge(s_sq, 6 * k.n + 3)
                    sp.dma_start(scratch[par, 0, :, :, :], sq[:, par, 0, :, Q:]).then_inc(s_wr[par], 16)
                    sp.wait_ge(s_sq, 6 * k.n + 6)
                    sp.dma_start(scratch[par, 1, :, :, :], sq[:, par, 1, :, Q:]).then_inc(s_wr[par], 16)
                    sp.wait_ge(s_wr[par], 32 * (k.half + 1))
                    row = PR * REL
                    for b in range(2):
                        for h in range(2):
                            src = bass.AP(scratch.tensor, ((par * 2 + b) * 128 + h * Q) * row + Q - 1,
                                          [[row - 1, Q], [REL, PR], [1, Q]])
                            sp.dma_start(bias[h * Q:(h + 1) * Q, par, b, :, :], src).then_inc(s_rd[par], 16)

                sweep(sp, NT, skew, lead=0, lag=0)
                sp.dma_start(ew.b1[:, :, :], ew.a["b1"]).then_inc(ew.b1_in, 16)
                ew.load_stage(sp, 0)
                ew.load_w2(sp, 0, 0)

            @block.tensor
            def _(pe):
                pe.wait_ge(lw.loaded, lw.count)

                def transpose_xn(k):
                    if not k.on(NT):
                        return
                    pe.wait_ge(s_xn, k.n + 1)
                    wait(pe, s_kr, 2 * k.n)
                    for g in range(G):
                        last = nc.tensor.transpose(ringA[0][0:GC, g * 128:(g + 1) * 128],
                                                   xn[:, g * GC:(g + 1) * GC], ident[:, :])
                    last.then_inc(s_xT, 1)

                def project_kq(k):
                    if not k.on(NT):
                        return
                    pe.wait_ge(s_xnT, k.n + 1)
                    for which, bank, done in ((0, 1, s_q), (1, 0, s_k)):
                        if which == 0:
                            wait(pe, s_vsb, 2 * k.n)
                        for g in range(G):
                            for h in range(G):
                                last = nc.tensor.matmul(
                                    ringA[bank][0:GC, g * 128:(g + 1) * 128],
                                    wqkv[:, h, which * D + g * GC:which * D + (g + 1) * GC], xnT[:, h, :],
                                    start=h == 0, stop=h == G - 1)
                        last.then_inc(done, 1)

                def project_v(k):
                    if not k.on(NT):
                        return
                    pe.wait_ge(s_qb, 2 * k.n + 2)
                    for h in range(G):
                        last = nc.tensor.matmul(ringA[1][:, 0:D], xnT[:, h, :], wqkv[:, h, 2 * D:3 * D],
                                                start=h == 0, stop=h == G - 1)
                    last.then_inc(s_v, 1)

                def score(k, half):
                    if not k.on(NT):
                        return
                    if half == 0:
                        pe.wait_ge(s_qpad, 2 * k.n + 2)
                        pe.wait_ge(s_kr, 2 * k.n + 2)
                    for u in range(3 * half, 3 * half + 3):
                        b = u // 3
                        wait(pe, s_sq, 6 * k.n + u - 2)
                        for m in range(2):
                            j = 2 * (u % 3) + m
                            g, i = j // PG, j % PG
                            last = nc.tensor.matmul(ringS[u % 3][:, m, :], qpad[:, g, b, i * 128:(i + 1) * 128],
                                                    kr[:, g, b, :], start=True, stop=True)
                        last.then_inc(s_s, 1)

                def transpose_p(k):
                    if not k.on(NT):
                        return
                    pe.wait_ge(s_p, k.n + 1)
                    for r, js in ((0, range(0, 4)), (1, range(4, 6))):
                        wait(pe, (s_pTb, s_pTa)[r], k.n + r)
                        for j in js:
                            last = nc.tensor.transpose(psT[:, j % 4, :],
                                                       p2[:, j, :, :].rearrange("p b w -> p (b w)"), ident[:, :])
                        last.then_inc(s_t, 1)

                def weigh(k):
                    if not k.on(NT):
                        return
                    wait(pe, s_oT, k.n)
                    pe.wait_ge(s_pTa, k.n + 1)
                    for j in range(PR):
                        if j == 4:
                            pe.wait_ge(s_pTb, k.n + 1)
                        g, i = j // PG, j % PG
                        for b in range(2):
                            last = nc.tensor.matmul(psO[i * PC:(i + 1) * PC, 2 * g + b, :],
                                                    v[:, k.par, b, j * PC:(j + 1) * PC], pT[:, j, :],
                                                    start=True, stop=True)
                    last.then_inc(s_pv, 1)

                def project_out(k):
                    if not k.on(NT):
                        return
                    wait(pe, s_b2, k.n)
                    pe.wait_ge(s_oT, k.n + 1)
                    for g in range(G):
                        last = nc.tensor.matmul(psH[:, 0:D], oT[:, g, :], wo[:, g, :],
                                                start=g == 0, stop=g == G - 1)
                    last.then_inc(s_out, 1)

                def transpose_t(k):
                    if not k.on(NT):
                        return
                    pe.wait_ge(s_tt, 2 * k.n + 2)
                    for m in range(2):
                        last = nc.tensor.transpose(psH[:, m * 128:(m + 1) * 128], t[:, m * 128:(m + 1) * 128],
                                                   ident[:, :])
                    last.then_inc(s_tTm, 1)

                def gates(k):
                    if not k.on(NT):
                        return
                    pe.wait_ge(s_tT, k.n + 1)
                    for m in range(2):
                        last = nc.tensor.matmul(psH[:, 0:E], tT[:, m, :], gw[:, m, :], start=m == 0, stop=m == 1)
                    last.then_inc(s_gm, 1)

                def transpose_w(k):
                    if not k.on(NT):
                        return
                    pe.wait_ge(s_w32, k.n + 1)
                    nc.tensor.transpose(psH[0:2 * E, 0:128], w32[:, :].bitcast(F32), ident[:, :])\
                      .then_inc(s_wTm, 1)

                def expert_bias(k):
                    if not k.on(NT):
                        return
                    pe.wait_ge(s_wT, k.n + 1)
                    nc.tensor.matmul(psH[:, 0:D], w32T[:, :], b2[:, :], start=True, stop=True).then_inc(s_b2m, 1)

                def body(i):
                    transpose_xn(i + 1)
                    score(i, 0)
                    score(i, 1)
                    transpose_t(i + -2)
                    project_kq(i + 1)
                    gates(i + -2)
                    transpose_p(i + -1)
                    weigh(i + -1)
                    transpose_w(i + -2)
                    project_v(i + 1)
                    expert_bias(i + -2)
                    project_out(i + -1)

                sweep(pe, NT, body, lead=2, lag=3)

            @block.scalar
            def _(act):
                act.wait_ge(lw.loaded, lw.count)

                def copy_xnT(k):
                    if not k.on(NT):
                        return
                    act.wait_ge(s_xT, k.n + 1)
                    nc.scalar.activation(xnT[:, :, :], ringA[0][0:GC, 0:G * 128], ACT.Copy).then_inc(s_xnT, 1)

                def copy_k(k):
                    if not k.on(NT):
                        return
                    act.wait_ge(s_k, k.n + 1)
                    for g in range(G):
                        nc.scalar.activation(
                            kr[:, g, :, 0:Q],
                            ringA[0][0:GC, g * 128:(g + 1) * 128].rearrange("p (b w) -> p b w", b=2),
                            ACT.Identity, bias=bqk[:, G + g:G + g + 1]).then_inc(s_kr, 1)

                def copy_q(k):
                    if not k.on(NT):
                        return
                    act.wait_ge(s_q, k.n + 1)
                    for g in range(G):
                        nc.scalar.activation(qb[:, g, :], ringA[1][0:GC, g * 128:(g + 1) * 128], ACT.Identity,
                                             bias=bqk[:, g:g + 1]).then_inc(s_qb, 1)

                def copy_scores(k, half):
                    if not k.on(NT):
                        return
                    if half == 0:
                        wait(act, s_wr[k.par], 32 * k.half)
                    for u in range(3 * half, 3 * half + 3):
                        act.wait_ge(s_s, 6 * k.n + u + 1)
                        j = 2 * (u % 3)
                        nc.scalar.activation(sq[:, k.par, u // 3, j:j + 2, :], ringS[u % 3][:, :, :], ACT.Copy)\
                          .then_inc(s_sq, 1)

                def exps(k):
                    if not k.on(NT):
                        return
                    act.wait_ge(s_sub, k.n + 1)
                    nc.scalar.activation(z[:, :, :, :], z[:, :, :, :], ACT.Exp).then_inc(s_exp, 1)

                def copy_pT(k):
                    if not k.on(NT):
                        return
                    for r, (lo, hi) in enumerate(((0, 4), (4, 6))):
                        act.wait_ge(s_t, 2 * k.n + r + 1)
                        nc.scalar.activation(pT[:, lo:hi, :], psT[:, 0:hi - lo, :], ACT.Copy)\
                          .then_inc((s_pTa, s_pTb)[r], 1)

                def copy_tT(k):
                    if not k.on(NT):
                        return
                    act.wait_ge(s_tTm, k.n + 1)
                    nc.scalar.activation(tT[:, :, :], psH[:, 0:256], ACT.Copy).then_inc(s_tT, 1)

                def gate_exp(k):
                    if not k.on(NT):
                        return
                    act.wait_ge(s_gmx, k.n + 1)
                    nc.scalar.activation(gexp[:, :], gate[:, :], ACT.Exp, bias=gmax[:, 0:1]).then_inc(s_gex, 1)

                def body(i):
                    copy_scores(i, 0)
                    exps(i + -1)
                    copy_scores(i, 1)
                    copy_tT(i + -2)
                    copy_q(i + 1)
                    gate_exp(i + -2)
                    copy_pT(i + -1)
                    copy_k(i + 1)
                    copy_xnT(i + 2)

                sweep(act, NT, body, lead=2, lag=3)
                ew.round(act, 0, 0)

            @block.vector
            def _(dve):
                nc.vector.memset(mhalf[:, :], -0.5).then_inc(s_half, 1)
                dve.wait_ge(lw.loaded, lw.count)
                dve.wait_ge(s_vz, 1)

                def carry(n):
                    nc.vector.memset(idle[:, n:n + 1], 0.0)

                def norm1_stats(k):
                    if not k.on(NT):
                        return
                    do = Chain(dve, s_ln, 2, k)
                    do(nc.vector.bn_stats(stats[:, :], tile_of(hall, k)))
                    carry(0)
                    do(nc.vector.bn_aggr(meanvar[:, 0, :], stats[:, :]))
                    nc.vector.tensor_scalar(vareps[:, 0:1], meanvar[:, 0, 1:2], EPS, None, ALU.add)\
                      .then_inc(s_ve, 1)

                def norm1(k):
                    if not k.on(NT):
                        return
                    dve.wait_ge(s_rstd, k.n + 1)
                    wait(dve, s_xT, k.n)
                    nc.vector.tensor_scalar(xn[:, :], tile_of(hall, k), meanvar[:, 0, 0:1], rstd[:, 0:1],
                                            ALU.subtract, ALU.mult).then_inc(s_xn, 1)

                def copy_v(k):
                    if not k.on(NT):
                        return
                    dve.wait_ge(s_v, k.n + 1)
                    for b in range(2):
                        rows = slice(b * Q, (b + 1) * Q)
                        nc.vector.tensor_tensor(v[rows, k.par, b, :], ringA[1][rows, 0:D], bv[rows, :], ALU.add)\
                          .then_inc(s_vsb, 1)

                zr = z[:, :, :, :].rearrange("p j b w -> p (j b) w")

                def less_max(k):
                    if not k.on(NT):
                        return
                    dve.wait_ge(s_z, k.n + 1)
                    do = Chain(dve, s_sm, 2, k)
                    do(nc.vector.tensor_reduce(rowmax[:, :], zr, AX.X, ALU.max))
                    nc.vector.tensor_tensor(zr, zr, rowmax[:, :].unsqueeze(2).broadcast_to([128, 2 * PR, Q]),
                                            ALU.subtract).then_inc(s_sub, 1)

                def row_sum(k):
                    if not k.on(NT):
                        return
                    dve.wait_ge(s_exp, k.n + 1)
                    nc.vector.tensor_reduce(total[:, :], zr, AX.X, ALU.add).then_inc(s_sm, 1)
                    dve.wait_ge(s_sm, 2 * k.n + 2)
                    nc.vector.reciprocal(inv[:, :], total[:, :]).then_inc(s_inv, 1)

                def select_heads(k):
                    if not k.on(NT):
                        return
                    dve.wait_ge(s_pv, k.n + 1)
                    o = psO[0:GC, :, :].rearrange("p m (h w) -> p m h w", w=Q)
                    nc.vector.tensor_scalar(osel[:, :, :], o[:, :, 0, :], hmask[:, 0:1], None, ALU.mult)\
                      .then_inc(s_os, 1)
                    dve.wait_ge(s_os, k.n + 1)
                    nc.vector.scalar_tensor_tensor(
                        out=oT[:, :, :].rearrange("p g (b w) -> p (g b) w", w=Q), in0=o[:, :, 1, :],
                        scalar=hmask[:, 1:2], in1=osel[:, :, :], op0=ALU.mult, op1=ALU.add).then_inc(s_oT, 1)

                def bias_h(k):
                    if not k.on(NT):
                        return
                    nc.vector.tensor_tensor(h2[:, :], tile_of(hall, k), bo[:, :], ALU.add).then_inc(s_n2, 1)

                def norm2_stats(k):
                    if not k.on(NT):
                        return
                    do = Chain(dve, s_n2, 5, k, 1)
                    dve.wait_ge(s_n2, 5 * k.n + 1)
                    dve.wait_ge(s_out, k.n + 1)
                    do(nc.vector.tensor_tensor(h2[:, :], psH[:, 0:D], h2[:, :], ALU.add))
                    do(nc.vector.bn_stats(stats[:, :], h2[:, :]))
                    carry(1)
                    do(nc.vector.bn_aggr(meanvar[:, 1, :], stats[:, :]))
                    nc.vector.tensor_scalar(vareps[:, 1:2], meanvar[:, 1, 1:2], EPS, None, ALU.add)\
                      .then_inc(s_ve2, 1)

                def norm2(k):
                    if not k.on(NT):
                        return
                    dve.wait_ge(s_rstd2, k.n + 1)
                    nc.vector.tensor_scalar(hn[:, :], h2[:, :], meanvar[:, 1, 0:1], rstd[:, 1:2],
                                            ALU.subtract, ALU.mult).then_inc(s_hn, 1)
                    dve.wait_ge(s_hn, k.n + 1)
                    nc.vector.scalar_tensor_tensor(out=square[:, :], in0=hn[:, :], scalar=1.0, in1=hn[:, :],
                                                   op0=ALU.mult, op1=ALU.mult, accum_out=ss[:, :])\
                      .then_inc(s_ss, 1)
                    dve.wait_ge(s_ss, k.n + 1)
                    nc.vector.tensor_scalar(mseps[:, :], ss[:, :], 1.0 / D, EPS, ALU.mult, ALU.add)\
                      .then_inc(s_ms, 1)
                    nc.vector.tensor_tensor(tile_of(hall, k), h2[:, :], hn[:, :], ALU.add).then_inc(s_n2, 1)

                def scale_t(k):
                    if not k.on(NT):
                        return
                    dve.wait_ge(s_rr, k.n + 1)
                    nc.vector.scalar_tensor_tensor(out=t[:, 0:D], in0=hn[:, :], scalar=rrms[:, :],
                                                   in1=tscale[:, :], op0=ALU.mult, op1=ALU.mult)\
                      .then_inc(s_tt, 1)
                    nc.vector.scalar_tensor_tensor(out=t[:, D:256], in0=hn[:, 128:D], scalar=rrms[:, :],
                                                   in1=tscale[:, 128:D], op0=ALU.mult, op1=ALU.mult)\
                      .then_inc(s_tt, 1)

                def split_t(k):
                    if not k.on(NT):
                        return
                    dve.wait_ge(s_tT, k.n + 1)
                    cols = bass.ds(k.n * 128, 128)
                    nc.vector.tensor_copy(tAh[:, cols], tT[:, 0, :]).then_inc(s_sp, 1)
                    nc.vector.tensor_copy(tBs[0:64, cols], tT[0:64, 1, :]).then_inc(s_sp, 1)
                    nc.vector.tensor_copy(tBr[64:128, :], tT[64:128, 1, :]).then_inc(s_sp, 1)
                    dve.wait_ge(s_sp, 5 * k.n + 3)
                    nc.vector.tensor_tensor(tAl[:, cols], tT[:, 0, :], tAh[:, cols].bitcast(F32), ALU.subtract)\
                      .then_inc(s_sp, 1)
                    nc.vector.tensor_tensor(tBs[64:128, cols], tT[64:128, 1, :], tBr[64:128, :].bitcast(F32),
                                            ALU.subtract).then_inc(s_sp, 1)

                def compare(k):
                    if not k.on(NT):
                        return
                    do = Chain(dve, s_gs, 8, k)
                    dve.wait_ge(s_gm, k.n + 1)
                    do(nc.vector.tensor_tensor(gate[:, :], psH[:, 0:E], gb[:, :], ALU.add))
                    other = gate[:, :].unsqueeze(1).broadcast_to([128, E, E])
                    own = gate[:, :].unsqueeze(2).broadcast_to([128, E, E])
                    nc.vector.tensor_reduce(gmax[:, :], gate[:, :], AX.X, ALU.max, negate=True)\
                      .then_inc(s_gmx, 1)
                    nc.vector.tensor_tensor(above[:, :, :], other, own, ALU.is_gt).then_inc(s_gs, 1)
                    nc.vector.tensor_tensor(notbelow[:, :, :], other, own, ALU.is_ge).then_inc(s_gs, 1)

                def rank_gates(k):
                    if not k.on(NT):
                        return
                    do = Chain(dve, s_gs, 8, k, 3)
                    dve.wait_ge(s_gs, 8 * k.n + 3)
                    carry(2)
                    do(nc.vector.copy_predicated(above[:, :, :], lower[:, :, :], notbelow[:, :, :]))
                    do(nc.vector.tensor_reduce(rank[:, :], above[:, :, :], AX.X, ALU.add))

                def choose(k):
                    if not k.on(NT):
                        return
                    do = Chain(dve, s_gs, 8, k, 5)
                    dve.wait_ge(s_gex, k.n + 1)
                    do(nc.vector.scalar_tensor_tensor(out=chosen[:, :], in0=rank[:, :], scalar=float(TOPK),
                                                      in1=gexp[:, :], op0=ALU.is_lt, op1=ALU.mult))
                    do(nc.vector.reduce_sum(gsum[:, :], chosen[:, :], AX.X))
                    do(nc.vector.reciprocal(ginv[:, :], gsum[:, :]))

                def split_w(k):
                    if not k.on(NT):
                        return
                    do = Chain(dve, s_w32, 1, k)
                    nc.vector.tensor_scalar(w[:, :], chosen[:, :], ginv[:, :], None, ALU.mult).then_inc(s_gw, 1)
                    nc.vector.tensor_scalar(w32[:, 0:E], chosen[:, :], ginv[:, :], None, ALU.mult)\
                      .then_inc(s_gw, 1)
                    dve.wait_ge(s_gw, 2 * k.n + 2)
                    nc.vector.tensor_tensor(w32[:, E:2 * E], w[:, :], w32[:, 0:E].bitcast(F32), ALU.subtract)\
                      .then_inc(s_w32, 1)

                def copy_wT(k):
                    if not k.on(NT):
                        return
                    dve.wait_ge(s_wTm, k.n + 1)
                    nc.vector.tensor_copy(w32T[:, :], psH[0:2 * E, 0:128]).then_inc(s_wT, 1)
                    dve.wait_ge(s_wT, k.n + 1)
                    nc.vector.tensor_copy(wT[0:2 * E, bass.ds(k.n * 128, 128)], w32T[:, :]).then_inc(s_wTa, 1)

                def add_bias(k):
                    if not k.on(NT):
                        return
                    dve.wait_ge(s_b2m, k.n + 1)
                    nc.vector.tensor_tensor(tile_of(hall, k), tile_of(hall, k), psH[:, 0:D], ALU.add)\
                      .then_inc(s_b2, 1)

                def body(i):
                    norm1_stats(i + 2)
                    row_sum(i + -1)
                    split_t(i + -2)
                    compare(i + -2)
                    norm1(i + 2)
                    rank_gates(i + -2)
                    choose(i + -2)
                    split_w(i + -2)
                    select_heads(i + -1)
                    copy_wT(i + -2)
                    copy_v(i + 1)
                    add_bias(i + -2)
                    bias_h(i + -1)
                    norm2_stats(i + -1)
                    less_max(i)
                    norm2(i + -1)
                    scale_t(i + -1)

                s_gw = sem("l_w_steps")
                s_wTa = sem("l_wT_stored")
                sweep(dve, NT, body, lead=2, lag=3)

            @block.gpsimd
            def _(pool):
                nc.gpsimd.memset(v[:, :, :, :], 0.0).then_inc(s_vz, 1)

                def add_bias(k):
                    if not k.on(NT):
                        return
                    pool.wait_ge(s_rd[k.par], 64 * (k.half + 1))
                    wait(pool, s_p, k.n)
                    nc.gpsimd.tensor_tensor(z[:, :, :, :].rearrange("p j b w -> p b j w"),
                                            sq[:, k.par, :, :, 0:Q], bias[:, k.par, :, :, :], ALU.add)\
                      .then_inc(s_z, 1)

                def pad_q(k, g):
                    if not k.on(NT):
                        return
                    pool.wait_ge(s_qb, 2 * k.n + g + 1)
                    src = qb[:, g, :].rearrange("p (b w) -> p b w", b=2)
                    nc.gpsimd.tensor_tensor(
                        qpad[:, g, :, :].rearrange("p b (m w) -> p b m w", w=Q),
                        src.unsqueeze(2).broadcast_to([GC, 2, 2 * PG, Q]),
                        qmask[:, :, :].unsqueeze(1).broadcast_to([GC, 2, 2 * PG, Q]), ALU.mult)\
                      .then_inc(s_qpad, 1)

                def normalise(k):
                    if not k.on(NT):
                        return
                    pool.wait_ge(s_inv, k.n + 1)
                    wait(pool, s_t, 2 * k.n)
                    nc.gpsimd.tensor_tensor(p2[:, :, :, :].rearrange("p j b w -> p (j b) w"),
                                            z[:, :, :, :].rearrange("p j b w -> p (j b) w"),
                                            inv[:, :].unsqueeze(2).broadcast_to([128, 2 * PR, Q]),
                                            ALU.mult).then_inc(s_p, 1)

                def power(k, n):
                    need, src, dst, done = ((s_ve, vareps[:, 0:1], rstd[:, 0:1], s_rstd),
                                            (s_ve2, vareps[:, 1:2], rstd[:, 1:2], s_rstd2),
                                            (s_ms, mseps[:, :], rrms[:, :], s_rr))[n]
                    if not k.on(NT):
                        return
                    pool.wait_ge(need, k.n + 1)
                    nc.gpsimd.tensor_tensor(dst, src, mhalf[:, :], ALU.pow).then_inc(done, 1)

                def body(i):
                    power(i + 2, 0)
                    normalise(i + -1)
                    pad_q(i + 1, 0)
                    pad_q(i + 1, 1)
                    add_bias(i)
                    power(i + -1, 1)
                    power(i + -1, 2)

                pool.wait_ge(s_half, 1)
                sweep(pool, NT, body, lead=2, lag=3)
                ew.rest(pool, 0, 0)


def experts(nc, hall, tAh, tAl, tBs, wT, out, ew):
    STEPS = EP * NC
    with ExitStack() as c:
        sb = lambda n, s, d=F32: c.enter_context(nc.sbuf_tensor(n, s, d))
        ps = lambda n, s: c.enter_context(nc.psum_tensor(n, s, F32))
        sem = lambda n: c.enter_context(nc.semaphore(n))
        w1h, w1l, sel, w2, b1 = ew.w1h, ew.w1l, ew.sel, ew.w2, ew.b1
        s_w2, s_hi, s_lo = ew.w2_in, ew.high, ew.low
        b1g = sb("e_b1_pair", [128, 2, 6])
        glu = sb("e_glu", [128, 2, CH])
        lin = sb("e_lin", [128, 2, CH])
        sig = sb("e_sig", [128, 2, CH])
        y = sb("e_act", [128, 2, 3, CH])
        psG = [ps(f"e_psG{n}", [128, CH]) for n in range(2)]
        psL = [ps(f"e_psL{n}", [128, CH]) for n in range(2)]
        psW = [ps(f"e_psW{n}", [128, CH]) for n in range(2)]
        psY = [ps(f"e_psY{n}", [128, 2, D]) for n in range(2)]

        s_bp = sem("e_b1_pair_done")
        s_g = sem("e_glu_mm")
        s_l = sem("e_lin_mm")
        s_wb = sem("e_weight_mm")
        s_gs = sem("e_glu_done")
        s_ls = sem("e_lin_done")
        s_u = sem("e_product_done")
        s_sg = sem("e_sigmoid_done")
        s_v = sem("e_weighted_done")
        s_a = sem("e_act_done")
        s_y = sem("e_out_mm")
        s_acc = sem("e_out_added")
        s_out = sem("e_written")

        class Ep:

            def __init__(self, p, r=None):
                self.par, self.n = p % 2, p if r is None else 2 * r + p
                self.half = p // 2 if r is None else r + p // 2

        def pairs(e, each):
            for p in range(2):
                each(Ep(p))
            with e.Fori(1, EP // 2 - 1) as r:
                for p in range(2):
                    each(Ep(p, r))
            for p in range(EP - 2, EP):
                each(Ep(p))

        def next_pair(ep, e, prepare):
            if not (isinstance(ep.n, int) and ep.n == EP - 1):
                prepare(e, ep.n + 1, 1 - ep.par)

        def chunks(e, ep, step, middle=None):
            step(ep, 0, 0, NC * ep.n)
            step(ep, 1, 1, NC * ep.n + 1)
            if middle:
                middle()
            with e.Fori(1, NC // 2) as r:
                for p in range(2):
                    step(ep, 2 * r + p, p, NC * ep.n + 2 * r + p)

        with nc.Block() as block:

            @block.sync
            def _(sp):
                for n in range(1, EP):
                    sp.wait_ge(s_hi, 3 * n)
                    sp.wait_ge(s_lo, 2 * n)
                    ew.load_stage(sp, n)
                    if n > 1:
                        sp.wait_ge(s_y, 2 * NC * (n - 1))
                    ew.load_w2(sp, n, n % 2)
                for ch in range(NC):
                    sp.wait_ge(s_acc, 2 * (NC * (EP - 1) + ch + 1))
                    sp.dma_start(out[:, ch * 4:(ch + 1) * 4, :],
                                 hall[:, ch * 4 * D:(ch + 1) * 4 * D].rearrange("p (t n) -> p t n", n=D))\
                      .then_inc(s_out, 16)
                sp.wait_ge(s_out, 16 * NC)

            @block.tensor
            def _(pe):
                def second(s, par, wpar, subs):
                    for sub in subs:
                        if sub == 0:
                            pe.wait_ge(s_a, 3 * s)
                        if sub % 2 == 0:
                            wait(pe, s_acc, 2 * (s - 2) + sub // 2 + 1)
                        for m in range(3):
                            last = nc.tensor.matmul(psY[sub // 2][:, sub % 2, :],
                                                    y[:, par, m, sub * 128:(sub + 1) * 128], w2[:, wpar, m, :],
                                                    start=m == 0, stop=m == 2)
                        if sub % 2:
                            last.then_inc(s_y, 1)

                def each(ep):
                    pe.wait_ge(s_lo, 2 * ep.n + 2)
                    pe.wait_ge(s_hi, 3 * ep.n + 3)

                    def step(ep, ch, par, s):
                        cols = bass.ds(ch * CH, CH)
                        for m in range(3):
                            n = 3 * s + m
                            ring = (par + m) % 2
                            for dst, half, need, done in ((psG, 0, s_gs, s_g), (psL, 1, s_ls, s_l)):
                                wait(pe, need, n - 1)
                                w = slice((2 * m + half) * 128, (2 * m + half + 1) * 128)
                                parts = ((w1h[:, ep.par, 0, w], tAh), (w1h[:, ep.par, 0, w], tAl),
                                         (w1l[:, ep.par, 0, w], tAh), (w1h[:, ep.par, 1, w], tBs),
                                         (w1l[:, ep.par, 1, w], tBs))
                                for q, (lhsT, rhs) in enumerate(parts):
                                    last = nc.tensor.matmul(dst[ring][:, :], lhsT, rhs[:, cols],
                                                            start=q == 0, stop=q == len(parts) - 1)
                                last.then_inc(done, 1)
                            wait(pe, s_v, n - 1)
                            nc.tensor.matmul(psW[ring][:, :], sel[:, ep.par, m, :], wT[:, cols],
                                             start=True, stop=True).then_inc(s_wb, 1)
                            if isinstance(s, int) and s == 0:
                                continue
                            wpar = 1 - ep.par if isinstance(ch, int) and ch == 0 else ep.par
                            if m == 0 and isinstance(ch, int) and ch == 1:
                                pe.wait_ge(s_w2[ep.par], 16 * (ep.half + 1))
                            second(s, 1 - par, wpar, ((0,), (1,), (2, 3))[m])

                    chunks(pe, ep, step)

                pairs(pe, each)
                second(STEPS, 1, 1, range(4))

            @block.scalar
            def _(act):
                def each(ep):
                    def step(ep, ch, par, s):
                        for m in range(3):
                            n, ring = 3 * s + m, (par + m) % 2
                            act.wait_ge(s_gs, n + 1)
                            wait(act, s_a, n - 1)
                            nc.scalar.activation(sig[:, ring, :], glu[:, ring, :], ACT.Sigmoid, scale=ALPHA)\
                               .then_inc(s_sg, 1)

                    chunks(act, ep, step, lambda: next_pair(ep, act, ew.round))

                pairs(act, each)

            @block.vector
            def _(dve):
                dve.wait_ge(ew.b1_in, 16)

                def each(ep):
                    nc.vector.tensor_copy(b1g[:, ep.par, :], b1[:, bass.ds(ep.n, 1), :]).then_inc(s_bp, 1)
                    dve.wait_ge(s_bp, 2 * ep.n + 1)
                    bl = b1g[:, ep.par, :].rearrange("p (m h) -> p m h", h=2)
                    nc.vector.tensor_scalar(bl[:, :, 1], bl[:, :, 1], 1.0, None, ALU.add).then_inc(s_bp, 1)
                    dve.wait_ge(s_bp, 2 * ep.n + 2)

                    def step(ep, ch, par, s):
                        for m in range(3):
                            n, ring = 3 * s + m, (par + m) % 2
                            dve.wait_ge(s_g, n + 1)
                            nc.vector.tensor_scalar(glu[:, ring, :], psG[ring][:, :], b1g[:, ep.par, 2 * m:2 * m + 1],
                                                    LIMIT, ALU.add, ALU.min).then_inc(s_gs, 1)
                            dve.wait_ge(s_l, n + 1)
                            wait(dve, s_a, n - 1)
                            nc.vector.tensor_scalar(lin[:, ring, :], psL[ring][:, :],
                                                    b1g[:, ep.par, 2 * m + 1:2 * m + 2], 1.0 - LIMIT,
                                                    ALU.add, ALU.max).then_inc(s_ls, 1)
                            dve.wait_ge(s_ls, n + 1)
                            nc.vector.scalar_tensor_tensor(out=lin[:, ring, :], in0=lin[:, ring, :],
                                                           scalar=1.0 + LIMIT, in1=glu[:, ring, :],
                                                           op0=ALU.min, op1=ALU.mult).then_inc(s_u, 1)
                            dve.wait_ge(s_sg, n + 1)
                            dve.wait_ge(s_wb, n + 1)
                            nc.vector.tensor_tensor(sig[:, ring, :], psW[ring][:, :], sig[:, ring, :], ALU.mult)\
                              .then_inc(s_v, 1)
                            if m == 2 and not (isinstance(s, int) and s == 0):
                                prev = ch - 1 if not (isinstance(ch, int) and ch == 0) else NC - 1
                                add(prev, s)

                    chunks(dve, ep, step)

                def add(ch, s):
                    for b in range(2):
                        dve.wait_ge(s_y, 2 * (s - 1) + b + 1)
                        part = hall[:, bass.ds((ch * 4 + 2 * b) * D, 2 * D)]
                        nc.vector.tensor_tensor(part, psY[b][:, :, :].rearrange("p t n -> p (t n)"), part,
                                                ALU.add).then_inc(s_acc, 1)

                pairs(dve, each)
                add(NC - 1, STEPS)

            @block.gpsimd
            def _(pool):
                def each(ep):
                    def step(ep, ch, par, s):
                        for m in range(3):
                            n, ring = 3 * s + m, (par + m) % 2
                            pool.wait_ge(s_u, n + 1)
                            pool.wait_ge(s_v, n + 1)
                            nc.gpsimd.tensor_tensor(y[:, par, m, :], lin[:, ring, :], sig[:, ring, :], ALU.mult)\
                              .then_inc(s_a, 1)

                    chunks(pool, ep, step, lambda: next_pair(ep, pool, ew.rest))

                pairs(pool, each)


def audio_tower(nc, a, out):
    with ExitStack() as c:
        sb = lambda n, s, d=F32: c.enter_context(nc.sbuf_tensor(n, s, d))
        hall = sb("hall", [128, NT * D])
        tAh = sb("tA_high", [128, T], F32R)
        tAl = sb("tA_low", [128, T], F32R)
        tBs = sb("tB_high_low", [128, T], F32R)
        wT = sb("wT", [128, T], F32R)
        ident = sb("ident", [128, 128])
        hmask = sb("hmask", [GC, 2])
        qmask = sb("qmask", [GC, 2 * PG, Q])
        scratch = nc.dram_tensor("rel_scratch", (2, 2, 128, PR, REL), F32, kind="Internal").ap()
        lw = LocalWeights(nc, c, a)
        pool_attention(nc, hall, wT, ident, hmask, qmask, lw, a)
        ew = ExpertWeights(nc, c, a)
        local_attention(nc, hall, tAh, tAl, tBs, wT, ident, hmask, qmask, scratch, lw, ew)
        experts(nc, hall, tAh, tAl, tBs, wT, out, ew)


def kernel(**inputs):
    import numpy as np
    import concourse.bacc as bacc
    from concourse.bass_utils import run_bass_kernel_spmd as run

    f = np.float32
    x = {n: np.asarray(v) for n, v in inputs.items()}

    def grouped(w):
        return np.ascontiguousarray(w.reshape(G, GC, -1).transpose(1, 0, 2))

    def rows(b):
        return np.ascontiguousarray(np.broadcast_to(b, (128, b.size)))

    def per_group(*bs):
        return np.ascontiguousarray(np.concatenate([b.reshape(G, GC).T for b in bs], axis=1))

    bqkv = x["L0_tok_b_qkv"]
    head = np.arange(GC) // DK
    hmask = np.stack([head % 2 == 0, head % 2 == 1], axis=1).astype(f)
    qmask = np.zeros((GC, 2 * PG, Q), f)
    qmask[np.arange(GC), head, :] = SCALE
    lower = (np.arange(E)[None, :] < np.arange(E)[:, None]).astype(np.int32)
    rel = np.clip(Q - 1 - np.arange(REL), -MAXREL, MAXREL) + MAXREL
    relT = np.tile(x["L0_attn_rel_emb"][rel].T, (GC // DK, 1))
    w1, b1 = x["L0_ffn_w1"].reshape(EP, 2, D, 2 * I), x["L0_ffn_b1"].reshape(EP, 2, 1, 2 * I)

    def tiles(w):
        parts = []
        for e in range(2):
            parts += [w[:, e, :, 0:128], w[:, e, :, I:I + 128]]
        for o in (0, I):
            parts += [w[:, 0, :, o + 128:o + I], w[:, 1, :, o + 128:o + I]]
        return np.concatenate(parts, axis=2)

    w1t = tiles(w1)
    w1k = np.stack([w1t[:, 0:128], np.concatenate([w1t[:, 128:D], w1t[:, 128:D]], axis=1)], axis=2)
    b1t = tiles(b1).reshape(EP, 6, 128)
    w2 = x["L0_ffn_w2"].reshape(EP, 2, I, D)
    w2k = np.stack([w2[:, 0, 0:128], w2[:, 1, 0:128], np.concatenate([w2[:, 0, 128:I], w2[:, 1, 128:I]], axis=1)],
                   axis=2)
    sel = np.zeros((128, EP, 3, 128), f)
    for p in range(EP):
        for half in (0, E):
            sel[half + 2 * p, p, 0, :] = 1.0
            sel[half + 2 * p + 1, p, 1, :] = 1.0
            sel[half + 2 * p, p, 2, 0:64] = 1.0
            sel[half + 2 * p + 1, p, 2, 64:128] = 1.0
    arrays = {
        "xT": np.ascontiguousarray(x["x"].reshape(B * N, D).T),
        "wqkvT": np.ascontiguousarray(x["L0_tok_w_qkv"].T), "wprojT": grouped(x["L0_tok_w_proj"].T),
        "bqk": per_group(bqkv[0:D], bqkv[D:2 * D]), "bv": rows(bqkv[2 * D:]), "bproj": rows(x["L0_tok_b_proj"]),
        "ident": np.eye(128, dtype=f), "hmask": hmask, "qmask": qmask,
        "awqkv": grouped(np.concatenate([x["L0_attn_Wq"], x["L0_attn_Wk"], x["L0_attn_Wv"]], axis=1)),
        "awo": grouped(x["L0_attn_Wo"]), "abqk": per_group(x["L0_attn_bq"], x["L0_attn_bk"]),
        "abv": rows(x["L0_attn_bv"]), "abo": rows(x["L0_attn_bo"]), "tscale": rows(x["L0_ffn_scale"]),
        "gwT": np.ascontiguousarray(x["L0_ffn_gate_w"].T), "gb": rows(x["L0_ffn_gate_b"]),
        "lower": np.ascontiguousarray(np.broadcast_to(lower, (128, E, E))),
        "b2dup": np.concatenate([x["L0_ffn_b2"], x["L0_ffn_b2"]]), "relT": np.ascontiguousarray(relT),
        "w1": np.ascontiguousarray(w1k.transpose(1, 0, 2, 3).reshape(128, -1)),
        "b1": np.ascontiguousarray(b1t.transpose(2, 0, 1)),
        "w2": np.ascontiguousarray(w2k.transpose(1, 0, 2, 3).reshape(128, -1)),
        "sel": sel.reshape(128, -1),
    }
    nc = bacc.Bacc("TRN2", target_bir_lowering=False, num_devices=1)
    feeds, aps = {}, {}
    for name, array in arrays.items():
        feeds["in_" + name] = array
        aps[name] = nc.dram_tensor("in_" + name, array.shape, mybir.dt.from_np(array.dtype), kind="ExternalInput").ap()
    out = nc.dram_tensor("out", (B, Q, D), F32, kind="ExternalOutput").ap()
    audio_tower(nc, aps, out.rearrange("b q n -> (b q) n").rearrange("(t p) n -> p t n", p=128))
    r = run(nc, [feeds], core_ids=[0])
    return r.results[0]["out"]
```

```python
import concourse.bass as bass
from concourse import mybir
from contextlib import ExitStack

F32 = mybir.dt.float32
F32R = mybir.dt.float32r
I32 = mybir.dt.int32
ALU = mybir.AluOpType
ACT = mybir.ActivationFunctionType
AX = mybir.AxisListType

B, N, D = 64, 256, 192
H, DK = 12, 16
Q = 64
STRIDE = N // Q
G, GC = 2, D // 2
PR = H // 2
PG = PR // G
PC = 2 * DK
MAXREL = 32
T = B * Q
NT = T // 128
TOK = 2 * N
REL = 128
E, TOPK, I = 16, 4, 192
EP = E // 2
M1 = 6 * 128
CH = 512
NC = T // CH
ALPHA, LIMIT, EPS = 1.702, 7.0, 1e-5
SCALE = DK ** -0.5


class At:

    def __init__(self, c, r=None):
        self.c, self.r, self.par = c, r, c % 2

    def __add__(self, d):
        return At(self.c + d, self.r)

    def __sub__(self, d):
        return self + -d

    def at(self, n):
        return self.r is None and self.c == n

    @property
    def n(self):
        return self.c if self.r is None else 2 * self.r + self.c

    @property
    def half(self):
        return self.c // 2 if self.r is None else self.r + self.c // 2

    def on(self, n):
        return self.r is not None or 0 <= self.c < n


def wait(e, sem, value):
    if not isinstance(value, int) or value > 0:
        e.wait_ge(sem, value)


def sweep(e, n, body, lead=1, lag=1):
    rounds = (n - 3 - lead) // 2
    for c in range(-lead, 3):
        body(At(c))
    with e.Fori(0, rounds) as r:
        for p in range(2):
            body(At(3 + p, r))
    for c in range(3 + 2 * rounds, n + lag):
        body(At(c))


class Chain:

    def __init__(self, e, sem, per, k, done=0):
        self.e, self.sem, self.base, self.m = e, sem, per * k.n, done

    def __call__(self, ins):
        self.m += 1
        ins.then_inc(self.sem, 1)
        self.e.wait_ge(self.sem, self.base + self.m)


def tile_of(hall, k):
    return hall[:, bass.ds(k.n * D, D)]


class LocalWeights:

    def __init__(self, nc, c, a):
        sb = lambda n, s, d=F32: c.enter_context(nc.sbuf_tensor(n, s, d))
        self.wqkv = sb("l_wqkv", [GC, G, 3 * D])
        self.wo = sb("l_wo", [GC, G, D])
        self.bqk = sb("l_bqk", [GC, 2 * G])
        self.bv = sb("l_bv", [128, D])
        self.bo = sb("l_bo", [128, D])
        self.tscale = sb("l_tscale", [128, D])
        self.gw = sb("l_gw", [128, 2, E])
        self.gb = sb("l_gb", [128, E])
        self.lower = sb("l_lower", [128, E, E], I32)
        self.b2 = sb("l_b2", [2 * E, D])
        self.kr = sb("l_k_rel", [GC, 2, G, 2, Q + REL])
        self.loaded = c.enter_context(nc.semaphore("l_weights"))
        self.zeros = c.enter_context(nc.semaphore("l_gate_zeros"))
        self.loads = (
            (self.wqkv[:, :, :], a["awqkv"]), (self.wo[:, :, :], a["awo"]), (self.bqk[:, :], a["abqk"]),
            (self.bv[:, :], a["abv"]), (self.bo[:, :], a["abo"]), (self.tscale[:, :], a["tscale"]),
            (self.gw[:, 0, :], a["gwT"][0:128, :]), (self.gw[0:D - 128, 1, :], a["gwT"][128:D, :]),
            (self.gb[:, :], a["gb"]), (self.lower[:, :, :], a["lower"]), (self.b2[:, :], a["b2dup"]),
            (self.kr[:, :, :, :, Q:].rearrange("p s g b w -> p (s g b) w"), a["relT"]))
        self.count = 16 * len(self.loads)


class ExpertWeights:

    HIGH, LOW = 13, 12

    def __init__(self, nc, c, a):
        sb = lambda n, s, d=F32: c.enter_context(nc.sbuf_tensor(n, s, d))
        sem = lambda n: c.enter_context(nc.semaphore(n))
        self.nc, self.a = nc, a
        self.stage = sb("e_w1_stage", [128, 2, M1])
        self.selst = sb("e_sel_stage", [128, 2, 128])
        self.w2st = sb("e_w2_stage", [128, 3, D])
        self.w1h = sb("e_w1_high", [128, 2, 2, M1], F32R)
        self.w1l = sb("e_w1_low", [128, 2, 2, M1], F32R)
        self.sel = sb("e_sel", [128, 2, 2, 128], F32R)
        self.w2a = sb("e_w2a", [128, 2, 3, 2, 128], F32R)
        self.w2b = sb("e_w2b", [128, 2, 3, 2, D - 128], F32R)
        self.b1 = sb("e_b1", [128, EP, 6])
        self.b1_in = sem("e_b1_in")
        self.staged = sem("e_stage_in")
        self.high = sem("e_high_done")
        self.low = sem("e_low_done")

    def load_stage(self, sp, n):
        for dst, name, width in ((self.stage, "w1", 2 * M1), (self.selst, "sel", 2 * 128),
                                 (self.w2st, "w2", 3 * D)):
            sp.dma_start(dst[:, :, :], self.a[name][:, bass.ds(n * width, width)]).then_inc(self.staged, 16)

    def select(self, act, n, par):
        act.wait_ge(self.staged, 48 * (n + 1))
        self.nc.scalar.activation(self.sel[:, par, :, :], self.selst[:, :, :], ACT.Copy).then_inc(self.high, 1)

    def piece(self, m, p, par):
        cols = bass.ds(512 * m + 256 * p, 256)
        flat = lambda t: t.rearrange("p m n -> p (m n)")[:, cols]
        yield flat(self.stage[:, :, :]), flat(self.w1h[:, par, :, :]), flat(self.w1l[:, par, :, :])
        m = bass.ds(m, 1)
        w, src = ((self.w2a, self.w2st[:, m, 0:128]), (self.w2b, self.w2st[:, m, 128:D]))[p]
        yield src, w[:, par, m, 0, :], w[:, par, m, 1, :]

    def round(self, m, p, par):
        for src, high, _ in self.piece(m, p, par):
            self.nc.scalar.activation(high, src, ACT.Copy).then_inc(self.high, 1)

    def rest(self, pool, n, m, p, par):
        pool.wait_ge(self.high, self.HIGH * n + 4 * m + 2 * p + 3)
        for src, high, low in self.piece(m, p, par):
            self.nc.gpsimd.tensor_tensor(low, src, high.bitcast(F32), ALU.subtract).then_inc(self.low, 1)


def pool_attention(nc, hall, wT, ident, hmask, qmask, lw, a):
    with ExitStack() as c:
        sb = lambda n, s, d=F32: c.enter_context(nc.sbuf_tensor(n, s, d))
        ps = lambda n, s: c.enter_context(nc.psum_tensor(n, s, F32))
        sem = lambda n: c.enter_context(nc.semaphore(n))
        x = sb("p_x", [128, 2, 2, TOK])
        xah = sb("p_xA_high", [128, 2, TOK], F32R)
        xal = sb("p_xA_low", [128, 2, TOK], F32R)
        xbs = sb("p_xB_high_low", [128, 2, TOK], F32R)
        wqk = sb("p_wqk", [128, 2, 2 * D])
        wqkh = sb("p_wqk_high", [128, 2, 2 * D], F32R)
        wqkl = sb("p_wqk_low", [128, 2, 2 * D], F32R)
        wv = sb("p_wv", [128, 2, D])
        wvs = sb("p_wv_high_low", [128, 2, 2, D], F32R)
        wproj = sb("p_wproj", [GC, G, D])
        bqk = sb("p_bqk", [GC, 2 * G])
        bv = sb("p_bv", [128, D])
        bproj = sb("p_bproj", [128, D])
        qmax = sb("p_qmax", [GC, G, 2, Q])
        qpad = sb("p_qpad", [GC, 2, G, 2, PG * 2 * Q])
        kT = sb("p_kT", [GC, 2, G, TOK])
        v = sb("p_v", [128, 2, 4, D])
        p = sb("p_p", [128, 2, PR, N])
        pT = sb("p_pT", [128, 2, PR * 2, 128])
        negmax = sb("p_negmax", [128, 2, PR])
        total = sb("p_total", [128, 2, PR])
        inv = sb("p_inv", [128, 2, PR])
        idle = sb("p_idle", [128, 2])
        osel = sb("p_osel", [GC, G * 2, Q])
        oT = sb("p_oT", [GC, G, 2 * Q])
        ringA = [ps(f"p_psA{n}", [128, 512]) for n in range(2)]
        scores = [ps(f"p_psS{n}", [128, 2, N]) for n in range(3)]
        ringT = [ps(f"p_psT{n}", [128, 4, 128]) for n in range(2)]
        psO = ps("p_psO", [128, 512])

        s_wqk = sem("p_wqk_in")
        s_w = sem("p_weights")
        s_wvh = sem("p_wv_high_done")
        s_wvl = sem("p_wv_low_done")
        s_vp = sem("p_v_part_done")
        s_wh = sem("p_wqk_high_done")
        s_wl = sem("p_wqk_low_done")
        s_xh = sem("p_x_high_done")
        s_xal = sem("p_xA_low_done")
        s_xbl = sem("p_xB_low_done")
        s_x = [sem(f"p_x_in{n}") for n in range(2)]
        s_qk = sem("p_qk_mm")
        s_v = sem("p_v_mm")
        s_qmax = sem("p_qmax_done")
        s_qpad = sem("p_qpad_done")
        s_kT = sem("p_kT_done")
        s_vsb = sem("p_v_done")
        s_s = sem("p_scores_mm")
        s_mx = sem("p_max_done")
        s_exp = sem("p_exp_done")
        s_inv = sem("p_inv_done")
        s_p = sem("p_probs_done")
        s_t = sem("p_transposed")
        s_ta = sem("p_pT_by_act")
        s_tv = sem("p_pT_by_dve")
        s_pv = sem("p_pv_mm")
        s_osel = sem("p_osel_half")
        s_oT = sem("p_oT_done")
        s_out = sem("p_out_mm")
        s_h = sem("p_h_done")
        s_wz = sem("p_wT_zeros")

        loads_qk = ((wqk[:, 0, :], a["wqkvT"][0:128, 0:2 * D]), (wqk[0:64, 1, :], a["wqkvT"][128:D, 0:2 * D]),
                    (wqk[64:128, 1, :], a["wqkvT"][128:D, 0:2 * D]))
        loads = ((bqk[:, :], a["bqk"]), (qmask[:, :, :], a["qmask"]), (wv[:, 0, :], a["wqkvT"][0:128, 2 * D:]),
                 (wv[0:64, 1, :], a["wqkvT"][128:D, 2 * D:]), (wv[64:128, 1, :], a["wqkvT"][128:D, 2 * D:]), (bv[:, :], a["bv"]), (ident[:, :], a["ident"]),
                 (hmask[:, :], a["hmask"]), (wproj[:, :, :], a["wprojT"]), (bproj[:, :], a["bproj"]))
        W_ALL = 16 * len(loads)

        with nc.Block() as block:

            @block.sync
            def _(sp):
                for dst, src in loads_qk:
                    sp.dma_start(dst, src).then_inc(s_wqk, 16)

                def load(k):
                    if not k.on(NT):
                        return
                    wait(sp, s_xal, k.n - 1)
                    wait(sp, s_xbl, k.n - 1)
                    cols = bass.ds(k.n * TOK, TOK)
                    for dst, src in ((x[:, k.par, 0, :], a["xT"][0:128, cols]),
                                     (x[0:64, k.par, 1, :], a["xT"][128:D, cols]),
                                     (x[64:128, k.par, 1, :], a["xT"][128:D, cols])):
                        sp.dma_start(dst, src).then_inc(s_x[k.par], 16)

                load(At(0))
                for dst, src in loads:
                    sp.dma_start(dst, src).then_inc(s_w, 16)
                sweep(sp, NT, lambda k: load(k + 1), lead=0, lag=0)
                sp.wait_ge(lw.zeros, 1)
                for dst, src in lw.loads:
                    sp.dma_start(dst, src).then_inc(lw.loaded, 16)

            @block.tensor
            def _(pe):
                pe.wait_ge(s_wl, 1)

                def project_qk(k, which):
                    if not k.on(NT):
                        return
                    if which == 0:
                        pe.wait_ge(s_xh, 2 * k.n + 2)
                        pe.wait_ge(s_xal, k.n + 1)
                        pe.wait_ge(s_xbl, k.n + 1)
                    for g in range(G):
                        n = 2 * which + g
                        if n < 2:
                            wait(pe, s_vsb, 4 * k.n + n - 1)
                        else:
                            pe.wait_ge(s_qmax, 2 * k.n + g + 1)
                        w = slice(which * D + g * GC, which * D + (g + 1) * GC)
                        parts = ((wqkh[:, 0, w], xah), (wqkh[:, 0, w], xal), (wqkl[:, 0, w], xah),
                                 (wqkh[:, 1, w], xbs), (wqkl[:, 1, w], xbs))
                        for q, (lhsT, rhs) in enumerate(parts):
                            last = nc.tensor.matmul(ringA[n % 2][0:GC, :], lhsT, rhs[:, k.par, :],
                                                    start=q == 0, stop=q == len(parts) - 1)
                        last.then_inc(s_qk, 1)

                def project_v(k, t):
                    if not k.on(NT):
                        return
                    if k.c == 0 and t == 0:
                        pe.wait_ge(s_wvl, 1)
                    if t < 2:
                        pe.wait_ge(s_kT, 2 * k.n + t + 1)
                    else:
                        pe.wait_ge(s_vsb, 4 * k.n + t - 1)
                    tok = slice(t * 128, (t + 1) * 128)
                    nc.tensor.matmul(ringA[t % 2][:, 0:2 * D], xah[:, k.par, tok], wvs[:, 0, :, :],
                                     start=True, stop=False)
                    nc.tensor.matmul(ringA[t % 2][:, 0:D], xal[:, k.par, tok], wvs[:, 0, 0, :],
                                     start=False, stop=False)
                    nc.tensor.matmul(ringA[t % 2][:, 0:2 * D], xbs[:, k.par, tok], wvs[:, 1, :, :],
                                     start=False, stop=True).then_inc(s_v, 1)

                def score(k, b, u):
                    if not k.on(NT):
                        return
                    if b == 0 and u == 0:
                        pe.wait_ge(s_qpad, 4 * k.n + 4)
                        pe.wait_ge(s_kT, 2 * k.n + 2)
                    wait(pe, s_exp, 12 * k.n + 6 * (b - 1) + 2 * u + 2)
                    for m in range(2):
                        g, i = (2 * u + m) // PG, (2 * u + m) % PG
                        last = nc.tensor.matmul(
                            scores[u][:, m, :], qpad[:, k.par, g, b, i * 128:(i + 1) * 128],
                            kT[:, k.par, g, b * N:(b + 1) * N], start=True, stop=True)
                    last.then_inc(s_s, 1)

                def transpose_p(k, b, u):
                    if not k.on(NT):
                        return
                    n = 3 * b + u
                    s, per, before = ((s_tv, 2, 0), (s_ta, 4, 0), (s_ta, 4, 1),
                                      (s_tv, 2, 1), (s_ta, 4, 2), (s_ta, 4, 3))[n]
                    wait(pe, s, per * k.n + before)
                    pe.wait_ge(s_p, 6 * k.n + n + 1)
                    for m in range(4):
                        last = nc.tensor.transpose(
                            ringT[n % 2][:, m, :],
                            p[:, b, 2 * u + m // 2, (m % 2) * 128:(m % 2 + 1) * 128], ident[:, :])
                    last.then_inc(s_t, 1)

                def weigh(k, b, u):
                    if not k.on(NT):
                        return
                    if b == 0 and u == 0:
                        wait(pe, s_h, k.n)
                    if u == 0:
                        pe.wait_ge(s_vsb, 4 * k.n + 4)
                    if u == 1:
                        pe.wait_ge(s_tv, 2 * k.n + b + 1)
                    else:
                        pe.wait_ge(s_ta, 4 * k.n + 2 * b + u // 2 + 1)
                    for j in (2 * u, 2 * u + 1):
                        g, i = j // PG, j % PG
                        for kt in range(2):
                            last = nc.tensor.matmul(
                                psO[i * PC:(i + 1) * PC, (2 * g + b) * 128:(2 * g + b + 1) * 128],
                                v[:, k.par, 2 * b + kt, j * PC:(j + 1) * PC], pT[:, b, 2 * j + kt, :],
                                start=kt == 0, stop=kt == 1)
                    if u == 2:
                        last.then_inc(s_pv, 1)

                def project_out(k):
                    if not k.on(NT):
                        return
                    pe.wait_ge(s_oT, k.n + 1)
                    for g in range(G):
                        last = nc.tensor.matmul(psO[:, 0:D], oT[:, g, :], wproj[:, g, :],
                                                start=g == 0, stop=g == G - 1)
                    last.then_inc(s_out, 1)

                def body(i):
                    score(i, 0, 1)
                    project_v(i, 3)
                    transpose_p(i - 1, 0, 2)
                    weigh(i - 1, 0, 0)
                    weigh(i - 1, 0, 1)
                    transpose_p(i - 1, 1, 0)
                    score(i, 0, 2)
                    project_qk(i + 1, 0)
                    project_qk(i + 1, 1)
                    transpose_p(i - 1, 1, 1)
                    transpose_p(i - 1, 1, 2)
                    score(i, 1, 0)
                    weigh(i - 1, 0, 2)
                    weigh(i - 1, 1, 0)
                    weigh(i - 1, 1, 1)
                    score(i, 1, 1)
                    project_v(i + 1, 0)
                    weigh(i - 1, 1, 2)
                    transpose_p(i, 0, 0)
                    score(i, 1, 2)
                    project_v(i + 1, 1)
                    score(i + 1, 0, 0)
                    project_v(i + 1, 2)
                    project_out(i - 1)
                    transpose_p(i, 0, 1)

                sweep(pe, NT, body, lead=2, lag=2)

            @block.scalar
            def _(act):
                act.wait_ge(s_wqk, 16 * len(loads_qk))
                nc.scalar.activation(wqkh[:, :, :], wqk[:, :, :], ACT.Copy).then_inc(s_wh, 1)

                def round_x(k):
                    if not k.on(NT):
                        return
                    act.wait_ge(s_x[k.par], 48 * (k.half + 1))
                    wait(act, s_v, 4 * (k.n - 1))
                    nc.scalar.activation(xah[:, k.par, :], x[:, k.par, 0, :], ACT.Copy).then_inc(s_xh, 1)
                    nc.scalar.activation(xbs[:, k.par, :], x[:, k.par, 1, :], ACT.Copy).then_inc(s_xh, 1)

                def exps(k, b, u):
                    if not k.on(NT):
                        return
                    act.wait_ge(s_mx, 6 * k.n + 3 * b + u + 1)
                    for j in (2 * u, 2 * u + 1):
                        nc.scalar.activation(p[:, b, j, :], scores[j // 2][:, j % 2, :], ACT.Exp,
                                             bias=negmax[:, b, j:j + 1], scale=1.0,
                                             accum_out=total[:, b, j:j + 1]).then_inc(s_exp, 1)

                def copy_k(k, g):
                    if not k.on(NT):
                        return
                    if k.c == 0 and g == 0:
                        act.wait_ge(s_w, W_ALL)
                        nc.scalar.activation(wvs[:, :, 0, :], wv[:, :, :], ACT.Copy).then_inc(s_wvh, 1)
                    act.wait_ge(s_qk, 4 * k.n + 2 + g + 1)
                    nc.scalar.activation(kT[:, k.par, g, :], ringA[g][0:GC, :], ACT.Identity,
                                         bias=bqk[:, G + g:G + g + 1]).then_inc(s_kT, 1)

                def copy_pT(k, b, u):
                    if not k.on(NT):
                        return
                    n = 3 * b + u
                    act.wait_ge(s_t, 6 * k.n + n + 1)
                    nc.scalar.activation(pT[:, b, 4 * u:4 * u + 4, :], ringT[n % 2][:, :, :],
                                         ACT.Copy).then_inc(s_ta, 1)

                def body(i):
                    copy_pT(i - 1, 1, 0)
                    round_x(i + 2)
                    exps(i, 0, 1)
                    exps(i, 0, 2)
                    copy_k(i + 1, 0)
                    copy_pT(i - 1, 1, 2)
                    copy_k(i + 1, 1)
                    exps(i, 1, 0)
                    exps(i, 1, 1)
                    exps(i, 1, 2)
                    copy_pT(i, 0, 0)
                    copy_pT(i, 0, 2)
                    exps(i + 1, 0, 0)

                sweep(act, NT, body, lead=2, lag=2)

            @block.vector
            def _(dve):

                def rest_of_x(k):
                    if not k.on(NT):
                        return
                    dve.wait_ge(s_xh, 2 * k.n + 2)
                    low = xbs[64:128, k.par, :]
                    nc.vector.tensor_tensor(low, x[64:128, k.par, 1, :], low.bitcast(F32), ALU.subtract)\
                      .then_inc(s_xbl, 1)

                def pool_q(k, g):
                    if not k.on(NT):
                        return
                    dve.wait_ge(s_qk, 4 * k.n + g + 1)
                    nc.vector.tensor_reduce(
                        qmax[:, g, :, :],
                        ringA[g][0:GC, :].rearrange("p (b s w) -> p b w s", b=2, s=STRIDE),
                        AX.X, ALU.max).then_inc(s_qmax, 1)

                def pad_q(k, g):
                    if not k.on(NT):
                        return
                    if k.c == 0 and g == 0:
                        dve.wait_ge(s_w, W_ALL)
                    dve.wait_ge(s_qmax, 2 * k.n + g + 1)
                    for b in range(2):
                        nc.vector.scalar_tensor_tensor(
                            out=qpad[:, k.par, g, b, :].rearrange("p (m w) -> p m w", w=Q),
                            in0=qmax[:, g, b, :].unsqueeze(1).broadcast_to([GC, 2 * PG, Q]),
                            scalar=bqk[:, g:g + 1], in1=qmask[:, :, :],
                            op0=ALU.add, op1=ALU.mult).then_inc(s_qpad, 1)

                def row_max(k, b, u):
                    if not k.on(NT):
                        return
                    dve.wait_ge(s_s, 6 * k.n + 3 * b + u + 1)
                    nc.vector.tensor_reduce(negmax[:, b, 2 * u:2 * u + 2], scores[u][:, :, :], AX.X,
                                            ALU.max, negate=True).then_inc(s_mx, 1)

                def invert(k, b):
                    if not k.on(NT):
                        return
                    dve.wait_ge(s_exp, 12 * k.n + 6 * b + 6)
                    nc.vector.reciprocal(inv[:, b, :], total[:, b, :]).then_inc(s_inv, 1)

                def copy_pT(k, b):
                    if not k.on(NT):
                        return
                    n = 3 * b + 1
                    dve.wait_ge(s_t, 6 * k.n + n + 1)
                    nc.vector.tensor_copy(pT[:, b, 4:8, :], ringT[n % 2][:, :, :]).then_inc(s_tv, 1)

                def select_heads(k):
                    if not k.on(NT):
                        return
                    dve.wait_ge(s_pv, 2 * k.n + 2)
                    o = psO[0:GC, :].rearrange("p (m h w) -> p m h w", h=2, w=Q)
                    nc.vector.tensor_scalar(osel[:, :, :], o[:, :, 0, :], hmask[:, 0:1], None, ALU.mult)\
                      .then_inc(s_osel, 1)
                    dve.wait_ge(s_osel, k.n + 1)
                    nc.vector.scalar_tensor_tensor(
                        out=oT[:, :, :].rearrange("p g (b w) -> p (g b) w", w=Q), in0=o[:, :, 1, :],
                        scalar=hmask[:, 1:2], in1=osel[:, :, :], op0=ALU.mult, op1=ALU.add).then_inc(s_oT, 1)

                def copy_out(k):
                    if not k.on(NT):
                        return
                    dve.wait_ge(s_out, k.n + 1)
                    nc.vector.tensor_tensor(tile_of(hall, k), psO[:, 0:D], bproj[:, :], ALU.add)\
                      .then_inc(s_h, 1)

                def copy_v(k, t):
                    if not k.on(NT):
                        return
                    if k.c == 0 and t == 0:
                        dve.wait_ge(s_wvh, 1)
                        nc.vector.tensor_tensor(wvs[:, :, 1, :], wv[:, :, :], wvs[:, :, 0, :].bitcast(F32),
                                                ALU.subtract).then_inc(s_wvl, 1)
                    dve.wait_ge(s_v, 4 * k.n + t + 1)
                    nc.vector.tensor_tensor(v[:, k.par, t, :], ringA[t % 2][:, 0:D], bv[:, :], ALU.add)\
                      .then_inc(s_vp, 1)
                    dve.wait_ge(s_vp, 4 * k.n + t + 1)
                    nc.vector.tensor_tensor(v[:, k.par, t, :], ringA[t % 2][:, D:2 * D], v[:, k.par, t, :],
                                            ALU.add).then_inc(s_vsb, 1)

                def body(i):
                    invert(i - 1, 1)
                    copy_out(i - 2)
                    copy_pT(i - 1, 0)
                    row_max(i, 0, 0)
                    copy_v(i, 3)
                    row_max(i, 0, 1)
                    pool_q(i + 1, 0)
                    pool_q(i + 1, 1)
                    row_max(i, 0, 2)
                    copy_pT(i - 1, 1)
                    pad_q(i + 1, 0)
                    invert(i, 0)
                    row_max(i, 1, 0)
                    pad_q(i + 1, 1)
                    select_heads(i - 1)
                    row_max(i, 1, 1)
                    copy_v(i + 1, 0)
                    copy_v(i + 1, 1)
                    row_max(i, 1, 2)
                    copy_v(i + 1, 2)
                    rest_of_x(i + 2)

                sweep(dve, NT, body, lead=2, lag=2)

            @block.gpsimd
            def _(pool):
                nc.gpsimd.memset(lw.gw[:, 1, :], 0.0).then_inc(lw.zeros, 1)
                pool.wait_ge(s_wh, 1)
                nc.gpsimd.tensor_tensor(wqkl[:, :, :], wqk[:, :, :], wqkh[:, :, :].bitcast(F32), ALU.subtract)\
                  .then_inc(s_wl, 1)

                def rest_of_x(k):
                    if not k.on(NT):
                        return
                    pool.wait_ge(s_xh, 2 * k.n + 2)
                    nc.gpsimd.tensor_tensor(xal[:, k.par, :], x[:, k.par, 0, :], xah[:, k.par, :].bitcast(F32),
                                            ALU.subtract).then_inc(s_xal, 1)

                def normalise(k, b, u):
                    if not k.on(NT):
                        return
                    if u == 0:
                        pool.wait_ge(s_inv, 2 * k.n + b + 1)
                        nc.gpsimd.tensor_tensor(idle[:, b:b + 1], inv[:, b, 0:1], inv[:, b, 0:1], ALU.mult)
                    for j in (2 * u, 2 * u + 1):
                        last = nc.gpsimd.tensor_scalar(p[:, b, j, :], p[:, b, j, :], inv[:, b, j:j + 1],
                                                       1.0, ALU.mult, ALU.mult)
                    last.then_inc(s_p, 1)

                def body(i):
                    normalise(i, 0, 0)
                    normalise(i, 0, 1)
                    rest_of_x(i + 2)
                    normalise(i, 0, 2)
                    normalise(i, 1, 0)
                    normalise(i, 1, 1)
                    normalise(i, 1, 2)

                sweep(pool, NT, body, lead=2, lag=2)
                nc.gpsimd.memset(wT[:, :].bitcast(F32), 0.0).then_inc(s_wz, 1)
                pool.wait_ge(s_wz, 1)


def local_attention(nc, hall, tAh, tAl, tBs, wT, ident, hmask, qmask, scratch, lw, ew):
    with ExitStack() as c:
        sb = lambda n, s, d=F32: c.enter_context(nc.sbuf_tensor(n, s, d))
        ps = lambda n, s: c.enter_context(nc.psum_tensor(n, s, F32))
        sem = lambda n: c.enter_context(nc.semaphore(n))
        wqkv, wo, bqk, bv, bo, tscale = lw.wqkv, lw.wo, lw.bqk, lw.bv, lw.bo, lw.tscale
        gw, gb, lower, b2, kr = lw.gw, lw.gb, lw.lower, lw.b2, lw.kr
        mhalf = sb("l_minus_half", [128, 1])
        idle = sb("l_idle", [128, 3])
        stats = sb("l_stats", [128, 6])
        meanvar = sb("l_meanvar", [128, 2, 2])
        vareps = sb("l_vareps", [128, 2])
        rstd = sb("l_rstd", [128, 2])
        xn = sb("l_xn", [128, D])
        xnT = sb("l_xnT", [GC, G, 128])
        qpad = sb("l_qpad", [GC, G, 2, PG * 2 * Q])
        qb = sb("l_q", [GC, G, 2 * Q])
        v = sb("l_v", [128, 2, 2, D])
        sq = sb("l_sq", [128, 2, 2, PR, Q + REL])
        bias = sb("l_bias", [128, 2, 2, PR, Q])
        z = sb("l_z", [128, PR, 2, Q])
        p2 = sb("l_p", [128, PR, 2, Q])
        rowmax = sb("l_rowmax", [128, PR * 2])
        total = sb("l_total", [128, PR * 2])
        inv = sb("l_inv", [128, PR * 2])
        pT = sb("l_pT", [128, PR, 128])
        osel = sb("l_osel", [GC, G * 2, Q])
        oT = sb("l_oT", [GC, G, 2 * Q])
        h2 = sb("l_h2", [128, D])
        hn = sb("l_hn", [128, D])
        square = sb("l_square", [128, D])
        ss = sb("l_ss", [128, 1])
        mseps = sb("l_mseps", [128, 1])
        rrms = sb("l_rrms", [128, 1])
        t = sb("l_t", [128, 256])
        tT = sb("l_tT", [128, 2, 128])
        tBr = sb("l_tB_round", [128, 128], F32R)
        gate = sb("l_gate", [128, E])
        above = sb("l_above", [128, E, E])
        notbelow = sb("l_notbelow", [128, E, E])
        rank = sb("l_rank", [128, E])
        gmax = sb("l_gmax", [128, 1])
        gexp = sb("l_gexp", [128, E])
        chosen = sb("l_chosen", [128, E])
        gsum = sb("l_gsum", [128, 1])
        ginv = sb("l_ginv", [128, 1])
        w = sb("l_w", [128, E])
        w32 = sb("l_w32", [128, 2 * E], F32R)
        w32T = sb("l_w32T", [2 * E, 128])
        ringA = [ps(f"l_psA{n}", [128, 512]) for n in range(2)]
        ringS = [ps(f"l_psS{n}", [128, 2, Q + REL]) for n in range(3)]
        psT = ps("l_psT", [128, 4, 128])
        psO = ps("l_psO", [128, 512])
        psH = ps("l_psH", [128, 512])

        s_vz = sem("l_v_zeros")
        s_half = sem("l_minus_half_done")
        s_ln = sem("l_ln_steps")
        s_ve = sem("l_vareps_done")
        s_rstd = sem("l_rstd_done")
        s_xn = sem("l_xn_done")
        s_xT = sem("l_xn_transposed")
        s_xnT = sem("l_xnT_done")
        s_q = sem("l_q_mm")
        s_qb = sem("l_q_done")
        s_qpad = sem("l_qpad_done")
        s_k = sem("l_k_mm")
        s_kr = sem("l_k_done")
        s_v = sem("l_v_mm")
        s_vsb = sem("l_v_done")
        s_s = sem("l_scores_mm")
        s_sq = sem("l_sq_done")
        s_wr = [sem(f"l_rel_written{n}") for n in range(2)]
        s_rd = [sem(f"l_rel_read{n}") for n in range(2)]
        s_z = sem("l_z_done")
        s_rm = sem("l_rowmax_done")
        s_sm = sem("l_total_done")
        s_sub = sem("l_z_less_max")
        s_exp = sem("l_exp_done")
        s_inv = sem("l_inv_done")
        s_p = sem("l_probs_done")
        s_t = sem("l_p_transposed")
        s_pTa = sem("l_pT_first_done")
        s_pTb = sem("l_pT_rest_done")
        s_pv = sem("l_pv_mm")
        s_os = sem("l_osel_steps")
        s_oT = sem("l_oT_done")
        s_out = sem("l_out_mm")
        s_n2 = sem("l_norm2_steps")
        s_ve2 = sem("l_vareps2_done")
        s_rstd2 = sem("l_rstd2_done")
        s_hn = sem("l_hn_done")
        s_ss = sem("l_ss_done")
        s_ms = sem("l_mseps_done")
        s_rr = sem("l_rrms_done")
        s_tt = sem("l_t_done")
        s_tTm = sem("l_t_transposed")
        s_tT = sem("l_tT_done")
        s_th = sem("l_t_high_done")
        s_sp = sem("l_split_done")
        s_gm = sem("l_gate_mm")
        s_gs = sem("l_gate_steps")
        s_gmx = sem("l_gmax_done")
        s_gex = sem("l_gexp_done")
        s_w32 = sem("l_w32_done")
        s_wTm = sem("l_w32_transposed")
        s_wT = sem("l_w32T_done")
        s_b2m = sem("l_b2_mm")
        s_b2 = sem("l_b2_added")
        s_gw = sem("l_w_steps")
        s_wTa = sem("l_wT_stored")

        with nc.Block() as block:

            @block.sync
            def _(sp):
                def skew(k):
                    par = k.par
                    sp.wait_ge(s_sq, 6 * k.n + 3)
                    sp.dma_start(scratch[par, 0, :, :, :], sq[:, par, 0, :, Q:]).then_inc(s_wr[par], 16)
                    sp.wait_ge(s_sq, 6 * k.n + 6)
                    sp.dma_start(scratch[par, 1, :, :, :], sq[:, par, 1, :, Q:]).then_inc(s_wr[par], 16)
                    sp.wait_ge(s_wr[par], 32 * (k.half + 1))
                    row = PR * REL
                    for b in range(2):
                        for h in range(2):
                            src = bass.AP(scratch.tensor, ((par * 2 + b) * 128 + h * Q) * row + Q - 1,
                                          [[row - 1, Q], [REL, PR], [1, Q]])
                            sp.dma_start(bias[h * Q:(h + 1) * Q, par, b, :, :], src).then_inc(s_rd[par], 16)

                sweep(sp, NT, skew, lead=0, lag=0)
                sp.dma_start(ew.b1[:, :, :], ew.a["b1"]).then_inc(ew.b1_in, 16)
                ew.load_stage(sp, 0)

            @block.tensor
            def _(pe):
                pe.wait_ge(lw.loaded, lw.count)

                def transpose_xn(k):
                    if not k.on(NT):
                        return
                    pe.wait_ge(s_xn, k.n + 1)
                    wait(pe, s_kr, 2 * k.n)
                    for g in range(G):
                        last = nc.tensor.transpose(ringA[0][0:GC, g * 128:(g + 1) * 128],
                                                   xn[:, g * GC:(g + 1) * GC], ident[:, :])
                    last.then_inc(s_xT, 1)

                def project_q(k):
                    if not k.on(NT):
                        return
                    pe.wait_ge(s_xnT, k.n + 1)
                    wait(pe, s_vsb, 2 * k.n)
                    project(0, 1, s_q)

                def project_k(k):
                    if not k.on(NT):
                        return
                    pe.wait_ge(s_xnT, k.n + 1)
                    project(1, 0, s_k)

                def project(which, bank, done):
                    for g in range(G):
                        for h in range(G):
                            last = nc.tensor.matmul(
                                ringA[bank][0:GC, g * 128:(g + 1) * 128],
                                wqkv[:, h, which * D + g * GC:which * D + (g + 1) * GC], xnT[:, h, :],
                                start=h == 0, stop=h == G - 1)
                    last.then_inc(done, 1)

                def project_v(k):
                    if not k.on(NT):
                        return
                    pe.wait_ge(s_qb, 2 * k.n + 2)
                    for h in range(G):
                        last = nc.tensor.matmul(ringA[1][:, 0:D], xnT[:, h, :], wqkv[:, h, 2 * D:3 * D],
                                                start=h == 0, stop=h == G - 1)
                    last.then_inc(s_v, 1)

                def score(k, half):
                    if not k.on(NT):
                        return
                    if half == 0:
                        pe.wait_ge(s_qpad, 2 * k.n + 2)
                        pe.wait_ge(s_kr, 2 * k.n + 2)
                    for u in range(3 * half, 3 * half + 3):
                        b = u // 3
                        wait(pe, s_sq, 6 * k.n + u - 2)
                        for m in range(2):
                            j = 2 * (u % 3) + m
                            g, i = j // PG, j % PG
                            last = nc.tensor.matmul(ringS[u % 3][:, m, :], qpad[:, g, b, i * 128:(i + 1) * 128],
                                                    kr[:, k.par, g, b, :], start=True, stop=True)
                        last.then_inc(s_s, 1)

                def transpose_p(k, r):
                    if not k.on(NT):
                        return
                    pe.wait_ge(s_p, k.n + 1)
                    wait(pe, (s_pTb, s_pTa)[r], k.n + r)
                    for j in (range(0, 4), range(4, 6))[r]:
                        last = nc.tensor.transpose(psT[:, j % 4, :],
                                                   p2[:, j, :, :].rearrange("p b w -> p (b w)"), ident[:, :])
                    last.then_inc(s_t, 1)

                def weigh(k):
                    if not k.on(NT):
                        return
                    wait(pe, s_n2, 5 * k.n - 3)
                    pe.wait_ge(s_pTa, k.n + 1)
                    for j in range(PR):
                        if j == 4:
                            pe.wait_ge(s_pTb, k.n + 1)
                        g, i = j // PG, j % PG
                        for b in range(2):
                            last = nc.tensor.matmul(psO[i * PC:(i + 1) * PC, (2 * g + b) * 128:(2 * g + b + 1) * 128],
                                                    v[:, k.par, b, j * PC:(j + 1) * PC], pT[:, j, :],
                                                    start=True, stop=True)
                    last.then_inc(s_pv, 1)

                def project_out(k):
                    if not k.on(NT):
                        return
                    pe.wait_ge(s_oT, k.n + 1)
                    for g in range(G):
                        last = nc.tensor.matmul(psO[:, 0:D], oT[:, g, :], wo[:, g, :],
                                                start=g == 0, stop=g == G - 1)
                    last.then_inc(s_out, 1)

                def transpose_t(k):
                    if not k.on(NT):
                        return
                    wait(pe, s_b2, k.n)
                    pe.wait_ge(s_tt, 2 * k.n + 2)
                    for m in range(2):
                        last = nc.tensor.transpose(psH[:, m * 128:(m + 1) * 128], t[:, m * 128:(m + 1) * 128],
                                                   ident[:, :])
                    last.then_inc(s_tTm, 1)

                def gates(k):
                    if not k.on(NT):
                        return
                    pe.wait_ge(s_tT, k.n + 1)
                    for m in range(2):
                        last = nc.tensor.matmul(psH[:, 0:E], tT[:, m, :], gw[:, m, :], start=m == 0, stop=m == 1)
                    last.then_inc(s_gm, 1)

                def transpose_w(k):
                    if not k.on(NT):
                        return
                    pe.wait_ge(s_w32, k.n + 1)
                    nc.tensor.transpose(psH[0:2 * E, 0:128], w32[:, :].bitcast(F32), ident[:, :])\
                      .then_inc(s_wTm, 1)

                def expert_bias(k):
                    if not k.on(NT):
                        return
                    pe.wait_ge(s_wT, k.n + 1)
                    nc.tensor.matmul(psH[:, 0:D], w32T[:, :], b2[:, :], start=True, stop=True).then_inc(s_b2m, 1)

                def body(i):
                    transpose_t(i - 2)
                    project_q(i + 1)
                    project_k(i + 1)
                    gates(i - 2)
                    transpose_p(i - 1, 0)
                    transpose_p(i - 1, 1)
                    weigh(i - 1)
                    transpose_w(i - 2)
                    project_v(i + 1)
                    expert_bias(i - 2)
                    project_out(i - 1)
                    transpose_xn(i + 2)
                    score(i + 1, 0)
                    score(i + 1, 1)

                sweep(pe, NT, body, lead=2, lag=3)

            @block.scalar
            def _(act):
                act.wait_ge(lw.loaded, lw.count)

                def copy_xnT(k):
                    if not k.on(NT):
                        return
                    act.wait_ge(s_xT, k.n + 1)
                    nc.scalar.activation(xnT[:, :, :], ringA[0][0:GC, 0:G * 128], ACT.Copy).then_inc(s_xnT, 1)

                def copy_k(k):
                    if not k.on(NT):
                        return
                    act.wait_ge(s_k, k.n + 1)
                    wait(act, s_s, 6 * (k.n - 1))
                    for g in range(G):
                        nc.scalar.activation(
                            kr[:, k.par, g, :, 0:Q],
                            ringA[0][0:GC, g * 128:(g + 1) * 128].rearrange("p (b w) -> p b w", b=2),
                            ACT.Identity, bias=bqk[:, G + g:G + g + 1]).then_inc(s_kr, 1)

                def copy_q(k):
                    if not k.on(NT):
                        return
                    act.wait_ge(s_q, k.n + 1)
                    for g in range(G):
                        nc.scalar.activation(qb[:, g, :], ringA[1][0:GC, g * 128:(g + 1) * 128], ACT.Identity,
                                             bias=bqk[:, g:g + 1]).then_inc(s_qb, 1)

                def copy_scores(k, half):
                    if not k.on(NT):
                        return
                    if half == 0:
                        wait(act, s_wr[k.par], 32 * k.half)
                    for u in range(3 * half, 3 * half + 3):
                        act.wait_ge(s_s, 6 * k.n + u + 1)
                        j = 2 * (u % 3)
                        nc.scalar.activation(sq[:, k.par, u // 3, j:j + 2, :], ringS[u % 3][:, :, :], ACT.Copy)\
                          .then_inc(s_sq, 1)

                def exps(k):
                    if not k.on(NT):
                        return
                    act.wait_ge(s_sub, k.n + 1)
                    nc.scalar.activation(z[:, :, :, :], z[:, :, :, :], ACT.Exp).then_inc(s_exp, 1)

                def copy_pT(k, r):
                    if not k.on(NT):
                        return
                    lo, hi = ((0, 4), (4, 6))[r]
                    act.wait_ge(s_t, 2 * k.n + r + 1)
                    nc.scalar.activation(pT[:, lo:hi, :], psT[:, 0:hi - lo, :], ACT.Copy)\
                      .then_inc((s_pTa, s_pTb)[r], 1)

                def copy_tT(k):
                    if not k.on(NT):
                        return
                    act.wait_ge(s_tTm, k.n + 1)
                    nc.scalar.activation(tT[:, :, :], psH[:, 0:256], ACT.Copy).then_inc(s_tT, 1)

                def round_t(k):
                    if not k.on(NT):
                        return
                    act.wait_ge(s_tT, k.n + 1)
                    wait(act, s_sp, 2 * k.n)
                    cols = bass.ds(k.n * 128, 128)
                    nc.scalar.activation(tAh[:, cols], tT[:, 0, :], ACT.Copy).then_inc(s_th, 1)
                    nc.scalar.activation(tBs[0:64, cols], tT[0:64, 1, :], ACT.Copy).then_inc(s_th, 1)
                    nc.scalar.activation(tBr[64:128, :], tT[64:128, 1, :], ACT.Copy).then_inc(s_th, 1)

                def select_first(k):
                    if not k.on(NT):
                        return
                    act.wait_ge(s_pv, k.n + 1)
                    wait(act, s_oT, k.n)
                    o = psO[0:GC, :].rearrange("p (m h w) -> p m h w", h=2, w=Q)
                    nc.scalar.activation(osel[:, :, :], o[:, :, 0, :], ACT.Identity, scale=hmask[:, 0:1])\
                      .then_inc(s_os, 1)

                def gate_exp(k):
                    if not k.on(NT):
                        return
                    act.wait_ge(s_gmx, k.n + 1)
                    nc.scalar.activation(gexp[:, :], gate[:, :], ACT.Exp, bias=gmax[:, 0:1]).then_inc(s_gex, 1)

                def body(i):
                    round_t(i - 2)
                    copy_pT(i - 1, 0)
                    gate_exp(i - 2)
                    copy_k(i + 1)
                    copy_pT(i - 1, 1)
                    select_first(i - 1)
                    copy_scores(i + 1, 0)
                    copy_scores(i + 1, 1)
                    exps(i)
                    copy_xnT(i + 2)
                    copy_tT(i - 1)
                    copy_q(i + 2)

                sweep(act, NT, body, lead=2, lag=3)
                ew.select(act, 0, 0)
                for m in range(3):
                    for p in range(2):
                        ew.round(m, p, 0)

            @block.vector
            def _(dve):
                nc.vector.memset(mhalf[:, :], -0.5).then_inc(s_half, 1)
                dve.wait_ge(lw.loaded, lw.count)
                dve.wait_ge(s_vz, 1)

                def carry(n):
                    nc.vector.memset(idle[:, n:n + 1], 0.0)

                def norm1_stats(k):
                    if not k.on(NT):
                        return
                    do = Chain(dve, s_ln, 2, k)
                    do(nc.vector.bn_stats(stats[:, :], tile_of(hall, k)))
                    carry(0)
                    do(nc.vector.bn_aggr(meanvar[:, 0, :], stats[:, :]))
                    nc.vector.tensor_scalar(vareps[:, 0:1], meanvar[:, 0, 1:2], EPS, None, ALU.add)\
                      .then_inc(s_ve, 1)

                def norm1(k):
                    if not k.on(NT):
                        return
                    dve.wait_ge(s_rstd, k.n + 1)
                    wait(dve, s_xT, k.n)
                    nc.vector.tensor_scalar(xn[:, :], tile_of(hall, k), meanvar[:, 0, 0:1], rstd[:, 0:1],
                                            ALU.subtract, ALU.mult).then_inc(s_xn, 1)

                def copy_v(k):
                    if not k.on(NT):
                        return
                    dve.wait_ge(s_v, k.n + 1)
                    for b in range(2):
                        rows = slice(b * Q, (b + 1) * Q)
                        nc.vector.tensor_tensor(v[rows, k.par, b, :], ringA[1][rows, 0:D], bv[rows, :], ALU.add)\
                          .then_inc(s_vsb, 1)

                zr = z[:, :, :, :].rearrange("p j b w -> p (j b) w")

                def row_max(k):
                    if not k.on(NT):
                        return
                    dve.wait_ge(s_z, k.n + 1)
                    nc.vector.tensor_reduce(rowmax[:, :], zr, AX.X, ALU.max).then_inc(s_rm, 1)

                def less_max(k):
                    if not k.on(NT):
                        return
                    dve.wait_ge(s_rm, k.n + 1)
                    nc.vector.tensor_tensor(zr, zr, rowmax[:, :].unsqueeze(2).broadcast_to([128, 2 * PR, Q]),
                                            ALU.subtract).then_inc(s_sub, 1)

                def row_sum(k):
                    if not k.on(NT):
                        return
                    dve.wait_ge(s_exp, k.n + 1)
                    nc.vector.tensor_reduce(total[:, :], zr, AX.X, ALU.add).then_inc(s_sm, 1)

                def invert(k):
                    if not k.on(NT):
                        return
                    dve.wait_ge(s_sm, k.n + 1)
                    nc.vector.reciprocal(inv[:, :], total[:, :]).then_inc(s_inv, 1)

                def select_heads(k):
                    if not k.on(NT):
                        return
                    o = psO[0:GC, :].rearrange("p (m h w) -> p m h w", h=2, w=Q)
                    dve.wait_ge(s_os, k.n + 1)
                    nc.vector.scalar_tensor_tensor(
                        out=oT[:, :, :].rearrange("p g (b w) -> p (g b) w", w=Q), in0=o[:, :, 1, :],
                        scalar=hmask[:, 1:2], in1=osel[:, :, :], op0=ALU.mult, op1=ALU.add).then_inc(s_oT, 1)

                def bias_h(k):
                    if not k.on(NT):
                        return
                    nc.vector.tensor_tensor(h2[:, :], tile_of(hall, k), bo[:, :], ALU.add).then_inc(s_n2, 1)

                def norm2_stats(k):
                    if not k.on(NT):
                        return
                    do = Chain(dve, s_n2, 5, k, 1)
                    dve.wait_ge(s_n2, 5 * k.n + 1)
                    dve.wait_ge(s_out, k.n + 1)
                    do(nc.vector.tensor_tensor(h2[:, :], psO[:, 0:D], h2[:, :], ALU.add))
                    do(nc.vector.bn_stats(stats[:, :], h2[:, :]))
                    carry(1)
                    do(nc.vector.bn_aggr(meanvar[:, 1, :], stats[:, :]))
                    nc.vector.tensor_scalar(vareps[:, 1:2], meanvar[:, 1, 1:2], EPS, None, ALU.add)\
                      .then_inc(s_ve2, 1)

                def norm2(k):
                    if not k.on(NT):
                        return
                    dve.wait_ge(s_rstd2, k.n + 1)
                    nc.vector.tensor_scalar(hn[:, :], h2[:, :], meanvar[:, 1, 0:1], rstd[:, 1:2],
                                            ALU.subtract, ALU.mult).then_inc(s_hn, 1)
                    dve.wait_ge(s_hn, k.n + 1)
                    nc.vector.scalar_tensor_tensor(out=square[:, :], in0=hn[:, :], scalar=1.0, in1=hn[:, :],
                                                   op0=ALU.mult, op1=ALU.mult, accum_out=ss[:, :])\
                      .then_inc(s_ss, 1)
                    dve.wait_ge(s_ss, k.n + 1)
                    nc.vector.tensor_scalar(mseps[:, :], ss[:, :], 1.0 / D, EPS, ALU.mult, ALU.add)\
                      .then_inc(s_ms, 1)
                    nc.vector.tensor_tensor(tile_of(hall, k), h2[:, :], hn[:, :], ALU.add).then_inc(s_n2, 1)

                def scale_t(k):
                    if not k.on(NT):
                        return
                    dve.wait_ge(s_rr, k.n + 1)
                    nc.vector.scalar_tensor_tensor(out=t[:, 0:D], in0=hn[:, :], scalar=rrms[:, :],
                                                   in1=tscale[:, :], op0=ALU.mult, op1=ALU.mult)\
                      .then_inc(s_tt, 1)
                    nc.vector.scalar_tensor_tensor(out=t[:, D:256], in0=hn[:, 128:D], scalar=rrms[:, :],
                                                   in1=tscale[:, 128:D], op0=ALU.mult, op1=ALU.mult)\
                      .then_inc(s_tt, 1)

                def split_t(k):
                    if not k.on(NT):
                        return
                    dve.wait_ge(s_th, 3 * k.n + 3)
                    cols = bass.ds(k.n * 128, 128)
                    nc.vector.tensor_tensor(tAl[:, cols], tT[:, 0, :], tAh[:, cols].bitcast(F32), ALU.subtract)\
                      .then_inc(s_sp, 1)
                    nc.vector.tensor_tensor(tBs[64:128, cols], tT[64:128, 1, :], tBr[64:128, :].bitcast(F32),
                                            ALU.subtract).then_inc(s_sp, 1)

                def compare(k):
                    if not k.on(NT):
                        return
                    do = Chain(dve, s_gs, 8, k)
                    dve.wait_ge(s_gm, k.n + 1)
                    do(nc.vector.tensor_tensor(gate[:, :], psH[:, 0:E], gb[:, :], ALU.add))
                    other = gate[:, :].unsqueeze(1).broadcast_to([128, E, E])
                    own = gate[:, :].unsqueeze(2).broadcast_to([128, E, E])
                    nc.vector.tensor_reduce(gmax[:, :], gate[:, :], AX.X, ALU.max, negate=True)\
                      .then_inc(s_gmx, 1)
                    nc.vector.tensor_tensor(above[:, :, :], other, own, ALU.is_gt).then_inc(s_gs, 1)
                    nc.vector.tensor_tensor(notbelow[:, :, :], other, own, ALU.is_ge).then_inc(s_gs, 1)

                def rank_gates(k):
                    if not k.on(NT):
                        return
                    do = Chain(dve, s_gs, 8, k, 3)
                    dve.wait_ge(s_gs, 8 * k.n + 3)
                    carry(2)
                    do(nc.vector.copy_predicated(above[:, :, :], lower[:, :, :], notbelow[:, :, :]))
                    do(nc.vector.tensor_reduce(rank[:, :], above[:, :, :], AX.X, ALU.add))

                def choose(k):
                    if not k.on(NT):
                        return
                    do = Chain(dve, s_gs, 8, k, 5)
                    dve.wait_ge(s_gex, k.n + 1)
                    do(nc.vector.scalar_tensor_tensor(out=chosen[:, :], in0=rank[:, :], scalar=float(TOPK),
                                                      in1=gexp[:, :], op0=ALU.is_lt, op1=ALU.mult))
                    do(nc.vector.reduce_sum(gsum[:, :], chosen[:, :], AX.X))
                    do(nc.vector.reciprocal(ginv[:, :], gsum[:, :]))

                def split_w(k):
                    if not k.on(NT):
                        return
                    do = Chain(dve, s_w32, 1, k)
                    nc.vector.tensor_scalar(w[:, :], chosen[:, :], ginv[:, :], None, ALU.mult).then_inc(s_gw, 1)
                    nc.vector.tensor_scalar(w32[:, 0:E], chosen[:, :], ginv[:, :], None, ALU.mult)\
                      .then_inc(s_gw, 1)
                    dve.wait_ge(s_gw, 2 * k.n + 2)
                    nc.vector.tensor_tensor(w32[:, E:2 * E], w[:, :], w32[:, 0:E].bitcast(F32), ALU.subtract)\
                      .then_inc(s_w32, 1)

                def copy_wT(k):
                    if not k.on(NT):
                        return
                    dve.wait_ge(s_wTm, k.n + 1)
                    nc.vector.tensor_copy(w32T[:, :], psH[0:2 * E, 0:128]).then_inc(s_wT, 1)
                    dve.wait_ge(s_wT, k.n + 1)
                    nc.vector.tensor_copy(wT[0:2 * E, bass.ds(k.n * 128, 128)], w32T[:, :]).then_inc(s_wTa, 1)

                def add_bias(k):
                    if not k.on(NT):
                        return
                    dve.wait_ge(s_b2m, k.n + 1)
                    nc.vector.tensor_tensor(tile_of(hall, k), tile_of(hall, k), psH[:, 0:D], ALU.add)\
                      .then_inc(s_b2, 1)

                def body(i):
                    scale_t(i - 2)
                    row_sum(i - 1)
                    invert(i - 1)
                    norm1_stats(i + 2)
                    compare(i - 2)
                    norm1(i + 2)
                    split_t(i - 2)
                    rank_gates(i - 2)
                    choose(i - 2)
                    split_w(i - 2)
                    select_heads(i - 1)
                    copy_wT(i - 2)
                    copy_v(i + 1)
                    bias_h(i - 1)
                    add_bias(i - 2)
                    norm2_stats(i - 1)
                    row_max(i)
                    norm2(i - 1)
                    less_max(i)
                sweep(dve, NT, body, lead=2, lag=3)

            @block.gpsimd
            def _(pool):
                nc.gpsimd.memset(v[:, :, :, :], 0.0).then_inc(s_vz, 1)

                def add_bias(k):
                    if not k.on(NT):
                        return
                    pool.wait_ge(s_rd[k.par], 64 * (k.half + 1))
                    wait(pool, s_p, k.n)
                    nc.gpsimd.tensor_tensor(z[:, :, :, :].rearrange("p j b w -> p b j w"),
                                            sq[:, k.par, :, :, 0:Q], bias[:, k.par, :, :, :], ALU.add)\
                      .then_inc(s_z, 1)

                def pad_q(k, g):
                    if not k.on(NT):
                        return
                    pool.wait_ge(s_qb, 2 * k.n + g + 1)
                    wait(pool, s_s, 6 * k.n)
                    src = qb[:, g, :].rearrange("p (b w) -> p b w", b=2)
                    nc.gpsimd.tensor_tensor(
                        qpad[:, g, :, :].rearrange("p b (m w) -> p b m w", w=Q),
                        src.unsqueeze(2).broadcast_to([GC, 2, 2 * PG, Q]),
                        qmask[:, :, :].unsqueeze(1).broadcast_to([GC, 2, 2 * PG, Q]), ALU.mult)\
                      .then_inc(s_qpad, 1)

                def normalise(k):
                    if not k.on(NT):
                        return
                    pool.wait_ge(s_inv, k.n + 1)
                    wait(pool, s_t, 2 * k.n)
                    nc.gpsimd.tensor_tensor(p2[:, :, :, :].rearrange("p j b w -> p (j b) w"),
                                            z[:, :, :, :].rearrange("p j b w -> p (j b) w"),
                                            inv[:, :].unsqueeze(2).broadcast_to([128, 2 * PR, Q]),
                                            ALU.mult).then_inc(s_p, 1)

                def power(k, n):
                    need, src, dst, done = ((s_ve, vareps[:, 0:1], rstd[:, 0:1], s_rstd),
                                            (s_ve2, vareps[:, 1:2], rstd[:, 1:2], s_rstd2),
                                            (s_ms, mseps[:, :], rrms[:, :], s_rr))[n]
                    if not k.on(NT):
                        return
                    pool.wait_ge(need, k.n + 1)
                    nc.gpsimd.tensor_tensor(dst, src, mhalf[:, :], ALU.pow).then_inc(done, 1)

                def body(i):
                    normalise(i - 1)
                    power(i + 2, 0)
                    pad_q(i + 1, 0)
                    pad_q(i + 1, 1)
                    add_bias(i)
                    power(i - 1, 1)
                    power(i - 1, 2)

                pool.wait_ge(s_half, 1)
                sweep(pool, NT, body, lead=2, lag=3)
                for m in range(3):
                    for p in range(2):
                        ew.rest(pool, 0, m, p, 0)


def experts(nc, hall, tAh, tAl, tBs, wT, ident, out, ew):
    STEPS = EP * NC
    with ExitStack() as c:
        sb = lambda n, s, d=F32: c.enter_context(nc.sbuf_tensor(n, s, d))
        ps = lambda n, s: c.enter_context(nc.psum_tensor(n, s, F32))
        sem = lambda n: c.enter_context(nc.semaphore(n))
        w1h, w1l, sel, w2a, w2b, b1 = ew.w1h, ew.w1l, ew.sel, ew.w2a, ew.w2b, ew.b1
        b1g = sb("e_b1_pair", [128, 2, 6])
        glu = sb("e_glu", [128, 2, CH])
        lin = sb("e_lin", [128, 2, CH])
        sig = sb("e_sig", [128, 2, CH])
        yh = sb("e_act_high", [128, 3, CH], F32R)
        yl = sb("e_act_low", [128, 3, CH], F32R)
        accs = [sb("e_accA", [128, T]), sb("e_accB", [128, T])]
        psG = [ps(f"e_psG{n}", [128, CH]) for n in range(2)]
        psL = [ps(f"e_psL{n}", [128, CH]) for n in range(2)]
        psW = [ps(f"e_psW{n}", [128, CH]) for n in range(2)]
        psY = [ps(f"e_psY{n}", [128, CH]) for n in range(2)]

        s_bp = sem("e_b1_pair_done")
        s_g = sem("e_glu_mm")
        s_l = sem("e_lin_mm")
        s_wb = sem("e_weight_mm")
        s_gs = sem("e_glu_done")
        s_l0 = sem("e_lin_copied")
        s_ls = sem("e_lin_clamped")
        s_u = sem("e_product_done")
        s_sg = sem("e_sigmoid_done")
        s_v = sem("e_weighted_done")
        s_a = sem("e_act_done")
        s_yh = sem("e_act_high_done")
        s_yl = sem("e_act_low_done")
        s_y = sem("e_out_mm")
        s_acc = sem("e_out_added")
        s_tr = sem("e_sums_transposed")
        s_h = sem("e_hall_done")
        s_out = sem("e_written")

        class Ep:

            def __init__(self, p, r=None):
                self.par, self.n = p % 2, p if r is None else 2 * r + p

        def pairs(e, each):
            for p in range(2):
                each(Ep(p))
            with e.Fori(1, EP // 2 - 1) as r:
                for p in range(2):
                    each(Ep(p, r))
            for p in range(EP - 2, EP):
                each(Ep(p))

        def has_next(ep):
            return not (isinstance(ep.n, int) and ep.n == EP - 1)

        def chunks(e, ep, step, before=None):
            step(ep, 0, 0, NC * ep.n, None)
            step(ep, 1, 1, NC * ep.n + 1, None)
            if before and has_next(ep):
                before()
            with e.Fori(1, NC // 2) as r:
                for p in range(2):
                    step(ep, 2 * r + p, p, NC * ep.n + 2 * r + p, (r - 1, p) if has_next(ep) else None)

        with nc.Block() as block:

            @block.sync
            def _(sp):
                for n in range(1, EP):
                    sp.wait_ge(ew.high, ew.HIGH * n)
                    sp.wait_ge(ew.low, ew.LOW * n)
                    ew.load_stage(sp, n)
                for ch in range(NC):
                    sp.wait_ge(s_h, 3 * (ch + 1))
                    sp.dma_start(out[:, ch * 4:(ch + 1) * 4, :],
                                 hall[:, ch * 4 * D:(ch + 1) * 4 * D].rearrange("p (t n) -> p t n", n=D))\
                      .then_inc(s_out, 16)
                sp.wait_ge(s_out, 16 * NC)

            @block.tensor
            def _(pe):
                def first(ep, cols, par, s, m, half):
                    n, ring = 3 * s + m, (par + m) % 2
                    dst, need, done = ((psG, s_gs, s_g), (psL, s_l0, s_l))[half]
                    wait(pe, need, n - 1)
                    w = slice((2 * m + half) * 128, (2 * m + half + 1) * 128)
                    parts = ((w1h[:, ep.par, 0, w], tAh), (w1h[:, ep.par, 0, w], tAl), (w1l[:, ep.par, 0, w], tAh),
                             (w1h[:, ep.par, 1, w], tBs), (w1l[:, ep.par, 1, w], tBs))
                    for q, (lhsT, rhs) in enumerate(parts):
                        last = nc.tensor.matmul(dst[ring][:, :], lhsT, rhs[:, cols],
                                                start=q == 0, stop=q == len(parts) - 1)
                    last.then_inc(done, 1)

                def second(s, m, wpar):
                    if isinstance(s, int) and s == 0:
                        return
                    if m == 0:
                        wait(pe, s_acc, 2 * (s - 1))
                    pe.wait_ge(s_yh, 3 * s + m - 2)
                    pe.wait_ge(s_yl, 3 * s + m - 2)
                    wh, wl, wb = w2a[:, wpar, m, 0, :], w2a[:, wpar, m, 1, :], w2b[:, wpar, m, :, :]
                    for bank, lhsT, rhs, q in ((0, wh, yh, 0), (0, wl, yh, 1), (1, wb, yh, 0),
                                               (0, wh, yl, 2), (1, wb, yl, 2)):
                        last = nc.tensor.matmul(psY[bank][:, :], lhsT, rhs[:, m, :],
                                                start=m == 0 and q == 0, stop=m == 2 and q == 2)
                    last.then_inc(s_y, 1)

                def each(ep):
                    pe.wait_ge(ew.low, ew.LOW * (ep.n + 1))
                    pe.wait_ge(ew.high, ew.HIGH * (ep.n + 1))

                    def step(ep, ch, par, s, piece):
                        cols = bass.ds(ch * CH, CH)
                        wpar = 1 - ep.par if isinstance(ch, int) and ch == 0 else ep.par
                        first(ep, cols, par, s, 0, 0)
                        first(ep, cols, par, s, 0, 1)
                        first(ep, cols, par, s, 1, 0)
                        wait(pe, s_v, 3 * s)
                        for m in range(2):
                            nc.tensor.matmul(psW[m][:, :], sel[:, ep.par, m, :], wT[:, cols],
                                             start=True, stop=True).then_inc(s_wb, 1)
                        first(ep, cols, par, s, 1, 1)
                        second(s, 0, wpar)
                        first(ep, cols, par, s, 2, 0)
                        first(ep, cols, par, s, 2, 1)
                        second(s, 1, wpar)
                        second(s, 2, wpar)

                    chunks(pe, ep, step)

                pairs(pe, each)
                for m in range(3):
                    second(STEPS, m, 1)
                pe.wait_ge(s_gs, 3 * STEPS)
                pe.wait_ge(s_l0, 3 * STEPS)
                for ch in range(NC):
                    pe.wait_ge(s_acc, 2 * (NC * (EP - 1) + ch + 1))
                    wait(pe, s_h, 3 * (ch - 1))
                    for acc, bank in zip(accs, (psG[ch % 2], psL[ch % 2])):
                        for tile in range(4):
                            last = nc.tensor.transpose(
                                bank[:, tile * 128:(tile + 1) * 128],
                                acc[:, ch * CH + tile * 128:ch * CH + (tile + 1) * 128], ident[:, :])
                    last.then_inc(s_tr, 1)

            @block.scalar
            def _(act):
                def high(s, m, ring):
                    n = 3 * s + m
                    act.wait_ge(s_a, n + 1)
                    wait(act, s_y, n - 2)
                    nc.scalar.activation(yh[:, m, :], sig[:, ring, :], ACT.Copy).then_inc(s_yh, 1)

                def each(ep):
                    act.wait_ge(s_bp, 2 * ep.n + 2)

                    def step(ep, ch, par, s, piece):
                        if piece:
                            ew.round(*piece, 1 - ep.par)
                        for m in range(3):
                            n, ring = 3 * s + m, (par + m) % 2
                            if m == 2:
                                high(s, 0, ring)
                            elif not (isinstance(s, int) and s == 0):
                                high(s - 1, m + 1, ring)
                            act.wait_ge(s_l, n + 1)
                            wait(act, s_a, n - 1)
                            nc.scalar.activation(lin[:, ring, :], psL[ring][:, :], ACT.Identity,
                                                 bias=b1g[:, ep.par, 2 * m + 1:2 * m + 2]).then_inc(s_l0, 1)
                            act.wait_ge(s_gs, n + 1)
                            wait(act, s_yl, n - 1)
                            nc.scalar.activation(sig[:, ring, :], glu[:, ring, :], ACT.Sigmoid, scale=ALPHA)\
                               .then_inc(s_sg, 1)

                    chunks(act, ep, step, lambda: ew.select(act, ep.n + 1, 1 - ep.par))

                pairs(act, each)
                high(STEPS - 1, 1, 0)
                high(STEPS - 1, 2, 1)

            @block.vector
            def _(dve):
                dve.wait_ge(ew.b1_in, 16)

                def each(ep):
                    nc.vector.tensor_copy(b1g[:, ep.par, :], b1[:, bass.ds(ep.n, 1), :]).then_inc(s_bp, 1)
                    dve.wait_ge(s_bp, 2 * ep.n + 1)
                    bl = b1g[:, ep.par, :].rearrange("p (m h) -> p m h", h=2)
                    nc.vector.tensor_scalar(bl[:, :, 1], bl[:, :, 1], 1.0, None, ALU.add).then_inc(s_bp, 1)
                    dve.wait_ge(s_bp, 2 * ep.n + 2)

                    def step(ep, ch, par, s, piece):
                        for m in range(3):
                            n, ring = 3 * s + m, (par + m) % 2
                            dve.wait_ge(s_g, n + 1)
                            nc.vector.tensor_scalar(glu[:, ring, :], psG[ring][:, :], b1g[:, ep.par, 2 * m:2 * m + 1],
                                                    LIMIT, ALU.add, ALU.min).then_inc(s_gs, 1)
                            if m:
                                weight(s, m - 1, 1 - ring)
                            elif not (isinstance(s, int) and s == 0):
                                weight(s - 1, 2, 1 - ring)
                            if m == 0:
                                add_last(ep, ch, s)
                            dve.wait_ge(s_l0, n + 1)
                            nc.vector.tensor_scalar(lin[:, ring, :], lin[:, ring, :], 1.0 - LIMIT, 1.0 + LIMIT,
                                                    ALU.max, ALU.min).then_inc(s_ls, 1)
                            dve.wait_ge(s_ls, n + 1)
                            nc.vector.tensor_tensor(lin[:, ring, :], lin[:, ring, :], glu[:, ring, :], ALU.mult)\
                              .then_inc(s_u, 1)
                    chunks(dve, ep, step)

                def weight(s, m, ring):
                    dve.wait_ge(s_sg, 3 * s + m + 1)
                    if m < 2:
                        dve.wait_ge(s_wb, 2 * s + m + 1)
                        nc.vector.tensor_tensor(sig[:, ring, :], psW[m][:, :], sig[:, ring, :], ALU.mult)\
                          .then_inc(s_v, 1)
                    else:
                        nc.vector.tensor_tensor(sig[0:64, ring, :], psW[0][0:64, :], sig[0:64, ring, :], ALU.mult)
                        nc.vector.tensor_tensor(sig[64:128, ring, :], psW[1][64:128, :], sig[64:128, ring, :],
                                                ALU.mult).then_inc(s_v, 1)

                def add_last(ep, ch, s):
                    if isinstance(s, int) and s < 2:
                        return
                    before = isinstance(ch, int)
                    whose = ep.n - 1 if before else ep.n
                    add(ch + NC - 2 if before else ch - 2, s - 2, isinstance(whose, int) and whose == 0)

                def add(ch, s, starts):
                    dve.wait_ge(s_y, 3 * s + 3)
                    for acc, bank in zip(accs, psY):
                        part = acc[:, bass.ds(ch * CH, CH)]
                        if starts:
                            nc.vector.tensor_copy(part, bank[:, :]).then_inc(s_acc, 1)
                        else:
                            nc.vector.tensor_tensor(part, bank[:, :], part, ALU.add).then_inc(s_acc, 1)

                pairs(dve, each)
                weight(STEPS - 1, 2, 1)
                add(NC - 2, STEPS - 2, False)
                add(NC - 1, STEPS - 1, False)
                for ch in range(NC):
                    dve.wait_ge(s_tr, ch + 1)
                    h = hall[:, ch * 4 * D:(ch + 1) * 4 * D].rearrange("p (t n) -> p t n", n=D)
                    a = psG[ch % 2][:, :].rearrange("p (t n) -> p t n", n=128)
                    b = psL[ch % 2][:, :].rearrange("p (t n) -> p t n", n=128)
                    nc.vector.tensor_tensor(h[:, :, 0:128], a, h[:, :, 0:128], ALU.add).then_inc(s_h, 1)
                    nc.vector.tensor_tensor(h[:, :, 128:D], b[:, :, 0:64], h[:, :, 128:D], ALU.add).then_inc(s_h, 1)
                    dve.wait_ge(s_h, 3 * ch + 2)
                    nc.vector.tensor_tensor(h[:, :, 128:D], b[:, :, 64:128], h[:, :, 128:D], ALU.add)\
                      .then_inc(s_h, 1)

            @block.gpsimd
            def _(pool):
                def each(ep):
                    def step(ep, ch, par, s, piece):
                        for m in range(3):
                            n, ring = 3 * s + m, (par + m) % 2
                            pool.wait_ge(s_u, n + 1)
                            pool.wait_ge(s_v, n + 1)
                            nc.gpsimd.tensor_tensor(sig[:, ring, :], lin[:, ring, :], sig[:, ring, :], ALU.mult)\
                              .then_inc(s_a, 1)
                            if m == 0 and piece:
                                ew.rest(pool, ep.n + 1, *piece, 1 - ep.par)
                            pool.wait_ge(s_yh, n + 1)
                            nc.gpsimd.tensor_tensor(yl[:, m, :], sig[:, ring, :], yh[:, m, :].bitcast(F32),
                                                    ALU.subtract).then_inc(s_yl, 1)

                    chunks(pool, ep, step)

                pairs(pool, each)


def audio_tower(nc, a, out):
    with ExitStack() as c:
        sb = lambda n, s, d=F32: c.enter_context(nc.sbuf_tensor(n, s, d))
        hall = sb("hall", [128, NT * D])
        tAh = sb("tA_high", [128, T], F32R)
        tAl = sb("tA_low", [128, T], F32R)
        tBs = sb("tB_high_low", [128, T], F32R)
        wT = sb("wT", [128, T], F32R)
        ident = sb("ident", [128, 128])
        hmask = sb("hmask", [GC, 2])
        qmask = sb("qmask", [GC, 2 * PG, Q])
        scratch = nc.dram_tensor("rel_scratch", (2, 2, 128, PR, REL), F32, kind="Internal").ap()
        lw = LocalWeights(nc, c, a)
        pool_attention(nc, hall, wT, ident, hmask, qmask, lw, a)
        ew = ExpertWeights(nc, c, a)
        local_attention(nc, hall, tAh, tAl, tBs, wT, ident, hmask, qmask, scratch, lw, ew)
        experts(nc, hall, tAh, tAl, tBs, wT, ident, out, ew)


def kernel(**inputs):
    import numpy as np
    import concourse.bacc as bacc
    from concourse.bass_utils import run_bass_kernel_spmd as run

    f = np.float32
    x = {n: np.asarray(v) for n, v in inputs.items()}

    def grouped(w):
        return np.ascontiguousarray(w.reshape(G, GC, -1).transpose(1, 0, 2))

    def rows(b):
        return np.ascontiguousarray(np.broadcast_to(b, (128, b.size)))

    def per_group(*bs):
        return np.ascontiguousarray(np.concatenate([b.reshape(G, GC).T for b in bs], axis=1))

    bqkv = x["L0_tok_b_qkv"]
    head = np.arange(GC) // DK
    hmask = np.stack([head % 2 == 0, head % 2 == 1], axis=1).astype(f)
    qmask = np.zeros((GC, 2 * PG, Q), f)
    qmask[np.arange(GC), head, :] = SCALE
    lower = (np.arange(E)[None, :] < np.arange(E)[:, None]).astype(np.int32)
    rel = np.clip(Q - 1 - np.arange(REL), -MAXREL, MAXREL) + MAXREL
    relT = np.tile(x["L0_attn_rel_emb"][rel].T, (GC // DK, 1))
    relT = np.broadcast_to(relT[:, None, :], (GC, 4 * G, REL))
    w1, b1 = x["L0_ffn_w1"].reshape(EP, 2, D, 2 * I), x["L0_ffn_b1"].reshape(EP, 2, 1, 2 * I)

    def tiles(w):
        parts = []
        for e in range(2):
            parts += [w[:, e, :, 0:128], w[:, e, :, I:I + 128]]
        for o in (0, I):
            parts += [w[:, 0, :, o + 128:o + I], w[:, 1, :, o + 128:o + I]]
        return np.concatenate(parts, axis=2)

    w1t = tiles(w1)
    w1k = np.stack([w1t[:, 0:128], np.concatenate([w1t[:, 128:D], w1t[:, 128:D]], axis=1)], axis=2)
    b1t = tiles(b1).reshape(EP, 6, 128)
    w2 = x["L0_ffn_w2"].reshape(EP, 2, I, D)
    w2k = np.stack([w2[:, 0, 0:128], w2[:, 1, 0:128], np.concatenate([w2[:, 0, 128:I], w2[:, 1, 128:I]], axis=1)],
                   axis=2)
    sel = np.zeros((128, EP, 2, 128), f)
    for p in range(EP):
        for half in (0, E):
            sel[half + 2 * p, p, 0, :] = 1.0
            sel[half + 2 * p + 1, p, 1, :] = 1.0
    arrays = {
        "xT": np.ascontiguousarray(x["x"].reshape(B * N, D).T),
        "wqkvT": np.ascontiguousarray(x["L0_tok_w_qkv"].T), "wprojT": grouped(x["L0_tok_w_proj"].T),
        "bqk": per_group(bqkv[0:D], bqkv[D:2 * D]), "bv": rows(bqkv[2 * D:]), "bproj": rows(x["L0_tok_b_proj"]),
        "ident": np.eye(128, dtype=f), "hmask": hmask, "qmask": qmask,
        "awqkv": grouped(np.concatenate([x["L0_attn_Wq"], x["L0_attn_Wk"], x["L0_attn_Wv"]], axis=1)),
        "awo": grouped(x["L0_attn_Wo"]), "abqk": per_group(x["L0_attn_bq"], x["L0_attn_bk"]),
        "abv": rows(x["L0_attn_bv"]), "abo": rows(x["L0_attn_bo"]), "tscale": rows(x["L0_ffn_scale"]),
        "gwT": np.ascontiguousarray(x["L0_ffn_gate_w"].T), "gb": rows(x["L0_ffn_gate_b"]),
        "lower": np.ascontiguousarray(np.broadcast_to(lower, (128, E, E))),
        "b2dup": np.concatenate([x["L0_ffn_b2"], x["L0_ffn_b2"]]), "relT": np.ascontiguousarray(relT),
        "w1": np.ascontiguousarray(w1k.transpose(1, 0, 2, 3).reshape(128, -1)),
        "b1": np.ascontiguousarray(b1t.transpose(2, 0, 1)),
        "w2": np.ascontiguousarray(w2k.transpose(1, 0, 2, 3).reshape(128, -1)),
        "sel": sel.reshape(128, -1),
    }
    nc = bacc.Bacc("TRN2", target_bir_lowering=False, num_devices=1)
    feeds, aps = {}, {}
    for name, array in arrays.items():
        feeds["in_" + name] = array
        aps[name] = nc.dram_tensor("in_" + name, array.shape, mybir.dt.from_np(array.dtype), kind="ExternalInput").ap()
    out = nc.dram_tensor("out", (B, Q, D), F32, kind="ExternalOutput").ap()
    audio_tower(nc, aps, out.rearrange("b q n -> (b q) n").rearrange("(t p) n -> p t n", p=128))
    r = run(nc, [feeds], core_ids=[0])
    return r.results[0]["out"]
```
